# Optimizing a Trainium2 kernel written in Bass

```python
import numpy as np
import jax
import jax.numpy as jnp

def _softmax(x, axis=-1):
    return jax.nn.softmax(x, axis=axis)

def _gelu(x):
    return jax.nn.gelu(x, approximate=True)

def _silu(x):
    return jax.nn.silu(x)

def _sigmoid(x):
    return jax.nn.sigmoid(x)

def _layernorm(x, axis=-1, eps=1e-05):
    m = jnp.mean(x, axis=axis, keepdims=True)
    v = jnp.var(x, axis=axis, keepdims=True)
    return (x - m) / jnp.sqrt(v + eps)

def _scatter_add(tgt, idx, src, axis=0):
    return tgt.at[idx].add(src)

def _segment_sum(src, seg, n):
    return jax.ops.segment_sum(src, seg, n)
kernel_name = 'mk_decoder_preln_d1_seqx_r4_377f78'

def setup_inputs(seed: int=0):
    np.random.seed(seed)
    _w = jnp.asarray

    def _rec_inputs():
        import jax
        import jax.numpy as jnp
        _rk = jax.random.key(seed)
        x = 7.22e-05 + 1 * jax.random.normal(jax.random.fold_in(_rk, 1), (16, 128, 512), jnp.float32)
        _lenS = 128 - jax.random.randint(jax.random.fold_in(_rk, 7), (16,), 0, max(1, 128 // 4) + 1, jnp.int32)
        _lenS2 = 128 - jax.random.randint(jax.random.fold_in(_rk, 8), (16,), 0, max(1, 128 // 4) + 1, jnp.int32)
        _ctx_1024P = jax.random.normal(jax.random.fold_in(_rk, 11), (16, 16, 256), jnp.float32)
        _ctx_1024c = jax.random.dirichlet(jax.random.fold_in(_rk, 511), 0.3 * jnp.ones((16,), jnp.float32), (16, 128))
        _ctx_1024t = jnp.einsum('bsk,bkd->bsd', _ctx_1024c, _ctx_1024P)
        _ctx_1024t = _ctx_1024t * jax.lax.rsqrt(jnp.mean(jnp.square(_ctx_1024t)) + 1e-12) * 0.953939
        ctx_1024 = -1.39393e-06 + 0.999914 * (_ctx_1024t + 0.3 * jax.random.normal(jax.random.fold_in(_rk, 611), (16, 128, 256), jnp.float32))
        fside_BxSx2_0 = jax.random.uniform(jax.random.fold_in(_rk, 12), (16, 128, 2), jnp.float32, 0.0, 0.999707)
        return (x, ctx_1024, fside_BxSx2_0)
    x, ctx_1024, fside_BxSx2_0 = _rec_inputs()

    def _L0_attn_setup():
        import jax, jax.numpy as jnp
        import numpy as np
        B, S, QD = (2, 1024, 512)
        H, D = (32, 64)
        INNER = H * D
        key = jax.random.key(seed)
        ks = jax.random.split(key, 6)
        scale = 1.0 / np.sqrt(QD)
        return {'hidden_states': jax.random.normal(ks[0], (B, S, QD), dtype=jnp.float32), 'Wq': jax.random.normal(ks[1], (QD, INNER), dtype=jnp.float32) * scale, 'Wk': jax.random.normal(ks[2], (QD, INNER), dtype=jnp.float32) * scale, 'Wv': jax.random.normal(ks[3], (QD, INNER), dtype=jnp.float32) * scale, 'Wo': jax.random.normal(ks[4], (INNER, QD), dtype=jnp.float32) * (1.0 / np.sqrt(INNER)), 'bo': jax.random.normal(ks[5], (QD,), dtype=jnp.float32) * 0.01}
    _L0_attn_all = _L0_attn_setup()
    _L0_attn_in = {k: v for k, v in _L0_attn_all.items() if k in ('Wq', 'Wk', 'Wv', 'Wo', 'bo')}
    del _L0_attn_all

    def _L0_xattn_setup():
        import jax, jax.numpy as jnp
        import numpy as np
        DIM = 512
        CTX_DIM = 256
        N_HEADS = 32
        HEAD_DIM = DIM // N_HEADS
        POS_DIM = 2
        B, N, CTXN = (2, 512, 512)
        ROPE_BASE = 10000.0

        def apply_axial_rope(x, pos):
            b, n, h, d = x.shape
            p = pos.shape[-1]
            dpa = d // p
            half = dpa // 2
            freqs = ROPE_BASE ** (-jnp.arange(half, dtype=x.dtype) / half)
            ang = pos[..., :, None] * freqs
            cos = jnp.cos(ang)[:, :, None, :, :]
            sin = jnp.sin(ang)[:, :, None, :, :]
            xr = x.reshape(b, n, h, p, half, 2)
            x1, x2 = (xr[..., 0], xr[..., 1])
            out = jnp.stack([x1 * cos - x2 * sin, x1 * sin + x2 * cos], axis=-1)
            return out.reshape(b, n, h, d)
        key = jax.random.key(seed)
        ks = jax.random.split(key, 8)
        x = jax.random.normal(ks[0], (B, N, DIM), jnp.float32)
        ctx = jax.random.normal(ks[1], (B, CTXN, CTX_DIM), jnp.float32)
        pos_map = jax.random.uniform(ks[2], (B, N, POS_DIM), jnp.float32)
        ctx_pos_map = jax.random.uniform(ks[3], (B, CTXN, POS_DIM), jnp.float32)
        Wq = jax.random.normal(ks[4], (DIM, DIM), jnp.float32) / np.sqrt(DIM)
        Wkv = jax.random.normal(ks[5], (CTX_DIM, 2 * DIM), jnp.float32) / np.sqrt(CTX_DIM)
        Wout = jax.random.normal(ks[6], (DIM, DIM), jnp.float32) / np.sqrt(DIM)
        bout = jnp.zeros((DIM,), jnp.float32)
        return {'x': x, 'ctx': ctx, 'pos_map': pos_map, 'ctx_pos_map': ctx_pos_map, 'Wq': Wq, 'Wkv': Wkv, 'Wout': Wout, 'bout': bout}
    _L0_xattn_all = _L0_xattn_setup()
    _L0_xattn_in = {k: v for k, v in _L0_xattn_all.items() if k in ('Wq', 'Wkv', 'Wout', 'bout')}
    del _L0_xattn_all

    def _L0_ffn_setup():
        import jax, jax.numpy as jnp
        import numpy as np
        _FP4_LUT = jnp.array([0.0, 0.5, 1.0, 1.5, 2.0, 3.0, 4.0, 6.0, -0.0, -0.5, -1.0, -1.5, -2.0, -3.0, -4.0, -6.0], dtype=jnp.float32)
        GROUP_SIZE = 128
        EPS = 1e-06

        def _dequant_fp4(packed_i32, scales_f16, group_size):
            out_f, in_p = packed_i32.shape
            w = packed_i32.astype(jnp.uint32)
            shifts = jnp.arange(8, dtype=jnp.uint32) * 4
            nib = w[:, :, None] >> shifts & jnp.uint32(15)
            vals = _FP4_LUT[nib.astype(jnp.int32)].reshape(out_f, in_p * 8)
            s = scales_f16.astype(jnp.float32).T
            s_full = jnp.repeat(s, group_size, axis=1)
            return vals * s_full
        key = jax.random.key(seed)
        k1, k2, k3, k4, k5 = jax.random.split(key, 5)
        B, S, H, I = (4, 512, 512, 1408)
        x = jax.random.normal(k1, (B, S, H), dtype=jnp.float32)
        gate_up_packed = jax.random.randint(k2, (2 * I, H // 8), 0, 2147483647, dtype=jnp.int32)
        gate_up_scales = jax.random.uniform(k3, (H // GROUP_SIZE, 2 * I), dtype=jnp.float32).astype(jnp.float16)
        down_packed = jax.random.randint(k4, (H, I // 8), 0, 2147483647, dtype=jnp.int32)
        down_scales = jax.random.uniform(k5, (I // GROUP_SIZE, H), dtype=jnp.float32).astype(jnp.float16)
        return {'x': x, 'gate_up_packed': gate_up_packed, 'gate_up_scales': gate_up_scales, 'down_packed': down_packed, 'down_scales': down_scales}
    _L0_ffn_all = _L0_ffn_setup()
    _L0_ffn_in = {k: v for k, v in _L0_ffn_all.items() if k in ('gate_up_packed', 'gate_up_scales', 'down_packed', 'down_scales')}
    del _L0_ffn_all
    return {'x': x, 'ctx_1024': ctx_1024, 'fside_BxSx2_0': fside_BxSx2_0, 'L0_attn_Wq': _L0_attn_in['Wq'], 'L0_attn_Wk': _L0_attn_in['Wk'], 'L0_attn_Wv': _L0_attn_in['Wv'], 'L0_attn_Wo': _L0_attn_in['Wo'], 'L0_attn_bo': _L0_attn_in['bo'], 'L0_xattn_Wq': _L0_xattn_in['Wq'], 'L0_xattn_Wkv': _L0_xattn_in['Wkv'], 'L0_xattn_Wout': _L0_xattn_in['Wout'], 'L0_xattn_bout': _L0_xattn_in['bout'], 'L0_ffn_gate_up_packed': _L0_ffn_in['gate_up_packed'], 'L0_ffn_gate_up_scales': _L0_ffn_in['gate_up_scales'], 'L0_ffn_down_packed': _L0_ffn_in['down_packed'], 'L0_ffn_down_scales': _L0_ffn_in['down_scales']}

def reference(x, ctx_1024, fside_BxSx2_0, L0_attn_Wq, L0_attn_Wk, L0_attn_Wv, L0_attn_Wo, L0_attn_bo, L0_xattn_Wq, L0_xattn_Wkv, L0_xattn_Wout, L0_xattn_bout, L0_ffn_gate_up_packed, L0_ffn_gate_up_scales, L0_ffn_down_packed, L0_ffn_down_scales):
    import jax
    import jax.numpy as jnp

    def _L0_attn_ref(hidden_states, Wq, Wk, Wv, Wo, bo):
        import jax, jax.numpy as jnp
        import numpy as np
        B, S, QD = (2, 1024, 512)
        H, D = (32, 64)
        INNER = H * D
        b, s, _ = hidden_states.shape

        def proj(W):
            return (hidden_states @ W).reshape(b, s, H, D).transpose(0, 2, 1, 3)
        q = jax.nn.relu(proj(Wq))
        k = jax.nn.relu(proj(Wk))
        v = proj(Wv)
        kv = jnp.einsum('bhsd,bhse->bhde', k, v)
        qkv = jnp.einsum('bhsd,bhde->bhse', q, kv)
        key_sum = k.sum(axis=2)
        normalizer = jnp.einsum('bhsd,bhd->bhs', q, key_sum)
        normalizer = jnp.clip(normalizer, 1e-06, None)[..., None]
        out = qkv / normalizer
        out = out.transpose(0, 2, 1, 3).reshape(b, s, INNER)
        return out @ Wo + bo

    def _L0_xattn_ref(x, ctx, pos_map, ctx_pos_map, Wq, Wkv, Wout, bout):
        import jax, jax.numpy as jnp
        import numpy as np
        DIM = 512
        CTX_DIM = 256
        N_HEADS = 32
        HEAD_DIM = DIM // N_HEADS
        POS_DIM = 2
        B, N, CTXN = (2, 512, 512)
        ROPE_BASE = 10000.0

        def apply_axial_rope(x, pos):
            b, n, h, d = x.shape
            p = pos.shape[-1]
            dpa = d // p
            half = dpa // 2
            freqs = ROPE_BASE ** (-jnp.arange(half, dtype=x.dtype) / half)
            ang = pos[..., :, None] * freqs
            cos = jnp.cos(ang)[:, :, None, :, :]
            sin = jnp.sin(ang)[:, :, None, :, :]
            xr = x.reshape(b, n, h, p, half, 2)
            x1, x2 = (xr[..., 0], xr[..., 1])
            out = jnp.stack([x1 * cos - x2 * sin, x1 * sin + x2 * cos], axis=-1)
            return out.reshape(b, n, h, d)
        b, n, _ = x.shape
        ctx_n = ctx.shape[1]
        q = (x @ Wq).reshape(b, n, N_HEADS, HEAD_DIM)
        k, v = jnp.split(ctx @ Wkv, 2, axis=-1)
        k = k.reshape(b, ctx_n, N_HEADS, HEAD_DIM)
        v = v.reshape(b, ctx_n, N_HEADS, HEAD_DIM)
        q = apply_axial_rope(q, pos_map)
        k = apply_axial_rope(k, ctx_pos_map)
        scale = 1.0 / np.sqrt(HEAD_DIM).astype(np.float32)
        logits = jnp.einsum('bqhd,bkhd->bhqk', q, k) * scale
        w = jax.nn.softmax(logits, axis=-1)
        attn = jnp.einsum('bhqk,bkhd->bqhd', w, v)
        attn = attn.reshape(b, n, N_HEADS * HEAD_DIM)
        return attn @ Wout + bout

    def _L0_ffn_ref(x, gate_up_packed, gate_up_scales, down_packed, down_scales):
        import jax, jax.numpy as jnp
        import numpy as np
        _FP4_LUT = jnp.array([0.0, 0.5, 1.0, 1.5, 2.0, 3.0, 4.0, 6.0, -0.0, -0.5, -1.0, -1.5, -2.0, -3.0, -4.0, -6.0], dtype=jnp.float32)
        GROUP_SIZE = 128
        EPS = 1e-06

        def _dequant_fp4(packed_i32, scales_f16, group_size):
            out_f, in_p = packed_i32.shape
            w = packed_i32.astype(jnp.uint32)
            shifts = jnp.arange(8, dtype=jnp.uint32) * 4
            nib = w[:, :, None] >> shifts & jnp.uint32(15)
            vals = _FP4_LUT[nib.astype(jnp.int32)].reshape(out_f, in_p * 8)
            s = scales_f16.astype(jnp.float32).T
            s_full = jnp.repeat(s, group_size, axis=1)
            return vals * s_full
        I = gate_up_packed.shape[0] // 2
        w_gu = _dequant_fp4(gate_up_packed, gate_up_scales, GROUP_SIZE)
        w_down = _dequant_fp4(down_packed, down_scales, GROUP_SIZE)
        gate_up = jnp.einsum('bsh,oh->bso', x, w_gu)
        gate, up = (gate_up[..., :I], gate_up[..., I:])
        h = jax.nn.silu(gate) * up
        y = jnp.einsum('bsi,hi->bsh', h, w_down)
        rms = jnp.sqrt(jnp.mean(y * y, axis=-1, keepdims=True) + EPS)
        return y / rms
    x = x + _L0_attn_ref(_layernorm(x, axis=-1), L0_attn_Wq, L0_attn_Wk, L0_attn_Wv, L0_attn_Wo, L0_attn_bo)
    x = x + _L0_xattn_ref(_layernorm(x, axis=-1), ctx_1024, fside_BxSx2_0, fside_BxSx2_0, L0_xattn_Wq, L0_xattn_Wkv, L0_xattn_Wout, L0_xattn_bout)
    x = x + _L0_ffn_ref(_layernorm(x, axis=-1), L0_ffn_gate_up_packed, L0_ffn_gate_up_scales, L0_ffn_down_packed, L0_ffn_down_scales)
    return x

_drawn_inputs = setup_inputs


def setup_inputs(seed=0):
    import zlib

    import numpy as np

    out = dict(_drawn_inputs(seed))
    spreads = {'L0_xattn_bout': (0.0, 0.1)}
    factors = {'L0_attn_bo': 5.213}
    for name, (base, spread) in spreads.items():
        noise = np.random.default_rng([zlib.crc32(name.encode()), seed]).standard_normal(out[name].shape)
        drawn = base * np.exp(spread * noise) if base else spread * noise
        out[name] = jnp.asarray(drawn.astype(out[name].dtype))
    for name, factor in factors.items():
        out[name] = (out[name] * factor).astype(out[name].dtype)
    return out
```

```python
import math
from contextlib import ExitStack

import concourse.bass as bass
from concourse import mybir

F32 = mybir.dt.float32
F32R = mybir.dt.float32r
F16 = mybir.dt.float16
I32 = mybir.dt.int32
U32 = mybir.dt.uint32
BF16 = mybir.dt.bfloat16
ALU = mybir.AluOpType
ACT = mybir.ActivationFunctionType
AX_X = mybir.AxisListType.X

P = 128
EPS_LN = 1e-5
EPS_RMS = 1e-6
START = 32


def done(n):
    return START + 1 + n


def start(engine, *semaphores):
    for s in semaphores:
        engine.sem_inc(s, START)


def matmul_split(pe, out, stationary, moving, first, last):
    pe.matmul(out, stationary[0], moving[0], start=first, stop=False)
    pe.matmul(out, stationary[0], moving[1], start=False, stop=False)
    return pe.matmul(out, stationary[1], moving[0], start=False, stop=last)


class LayerNorm:

    def __init__(self, nc, sb, sem, tag, x, cols, psum, ident, minus_half, batches, k_tiles):
        self.x, self.cols, self.psum, self.ident, self.minus_half = x, cols, psum, ident, minus_half
        self.nc, self.nb, self.kt = nc, batches, k_tiles
        self.stats = sb(tag + "stats", [P, 2, 6], F32)
        self.mean_var = sb(tag + "mean_var", [P, 2, 2], F32)
        self.var_eps = sb(tag + "var_eps", [P, 2, 1], F32)
        self.rstd = sb(tag + "rstd", [P, 2, 1], F32)
        self.normed = sb(tag + "normed", [P, 2, k_tiles * P], F32)
        self.stats_done = sem(tag + "stats_done")
        self.mean_done = sem(tag + "mean_done")
        self.var_done = sem(tag + "var_done")
        self.rstd_done = sem(tag + "rstd_done")
        self.norm_done = sem(tag + "norm_done")
        self.turned = sem(tag + "turned")
        self.hi_done = sem(tag + "hi_done")
        self.lo_done = sem(tag + "lo_done")

    def vector(self, dve, b):
        for h in range(2):
            dve.bn_stats(self.stats[:, h, :], self.x[:, b + h, :]).then_inc(self.stats_done, 1)
        for h in range(2):
            dve.wait_ge(self.stats_done, b + h + 1)
            dve.bn_aggr(self.mean_var[:, h, :], self.stats[:, h, :]).then_inc(self.mean_done, 1)
        for h in range(2):
            dve.wait_ge(self.mean_done, b + h + 1)
            dve.tensor_scalar(self.var_eps[:, h, :], self.mean_var[:, h, 1:2], EPS_LN, None,
                              ALU.add).then_inc(self.var_done, 1)
        for h in range(2):
            dve.wait_ge(self.rstd_done, b + h + 1)
            dve.wait_ge(self.turned, b)
            dve.tensor_scalar(self.normed[:, h, :], self.x[:, b + h, :], self.mean_var[:, h, 0:1],
                              self.rstd[:, h, :], ALU.subtract, ALU.mult).then_inc(self.norm_done, 1)
        for h in range(2):
            dve.wait_ge(self.hi_done, b + h + 1)
            at = slice(None), slice(None), slice((b + h) * P, (b + h + 1) * P)
            dve.tensor_tensor(self.cols[1][at], self.psum[:, h, :, :],
                              self.cols[0].bitcast(F32)[at], ALU.subtract).then_inc(self.lo_done, 1)

    def pool(self, pool, b):
        for h in range(2):
            pool.wait_ge(self.var_done, b + h + 1)
            pool.tensor_tensor(self.rstd[:, h, :], self.var_eps[:, h, :], self.minus_half[:, :],
                               ALU.pow).then_inc(self.rstd_done, 1)

    def tensor(self, pe, b):
        for h in range(2):
            pe.wait_ge(self.norm_done, b + h + 1)
            pe.wait_ge(self.lo_done, b)
            for k in range(self.kt):
                mm = pe.transpose(self.psum[:, h, k, :], self.normed[:, h, k * P:(k + 1) * P],
                                  self.ident[:, :])
            mm.then_inc(self.turned, 1)

    def scalar(self, act, b):
        for h in range(2):
            act.wait_ge(self.turned, b + h + 1)
            act.activation(self.cols[0][:, :, (b + h) * P:(b + h + 1) * P], self.psum[:, h, :, :],
                           ACT.Copy).then_inc(self.hi_done, 1)


def linear_attention(nc, x, ident, ones, minus_half, x_dram, Wq, Wk, Wv, Wo, bo):
    D, INNER = Wq.shape
    KT = D // P
    NB = x.shape[1]
    HD = 64
    GW = 256
    GROUPS = INNER // GW
    HG, PAIRS = GW // HD, GW // P
    AUG = HD + 1
    with ExitStack() as ctx:
        sb = lambda n, s, d: ctx.enter_context(nc.sbuf_tensor("a_" + n, s, d))
        ps = lambda n, s, d: ctx.enter_context(nc.psum_tensor("a_" + n, s, d))
        sem = lambda n: ctx.enter_context(nc.semaphore("a_" + n))

        h_cols = [sb(f"h_cols{s}", [P, KT, NB * P], F32R) for s in "hl"]
        wq_raw = sb("wq_raw", [P, KT, GW], F32)
        wkv_raw = sb("wkv_raw", [P, KT, 2, GW], F32)
        wo_raw = sb("wo_raw", [P, PAIRS, D], F32)
        wq = [[sb(f"wq{g}{s}", [P, KT, GW], F32R) for s in "hl"] for g in range(2)]
        wkv = [[sb(f"wkv{g}{s}", [P, KT, 2 * GW], F32R) for s in "hl"] for g in range(2)]
        wo = [[sb(f"wo{g}{s}", [P, PAIRS, D], F32R) for s in "hl"] for g in range(2)]
        q_cols = [sb(f"q_cols{i}", [P, PAIRS, 4 * P], F32) for i in range(2)]
        k_rows = [sb(f"k_rows{i}", [P, GW], F32) for i in range(2)]
        v_rows = [sb(f"v_rows{i}", [P, HG, AUG], F32) for i in range(2)]
        kv_diag = [sb(f"kv_diag{i}", [P, PAIRS, 2 * AUG], F32) for i in range(2)]
        pair_mask = sb("pair_mask", [P, PAIRS, 2, AUG], F32)
        denom = [sb(f"denom{i}", [P, HG, 1], F32) for i in range(2)]
        inv = [sb(f"inv{i}", [P, HG, 1], F32) for i in range(2)]
        o_rows = [sb(f"o_rows{i}", [P, HG, HD], F32) for i in range(2)]
        o_cols = [[sb(f"o_cols{i}{s}", [P, PAIRS, P], F32R) for s in "hl"] for i in range(2)]
        bias = sb("bias", [P, D], F32)

        q_ps = ps("q_ps", [P, 2, 512], F32)
        kv_ps = ps("kv_ps", [P, 2, 512], F32)
        kvm_ps = ps("kvm_ps", [P, 512], F32)
        num_ps = ps("num_ps", [P, 512], F32)
        turn_ps = ps("turn_ps", [P, 512], F32)
        y_ps = ps("y_ps", [P, 512], F32)
        ln_ps = q_ps[:, :, :].rearrange("p h (k t) -> p h k t", k=KT)
        num_heads = num_ps[:, 0:HG * AUG].rearrange("p (h e) -> p h e", h=HG)

        ln = LayerNorm(nc, sb, sem, "ln_", x, h_cols, ln_ps, ident, minus_half, NB, KT)

        x_in = [sem(f"x_in{q}") for q in range(4)]
        bias_in, raw_in = sem("bias_in"), sem("raw_in")
        ones_set, mask_set, mask_cut = sem("ones_set"), sem("mask_set"), sem("mask_cut")
        hi_split, weights_ready = sem("hi_split"), sem("weights_ready")
        bias_added = sem("bias_added")
        q_done, q_copied = sem("q_done"), sem("q_copied")
        kv_done, kv_copied = sem("kv_done"), sem("kv_copied")
        kvm_done, kvm_masked = sem("kvm_done"), sem("kvm_masked")
        num_done = sem("num_done")
        den_clipped, den_inverted, o_scaled = sem("den_clipped"), sem("den_inverted"), sem("o_scaled")
        o_turned, o_hi, o_lo = sem("o_turned"), sem("o_hi"), sem("o_lo")
        y_done, y_added = sem("y_done"), sem("y_added")

        STEPS = 2 * NB
        block = ctx.enter_context(nc.Block())

        @block.sync
        def _(sp):
            for q in range(4):
                sp.dma_start(x[:, 4 * q:4 * q + 4, :],
                             x_dram[4 * q:4 * q + 4].rearrange("b t d -> t b d")).then_inc(x_in[q], 16)
            sp.dma_start(bias[:, :], bo.rearrange("(a d) -> a d", a=1).to_broadcast([P, D])).then_inc(bias_in, 16)
            with sp.Fori(0, GROUPS) as g:
                sp.wait_ge(weights_ready, done(g * 3 - 1))
                for raw, W in ((wq_raw[:, :, :], Wq), (wkv_raw[:, :, 0, :], Wk), (wkv_raw[:, :, 1, :], Wv)):
                    sp.dma_start(raw, W.rearrange("(k p) n -> p k n", p=P)[:, :, bass.ds(g * GW, GW)])\
                        .then_inc(raw_in, 16)
                sp.dma_start(wo_raw[:, :, :], Wo.rearrange("(g j p) n -> g p j n", j=PAIRS, p=P)
                             [bass.ds(g, 1)].rearrange("g p j n -> (g p) j n")).then_inc(raw_in, 16)

        @block.gpsimd
        def _(pool):
            start(pool, hi_split, weights_ready)
            for i in range(2):
                pool.memset(v_rows[i][:, :, HD:AUG], 1.0).then_inc(ones_set, 1)
            pool.memset(pair_mask[:, :, :, :], 0.0).then_inc(mask_set, 1)
            pool.wait_ge(mask_set, 1)
            for e in range(2):
                pool.memset(pair_mask[HD * e:HD * (e + 1), :, e, :], 1.0).then_inc(mask_cut, 1)
            pool.wait_ge(mask_cut, 2)
            for b in range(0, NB, 2):
                ln.pool(pool, b)
            with pool.Fori(0, GROUPS // 2) as it:
                for gg in range(2):
                    g = it * 2 + gg
                    pool.wait_ge(raw_in, (g + 1) * 64)
                    pool.wait_ge(y_done, done((g - 2) * NB + NB - 1))
                    parts = ((wq_raw[:, :, :], wq[gg]),
                             (wkv_raw[:, :, :, :].rearrange("p k a n -> p k (a n)"), wkv[gg]),
                             (wo_raw[:, :, :], wo[gg]))
                    for raw, w in parts:
                        pool.tensor_tensor(w[0][:, :, :], raw, ones[:, :].unsqueeze(2).to_broadcast(list(raw.shape)), ALU.mult)\
                            .then_inc(hi_split, 1)
                    for n, (raw, w) in enumerate(parts):
                        pool.wait_ge(hi_split, done(g * 3 + n))
                        pool.tensor_tensor(w[1][:, :, :], raw, w[0][:, :, :].bitcast(F32), ALU.subtract)\
                            .then_inc(weights_ready, 1)

        @block.scalar
        def _(act):
            start(act, q_copied, kv_copied, o_hi)
            for b in range(0, NB, 2):
                ln.scalar(act, b)
            act.wait_ge(ones_set, 2)
            with act.Fori(0, GROUPS // 2) as it:
                n0 = it * STEPS
                for s in range(STEPS + 3):
                    if s % 4 == 0 and s < STEPS:
                        blk = it * (STEPS // 4) + s // 4
                        act.wait_ge(num_done, done(blk * 4 - 5))
                        for f in range(PAIRS):
                            act.wait_ge(q_done, done(blk * 2 + f))
                            act.activation(q_cols[s // 4 % 2][:, f, :], q_ps[:, f, :], ACT.Relu)\
                                .then_inc(q_copied, 1)
                    if s < STEPS:
                        p = s % 2
                        act.wait_ge(kv_done, done(n0 + s))
                        act.wait_ge(kvm_done, done(n0 + s - 2))
                        act.activation(k_rows[p][:, :], kv_ps[:, p, 0:GW], ACT.Relu)
                        act.activation(v_rows[p][:, :, 0:HD],
                                       kv_ps[:, p, GW:2 * GW].rearrange("p (h e) -> p h e", h=HG),
                                       ACT.Copy).then_inc(kv_copied, 1)
                    if s >= 3:
                        p = (s - 3) % 2
                        act.wait_ge(o_turned, done(n0 + s - 3))
                        act.wait_ge(y_done, done(n0 + s - 5))
                        act.activation(o_cols[p][0][:, :, :],
                                       turn_ps[:, 0:GW].rearrange("p (j t) -> p j t", j=PAIRS),
                                       ACT.Copy).then_inc(o_hi, 1)

        @block.tensor
        def _(pe):
            start(pe, q_done, kv_done, kvm_done, num_done, o_turned, y_done)
            for b in range(0, NB, 2):
                ln.tensor(pe, b)
            pe.wait_ge(ln.lo_done, NB)
            with pe.Fori(0, GROUPS // 2) as it:
                n0 = it * STEPS
                for s in range(STEPS + 4):
                    if s % NB == 0 and s < STEPS:
                        pe.wait_ge(weights_ready, done((it * 2 + s // NB) * 3 + 2))
                    if s % 4 == 0 and s < STEPS:
                        w, blk, tok = wq[s // NB], it * (STEPS // 4) + s // 4, s % NB * P
                        pe.wait_ge(q_copied, done(blk * 2 - 1))
                        for f in range(PAIRS):
                            for k in range(KT):
                                mm = matmul_split(pe, q_ps[:, f, :], [w[i][:, k, f * P:(f + 1) * P] for i in range(2)],
                                                  [h_cols[i][:, k, tok:tok + 4 * P] for i in range(2)], k == 0, k == KT - 1)
                            mm.then_inc(q_done, 1)
                    if s < STEPS:
                        w, tok = wkv[s // NB], s % NB * P
                        pe.wait_ge(kv_copied, done(n0 + s - 2))
                        for k in range(KT):
                            mm = matmul_split(pe, kv_ps[:, s % 2, :], [h_cols[i][:, k, tok:tok + P] for i in range(2)],
                                              [w[i][:, k, :] for i in range(2)], k == 0, k == KT - 1)
                        mm.then_inc(kv_done, 1)
                    if 1 <= s < STEPS + 1:
                        n, p = n0 + s - 1, (s - 1) % 2
                        pe.wait_ge(kv_copied, done(n))
                        pe.wait_ge(kvm_masked, done(n - 1))
                        for j in range(PAIRS):
                            mm = pe.matmul(kvm_ps[:, j * 2 * AUG:(j + 1) * 2 * AUG], k_rows[p][:, j * P:(j + 1) * P],
                                           v_rows[p][:, 2 * j:2 * j + 2, :].rearrange("p h e -> p (h e)"),
                                           start=True, stop=True)
                        mm.then_inc(kvm_done, 1)
                    if 2 <= s < STEPS + 2:
                        n, p, sl = n0 + s - 2, (s - 2) % 2, s - 2
                        pe.wait_ge(kvm_masked, done(n))
                        pe.wait_ge(q_copied, done((it * (STEPS // 4) + sl // 4) * 2 + 1))
                        pe.wait_ge(o_scaled, done(n - 1))
                        for j in range(PAIRS):
                            mm = pe.matmul(num_ps[:, j * 2 * AUG:(j + 1) * 2 * AUG],
                                           q_cols[sl // 4 % 2][:, j, sl % 4 * P:(sl % 4 + 1) * P],
                                           kv_diag[p][:, j, :], start=True, stop=True)
                        mm.then_inc(num_done, 1)
                    if 3 <= s < STEPS + 3:
                        n, p = n0 + s - 3, (s - 3) % 2
                        pe.wait_ge(o_scaled, done(n))
                        pe.wait_ge(o_lo, done(n - 1))
                        for j in range(PAIRS):
                            mm = pe.transpose(turn_ps[:, j * P:(j + 1) * P],
                                              o_rows[p][:, 2 * j:2 * j + 2, :].rearrange("p h e -> p (h e)"), ident[:, :])
                        mm.then_inc(o_turned, 1)
                    if s >= 4:
                        n, p, w = n0 + s - 4, (s - 4) % 2, wo[(s - 4) // NB]
                        pe.wait_ge(o_lo, done(n))
                        pe.wait_ge(y_added, done(n - 1))
                        for j in range(PAIRS):
                            mm = matmul_split(pe, y_ps[:, :], [o_cols[p][i][:, j, :] for i in range(2)],
                                              [w[i][:, j, :] for i in range(2)], j == 0, j == PAIRS - 1)
                        mm.then_inc(y_done, 1)

        @block.vector
        def _(dve):
            start(dve, kvm_masked, den_clipped, den_inverted, o_scaled, o_lo, y_added)
            for b in range(0, NB, 2):
                if b % 4 == 0:
                    dve.wait_ge(x_in[b // 4], 16)
                ln.vector(dve, b)
            dve.wait_ge(bias_in, 16)
            dve.wait_ge(mask_cut, 2)
            with dve.Fori(0, NB) as b:
                dve.tensor_tensor(x[:, b, :], x[:, b, :], bias[:, :], ALU.add).then_inc(bias_added, 1)
            dve.wait_ge(bias_added, NB)
            with dve.Fori(0, GROUPS // 2) as it:
                n0 = it * STEPS
                for s in range(1, STEPS + 5):
                    if s < STEPS + 1:
                        n, p = n0 + s - 1, (s - 1) % 2
                        dve.wait_ge(kvm_done, done(n))
                        dve.wait_ge(num_done, done(n - 2))
                        dve.tensor_tensor(kv_diag[p][:, :, :], kvm_ps[:, 0:PAIRS * 2 * AUG].rearrange("p (j e) -> p j e", j=PAIRS),
                                          pair_mask[:, :, :, :].rearrange("p j h e -> p j (h e)"), ALU.mult)\
                            .then_inc(kvm_masked, 1)
                    if 2 <= s < STEPS + 2:
                        n, p = n0 + s - 2, (s - 2) % 2
                        dve.wait_ge(num_done, done(n))
                        dve.tensor_scalar(denom[p][:, :, :], num_heads[:, :, HD:AUG], 1e-6, None,
                                          ALU.max).then_inc(den_clipped, 1)
                        dve.wait_ge(den_clipped, done(n))
                        dve.reciprocal(inv[p][:, :, :], denom[p][:, :, :]).then_inc(den_inverted, 1)
                        dve.wait_ge(den_inverted, done(n))
                        dve.wait_ge(o_turned, done(n - 2))
                        dve.tensor_tensor(o_rows[p][:, :, :], num_heads[:, :, 0:HD],
                                          inv[p][:, :, :].to_broadcast([P, HG, HD]), ALU.mult).then_inc(o_scaled, 1)
                    if 3 <= s < STEPS + 3:
                        n, p = n0 + s - 3, (s - 3) % 2
                        dve.wait_ge(o_hi, done(n))
                        dve.tensor_tensor(o_cols[p][1][:, :, :], turn_ps[:, 0:GW].rearrange("p (j t) -> p j t", j=PAIRS),
                                          o_cols[p][0][:, :, :].bitcast(F32), ALU.subtract).then_inc(o_lo, 1)
                    if s >= 4 and s - 4 < STEPS:
                        n, b = n0 + s - 4, (s - 4) % NB
                        dve.wait_ge(y_done, done(n))
                        dve.tensor_tensor(x[:, b, :], x[:, b, :], y_ps[:, :], ALU.add).then_inc(y_added, 1)
            dve.wait_ge(y_added, done(NB * GROUPS - 1))


class CrossAttention:

    def __init__(self, nc, ctx, x, ident, ones, minus_half, ctx_dram, pos, Wq, Wkv, Wout, bout):
        sb = lambda n, s, d: ctx.enter_context(nc.sbuf_tensor("b_" + n, s, d))
        ps = lambda n, s, d: ctx.enter_context(nc.psum_tensor("b_" + n, s, d))
        sem = lambda n: ctx.enter_context(nc.semaphore("b_" + n))
        self.nc, self.x, self.ident, self.ones, self.minus_half = nc, x, ident, ones, minus_half
        self.ctx_dram, self.pos_dram, self.Wq, self.Wkv, self.Wout, self.bout = ctx_dram, pos, Wq, Wkv, Wout, bout
        D = self.D = Wq.shape[0]
        self.KT, self.CT = D // P, Wkv.shape[0] // P
        self.NB = x.shape[1]
        self.H, self.HD = 32, 16
        self.CONSTS = 12
        self.SLOT = 64
        KT, CT, NB, H, HD, SLOT = self.KT, self.CT, self.NB, self.H, self.HD, self.SLOT

        self.wq = [sb(f"wq{s}", [P, KT, D], F32R) for s in "hl"]
        self.wkv = [sb(f"wkv{s}", [P, CT, 2 * D], F32R) for s in "hl"]
        self.wo = [sb(f"wo{s}", [P, KT, D], F32R) for s in "hl"]
        self.bias = sb("bias", [P, D], F32)
        self.pos = sb("pos", [P, NB, 2], F32)
        self.half_pi = sb("half_pi", [P, 1], F32)
        self.angle = sb("angle", [P, NB, 2, 4], F32)
        self.turns = sb("turns", [P, NB, 2, 4], F32)
        self.tables = sb("tables", [P, NB, 2, 2, 4, 2], F32)
        self.cos, self.sin = self.tables[:, :, 0, :, :, :], self.tables[:, :, 1, :, :, :]
        self.tables_now = sb("tables_now", [P, 2, HD], F32)
        self.stats = sb("stats", [P, NB, 6], F32)
        self.mean_var = sb("mean_var", [P, NB, 2], F32)
        self.var_eps = sb("var_eps", [P, NB], F32)
        self.rstd = sb("rstd", [P, NB], F32)
        self.normed = sb("normed", [P, D], F32)
        self.x_cols = [sb(f"x_cols{s}", [P, KT, P], F32R) for s in "hl"]
        self.ctx_rows = [sb(f"ctx_rows{i}", [P, CT * P], F32) for i in range(2)]
        self.ctx_cols = [sb(f"ctx_cols{s}", [P, CT, P], F32R) for s in "hl"]
        work = sb("work", [P, 12, D], F32)
        self.raw = [work[:, 0:4, :], work[:, 4:8, :].rearrange("p (k a) n -> p k (a n)", k=CT), work[:, 8:12, :]]
        self.rows = {"q": work[:, 0, :], "k": work[:, 1, :]}
        self.by_cos, self.by_sin = work[:, 2, :], work[:, 3, :]
        self.rotated = {"q": work[:, 4, :], "k": work[:, 5, :]}
        self.probs = [work[:, 6 + 2 * i:8 + 2 * i, :].rearrange("p a (h t) -> p (a h) t", t=P) for i in range(2)]
        self.o_cols = work[:, 10:12, :].rearrange("p a (g t) -> p (a g) t", t=P)
        self.slots = {w: sb(f"{w}_slots", [P, H, SLOT], F32R) for w in "qk"}
        self.q_cols = [sb(f"q_cols{i}", [P, H // 2, P], F32R) for i in range(2)]
        self.k_cols = [sb(f"k_cols{i}", [P, H // 2, 2, P], F32R) for i in range(2)]
        self.values = [sb(f"values{i}", [P, H, 32], F32) for i in range(2)]
        self.row_max = sb("row_max", [P, 8], F32)
        self.max_rows = sb("max_rows", [P, P], BF16)
        self.max_cols = sb("max_cols", [P, P], BF16)
        self.minus = sb("minus", [P, 8], F32)
        self.minus_head = sb("minus_head", [P, 8, P], BF16)
        self.ident16 = sb("ident16", [P, P], BF16)
        self.ident_r = sb("ident_r", [P, P], F32R)
        self.inv_sum = sb("inv_sum", [P, H, 1], F32)
        self.attn = sb("attn", [P, H, HD], F32)
        self.attn_cols = [sb(f"attn_cols{s}", [P, KT, P], F32R) for s in "hl"]

        self.ps_x = ps("ps_x", [P, 512], F32)
        self.ps_c = ps("ps_c", [P, 512], F32)
        self.ps_l = ps("ps_l", [P, 8, P], F32)
        self.ps_t = ps("ps_t", [P, 8, P], F32)
        self.ps_o = ps("ps_o", [P, H // 4, P], F32)
        self.out_heads = self.ps_o[:, :, :].rearrange("p g (h e) -> p (g h) e", e=32)

        self.w_in = [sem(f"w_in{i}") for i in range(3)]
        self.pos_in, self.bias_in = sem("pos_in"), sem("bias_in")
        self.ctx_in = [sem(f"ctx_in{i}") for i in range(2)]
        self.const_set = sem("const_set")
        self.minus_made = sem("minus_made")
        self.w_hi = sem("w_hi")
        self.w_lo = sem("w_lo")
        self.angle_step = sem("angle_step")
        self.trig = sem("trig")
        self.trig_signed = sem("trig_signed")
        self.stats_done = sem("stats_done")
        self.mean_done = sem("mean_done")
        self.var_done = sem("var_done")
        self.rstd_done = sem("rstd_done")
        self.normed_done = sem("normed_done")
        self.tables_copied = sem("tables_copied")
        self.ctx_turned = sem("ctx_turned")
        self.ctx_hi = sem("ctx_hi")
        self.ctx_lo = sem("ctx_lo")
        self.x_turned = sem("x_turned")
        self.x_hi = sem("x_hi")
        self.x_lo = sem("x_lo")
        self.k_done = sem("k_done")
        self.k_copied = sem("k_copied")
        self.v_done = sem("v_done")
        self.v_copied = sem("v_copied")
        self.q_done = sem("q_done")
        self.q_copied = sem("q_copied")
        self.rope_parts = sem("rope_parts")
        self.k_rotated = sem("k_rotated")
        self.q_rotated = sem("q_rotated")
        self.k_hi = sem("k_hi")
        self.k_lo = sem("k_lo")
        self.q_hi = sem("q_hi")
        self.q_lo = sem("q_lo")
        self.k_turned = sem("k_turned")
        self.k_cols_done = sem("k_cols_done")
        self.q_turned = sem("q_turned")
        self.q_cols_done = sem("q_cols_done")
        self.biased = sem("biased")
        self.logits_done = sem("logits_done")
        self.maxed = sem("maxed")
        self.o_copied = sem("o_copied")
        self.o_turned = sem("o_turned")
        self.ident_made = sem("ident_made")
        self.max_hi = sem("max_hi")
        self.max_lo = sem("max_lo")
        self.max_turned = sem("max_turned")
        self.max_copied = sem("max_copied")
        self.logits_t_done = sem("logits_t_done")
        self.exp_done = sem("exp_done")
        self.values_done = sem("values_done")
        self.inverted = sem("inverted")
        self.scaled = sem("scaled")
        self.attn_turned = sem("attn_turned")
        self.attn_hi = sem("attn_hi")
        self.attn_lo = sem("attn_lo")
        self.out_done = sem("out_done")
        self.added = sem("added")

    def turn_ctx(self, pe, m, p):
        pe.wait_ge(self.ctx_in[p], (m // 2 + 1) * 16 if isinstance(m, int) else (m + 2 - p) * 8)
        pe.wait_ge(self.k_cols_done, done(4 * m - 1))
        for k in range(self.CT):
            mm = pe.transpose(self.ps_c[:, k * P:(k + 1) * P], self.ctx_rows[p][:, k * P:(k + 1) * P], self.ident[:, :])
        mm.then_inc(self.ctx_turned, 1)

    def project_k(self, pe, m):
        pe.wait_ge(self.ctx_lo, done(m))
        for k in range(self.CT):
            mm = matmul_split(pe, self.ps_c[:, :], [c[:, k, :] for c in self.ctx_cols],
                              [w[:, k, 0:self.D] for w in self.wkv], k == 0, k == self.CT - 1)
        mm.then_inc(self.k_done, 1)

    def project_v(self, pe, m):
        pe.wait_ge(self.k_copied, done(m))
        for k in range(self.CT):
            mm = matmul_split(pe, self.ps_c[:, :], [c[:, k, :] for c in self.ctx_cols],
                              [w[:, k, self.D:2 * self.D] for w in self.wkv], k == 0, k == self.CT - 1)
        mm.then_inc(self.v_done, 1)

    def turn_x(self, pe, m):
        pe.wait_ge(self.normed_done, done(m))
        pe.wait_ge(self.added, done(m - 2))
        pe.wait_ge(self.q_cols_done, done(4 * m - 1))
        for k in range(self.KT):
            mm = pe.transpose(self.ps_x[:, k * P:(k + 1) * P], self.normed[:, k * P:(k + 1) * P], self.ident[:, :])
        mm.then_inc(self.x_turned, 1)

    def project_q(self, pe, m):
        pe.wait_ge(self.x_lo, done(m))
        for k in range(self.KT):
            mm = matmul_split(pe, self.ps_x[:, :], [c[:, k, :] for c in self.x_cols],
                              [w[:, k, :] for w in self.wq], k == 0, k == self.KT - 1)
        mm.then_inc(self.q_done, 1)

    def turn_slots(self, pe, which, m, j):
        if which == "k":
            into, ready, before, turned = self.ps_c, self.k_lo, self.v_copied, self.k_turned
            left = self.k_cols_done
        else:
            into, ready, before, turned = self.ps_x, self.q_hi, self.q_copied, self.q_turned
            left = self.q_cols_done
            pe.wait_ge(self.q_lo, done(m))
        pe.wait_ge(ready, done(m))
        if j == 0:
            pe.wait_ge(before, done(m))
        else:
            pe.wait_ge(left, done(4 * m + j - 1))
        for i in range(4):
            t = 4 * j + i
            mm = pe.transpose(into[:, i * P:(i + 1) * P].bitcast(F32R),
                              self.slots[which][:, 2 * t:2 * t + 2, :].rearrange("p h s -> p (h s)"), self.ident_r[:, :])
        mm.then_inc(turned, 1)

    def logits(self, pe, b, p, c):
        n = 4 * b + c
        pe.wait_ge(self.q_cols_done, done(n))
        pe.wait_ge(self.k_cols_done, done(n))
        pe.wait_ge(self.max_copied, done(n - 1))
        for i in range(4):
            t = 4 * c + i
            mm = pe.matmul(self.ps_l[:, 2 * i:2 * i + 2, :].rearrange("p r k -> p (r k)"), self.q_cols[p][:, t, :],
                           self.k_cols[p][:, t, :, :].rearrange("p r k -> p (r k)"), start=True, stop=True)
        mm.then_inc(self.logits_done, 1)

    def turn_max(self, pe, b, c):
        pe.wait_ge(self.max_lo, done(4 * b + c))
        pe.transpose(self.ps_l[:, 0, 0:P // 2].bitcast(BF16), self.max_rows[:, :], self.ident16[:, :])\
            .then_inc(self.max_turned, 1)

    def logits_t(self, pe, b, p, c):
        n = 4 * b + c
        pe.wait_ge(self.max_copied, done(n))
        pe.wait_ge(self.exp_done, done(n - 1))
        for h in range(8):
            t = 4 * c + h // 2
            pe.matmul(self.ps_t[:, h, :], self.k_cols[p][:, t, h % 2, :], self.q_cols[p][:, t, :], start=True, stop=False)
            mm = pe.matmul(self.ps_t[:, h, :], self.minus_head[:, h, :], self.max_cols[:, :], start=False, stop=True)
        mm.then_inc(self.logits_t_done, 1)

    def weigh_values(self, pe, b, p, c):
        n = 4 * b + c
        pe.wait_ge(self.exp_done, done(n))
        pe.wait_ge(self.v_copied, done(b))
        pe.wait_ge(self.scaled, done(b - 1))
        for h in range(8):
            j = h % 4
            mm = pe.matmul(self.ps_o[32 * j:32 * j + 32, 2 * c + h // 4, :], self.values[p][:, 8 * c + h, :],
                           self.probs[c % 2][:, h, :], start=True, stop=True)
        mm.then_inc(self.values_done, 1)

    def turn_out(self, pe, n):
        pe.wait_ge(self.o_copied, done(n))
        for g in range(self.H // 4):
            mm = pe.transpose(self.ps_o[:, g, :], self.o_cols[:, g, :], self.ident[:, :])
        mm.then_inc(self.o_turned, 1)

    def turn_attn(self, pe, n):
        pe.wait_ge(self.scaled, done(n))
        pe.wait_ge(self.q_cols_done, done(4 * n + 7 if not (isinstance(n, int) and n == self.NB - 1) else 4 * n + 3))
        rows = self.attn[:, :, :].rearrange("p h e -> p (h e)")
        for k in range(self.KT):
            mm = pe.transpose(self.ps_x[:, k * P:(k + 1) * P], rows[:, k * P:(k + 1) * P], self.ident[:, :])
        mm.then_inc(self.attn_turned, 1)

    def project_out(self, pe, n):
        pe.wait_ge(self.attn_lo, done(n))
        for k in range(self.KT):
            mm = matmul_split(pe, self.ps_x[:, :], [c[:, k, :] for c in self.attn_cols],
                              [w[:, k, :] for w in self.wo], k == 0, k == self.KT - 1)
        mm.then_inc(self.out_done, 1)

    def tensor_prepare_first(self, pe):
        self.turn_ctx(pe, 0, 0)
        self.turn_x(pe, 0)
        self.project_k(pe, 0)
        self.project_v(pe, 0)
        self.project_q(pe, 0)
        for which in "kq":
            for j in range(4):
                self.turn_slots(pe, which, 0, j)

    def tensor_step(self, pe, b, p, prepare, finish):
        m, n = b + 1, b - 1
        self.logits(pe, b, p, 0)
        if finish:
            self.turn_out(pe, n)
        if prepare:
            self.turn_ctx(pe, m, 1 - p)
            self.project_k(pe, m)
        self.turn_max(pe, b, 0)
        if finish:
            self.turn_attn(pe, n)
        self.logits(pe, b, p, 1)
        self.logits_t(pe, b, p, 0)
        if finish:
            self.project_out(pe, n)
        if prepare:
            self.project_v(pe, m)
        self.turn_max(pe, b, 1)
        if prepare:
            self.turn_x(pe, m)
        self.weigh_values(pe, b, p, 0)
        self.logits(pe, b, p, 2)
        self.logits_t(pe, b, p, 1)
        if prepare:
            self.turn_slots(pe, "k", m, 0)
            self.turn_slots(pe, "k", m, 1)
        self.turn_max(pe, b, 2)
        if prepare:
            self.project_q(pe, m)
        self.logits(pe, b, p, 3)
        self.weigh_values(pe, b, p, 1)
        self.logits_t(pe, b, p, 2)
        if prepare:
            self.turn_slots(pe, "k", m, 2)
            self.turn_slots(pe, "k", m, 3)
        self.turn_max(pe, b, 3)
        self.weigh_values(pe, b, p, 2)
        if prepare:
            self.turn_slots(pe, "q", m, 0)
        self.logits_t(pe, b, p, 3)
        if prepare:
            self.turn_slots(pe, "q", m, 1)
        self.weigh_values(pe, b, p, 3)
        if prepare:
            self.turn_slots(pe, "q", m, 2)
            self.turn_slots(pe, "q", m, 3)

    def ctx_high(self, act, m):
        act.wait_ge(self.ctx_turned, done(m))
        act.wait_ge(self.v_done, done(m - 1))
        act.activation(self.ctx_cols[0][:, :, :], self.ps_c[:, 0:self.CT * P].rearrange("p (k t) -> p k t", k=self.CT),
                       ACT.Copy).then_inc(self.ctx_hi, 1)

    def x_high(self, act, m):
        act.wait_ge(self.x_turned, done(m))
        act.wait_ge(self.q_done, done(m - 1))
        act.activation(self.x_cols[0][:, :, :], self.ps_x[:, :].rearrange("p (k t) -> p k t", k=self.KT),
                       ACT.Copy).then_inc(self.x_hi, 1)

    def copy_k(self, act, m):
        act.wait_ge(self.k_done, done(m))
        act.wait_ge(self.k_rotated, done(m - 1))
        act.activation(self.rows["k"][:, :], self.ps_c[:, :], ACT.Copy).then_inc(self.k_copied, 1)

    def copy_v(self, act, m, p):
        act.wait_ge(self.v_done, done(m))
        act.wait_ge(self.values_done, done(4 * m - 5))
        act.activation(self.values[p][:, :, 0:self.HD], self.ps_c[:, :].rearrange("p (h e) -> p h e", h=self.H),
                       ACT.Copy).then_inc(self.v_copied, 1)

    def copy_q(self, act, m):
        act.wait_ge(self.q_done, done(m))
        act.wait_ge(self.q_rotated, done(m - 1))
        act.activation(self.rows["q"][:, :], self.ps_x[:, :], ACT.Copy).then_inc(self.q_copied, 1)

    def copy_q_cols(self, act, m, p, j):
        act.wait_ge(self.q_turned, done(4 * m + j))
        act.wait_ge(self.logits_t_done, done(4 * m - 5))
        act.activation(self.q_cols[p][:, 4 * j:4 * j + 4, :], self.ps_x[:, :].rearrange("p (i t) -> p i t", i=4),
                       ACT.Copy).then_inc(self.q_cols_done, 1)

    def copy_max(self, act, b, c):
        act.wait_ge(self.max_turned, done(4 * b + c))
        act.wait_ge(self.logits_t_done, done(4 * b + c - 1))
        act.activation(self.max_cols[:, :], self.ps_l[:, 0, 0:P // 2].bitcast(BF16), ACT.Copy).then_inc(self.max_copied, 1)

    def exponential(self, act, b, c):
        n = 4 * b + c
        act.wait_ge(self.logits_t_done, done(n))
        act.wait_ge(self.values_done, done(n - 2))
        act.activation(self.probs[c % 2][:, :, :], self.ps_t[:, :, :], ACT.Exp, scale=1.0 / math.sqrt(self.HD))\
            .then_inc(self.exp_done, 1)

    def copy_out(self, act, b):
        act.wait_ge(self.values_done, done(4 * b + 3))
        act.wait_ge(self.o_turned, done(b - 1))
        act.activation(self.o_cols[:, :, :], self.ps_o[:, :, :], ACT.Copy).then_inc(self.o_copied, 1)

    def attn_high(self, act, n):
        act.wait_ge(self.attn_turned, done(n))
        act.wait_ge(self.out_done, done(n - 1))
        act.activation(self.attn_cols[0][:, :, :], self.ps_x[:, :].rearrange("p (k t) -> p k t", k=self.KT),
                       ACT.Copy).then_inc(self.attn_hi, 1)

    def scalar_prepare_first(self, act):
        self.ctx_high(act, 0)
        self.x_high(act, 0)
        self.copy_k(act, 0)
        self.copy_v(act, 0, 0)
        self.copy_q(act, 0)
        for j in range(4):
            self.copy_q_cols(act, 0, 0, j)

    def scalar_step(self, act, b, p, prepare, finish):
        m, n = b + 1, b - 1
        if prepare:
            self.ctx_high(act, m)
            self.copy_k(act, m)
        self.copy_max(act, b, 0)
        if finish:
            self.attn_high(act, n)
        self.exponential(act, b, 0)
        if prepare:
            self.copy_v(act, m, 1 - p)
        self.copy_max(act, b, 1)
        if prepare:
            self.x_high(act, m)
        self.exponential(act, b, 1)
        self.copy_max(act, b, 2)
        if prepare:
            self.copy_q(act, m)
        self.exponential(act, b, 2)
        self.copy_max(act, b, 3)
        if prepare:
            self.copy_q_cols(act, m, 1 - p, 0)
        self.exponential(act, b, 3)
        if prepare:
            self.copy_q_cols(act, m, 1 - p, 1)
        self.copy_out(act, b)
        if prepare:
            self.copy_q_cols(act, m, 1 - p, 2)
            self.copy_q_cols(act, m, 1 - p, 3)

    def normalise(self, dve, m):
        at = slice(m, m + 1) if isinstance(m, int) else bass.ds(m, 1)
        row = self.x[:, at, :].rearrange("p b d -> p (b d)")
        dve.wait_ge(self.x_turned, done(m - 1))
        dve.tensor_scalar(self.normed[:, :], row, self.mean_var[:, at, 0:1].rearrange("p b e -> p (b e)"),
                          self.rstd[:, at], ALU.subtract, ALU.mult).then_inc(self.normed_done, 1)

    def copy_tables(self, dve, m):
        at = slice(m, m + 1) if isinstance(m, int) else bass.ds(m, 1)
        dve.wait_ge(self.q_rotated, done(m - 1))
        dve.tensor_copy(self.tables_now[:, :, :], self.tables[:, at, :, :, :, :].rearrange("p b t a f e -> p (b t) (a f e)"))\
            .then_inc(self.tables_copied, 1)

    def ctx_low(self, dve, m):
        dve.wait_ge(self.ctx_hi, done(m))
        dve.tensor_tensor(self.ctx_cols[1][:, :, :], self.ps_c[:, 0:self.CT * P].rearrange("p (k t) -> p k t", k=self.CT),
                          self.ctx_cols[0][:, :, :].bitcast(F32), ALU.subtract).then_inc(self.ctx_lo, 1)

    def x_low(self, dve, m):
        dve.wait_ge(self.x_hi, done(m))
        dve.tensor_tensor(self.x_cols[1][:, :, :], self.ps_x[:, :].rearrange("p (k t) -> p k t", k=self.KT),
                          self.x_cols[0][:, :, :].bitcast(F32), ALU.subtract).then_inc(self.x_lo, 1)

    def fill_slots(self, dve, which, m):
        rot = self.rotated[which][:, :].rearrange("p (h e) -> p h e", h=self.H)
        slots, HD = self.slots[which], self.HD
        rotated, turned, hi_done, lo_done = ((self.k_rotated, self.k_turned, self.k_hi, self.k_lo) if which == "k" else
                                             (self.q_rotated, self.q_turned, self.q_hi, self.q_lo))
        dve.wait_ge(rotated, done(m))
        dve.wait_ge(turned, done(4 * m - 1))
        lo_at = 2 if which == "k" else 1
        hi_at = slots[:, :, 0:3 * HD].rearrange("p h (s e) -> p h s e", s=3)[:, :, 0:4 - lo_at:3 - lo_at, :]
        dve.tensor_copy(hi_at, rot.unsqueeze(2).to_broadcast([P, self.H, 2, HD])).then_inc(hi_done, 1)
        dve.wait_ge(hi_done, done(m))
        dve.tensor_tensor(slots[:, :, lo_at * HD:(lo_at + 1) * HD], rot, slots[:, :, 0:HD].bitcast(F32),
                          ALU.subtract).then_inc(lo_done, 1)

    def copy_k_cols(self, dve, m, p, j):
        dve.wait_ge(self.k_turned, done(4 * m + j))
        dve.wait_ge(self.logits_t_done, done(4 * m - 5))
        for r in range(2):
            at = slice(self.SLOT * r, self.SLOT * (r + 1))
            ins = dve.tensor_copy(self.k_cols[p][at, 4 * j:4 * j + 4, r, :],
                                  self.ps_c[at, :].rearrange("p (i t) -> p i t", i=4))
        ins.then_inc(self.k_cols_done, 1)

    def maxima(self, dve, b, c):
        n = 4 * b + c
        dve.wait_ge(self.logits_done, done(n))
        dve.tensor_reduce(self.row_max[:, :], self.ps_l[:, :, :], AX_X, ALU.max).then_inc(self.maxed, 1)
        dve.wait_ge(self.maxed, done(n))
        dve.wait_ge(self.max_turned, done(n - 1))
        dve.tensor_copy(self.max_rows[:, 0:8], self.row_max[:, :]).then_inc(self.max_hi, 1)
        dve.wait_ge(self.max_hi, done(n))
        dve.tensor_tensor(self.max_rows[:, 8:16], self.row_max[:, :], self.max_rows[:, 0:8], ALU.subtract)\
            .then_inc(self.max_lo, 1)

    def scale_heads(self, dve, b):
        dve.wait_ge(self.o_turned, done(b))
        dve.reciprocal(self.inv_sum[:, :, :], self.out_heads[:, :, self.HD:self.HD + 1]).then_inc(self.inverted, 1)
        dve.wait_ge(self.inverted, done(b))
        dve.wait_ge(self.attn_turned, done(b - 1))
        dve.tensor_tensor(self.attn[:, :, :], self.out_heads[:, :, 0:self.HD],
                          self.inv_sum[:, :, :].to_broadcast([P, self.H, self.HD]), ALU.mult).then_inc(self.scaled, 1)

    def attn_low(self, dve, n):
        dve.wait_ge(self.attn_hi, done(n))
        dve.tensor_tensor(self.attn_cols[1][:, :, :], self.ps_x[:, :].rearrange("p (k t) -> p k t", k=self.KT),
                          self.attn_cols[0][:, :, :].bitcast(F32), ALU.subtract).then_inc(self.attn_lo, 1)

    def add_output(self, dve, n):
        at = slice(n, n + 1) if isinstance(n, int) else bass.ds(n, 1)
        row = self.x[:, at, :].rearrange("p b d -> p (b d)")
        dve.wait_ge(self.out_done, done(n))
        dve.wait_ge(self.biased, done(n))
        dve.tensor_tensor(row, row, self.ps_x[:, :], ALU.add).then_inc(self.added, 1)

    def vector_prepare_first(self, dve):
        self.normalise(dve, 0)
        self.copy_tables(dve, 0)
        self.ctx_low(dve, 0)
        self.x_low(dve, 0)
        self.fill_slots(dve, "k", 0)
        for j in range(4):
            self.copy_k_cols(dve, 0, 0, j)
        self.fill_slots(dve, "q", 0)

    def vector_step(self, dve, b, p, prepare, finish):
        m, n = b + 1, b - 1
        self.maxima(dve, b, 0)
        if prepare:
            self.ctx_low(dve, m)
        if finish:
            self.scale_heads(dve, n)
            self.attn_low(dve, n)
        if prepare:
            self.normalise(dve, m)
            self.copy_tables(dve, m)
        if finish:
            self.add_output(dve, n)
        self.maxima(dve, b, 1)
        if prepare:
            self.x_low(dve, m)
            self.fill_slots(dve, "k", m)
        self.maxima(dve, b, 2)
        if prepare:
            self.copy_k_cols(dve, m, 1 - p, 0)
            self.copy_k_cols(dve, m, 1 - p, 1)
        self.maxima(dve, b, 3)
        if prepare:
            self.copy_k_cols(dve, m, 1 - p, 2)
            self.copy_k_cols(dve, m, 1 - p, 3)
            self.fill_slots(dve, "q", m)

    def rotate(self, pool, which, m):
        n = 2 * m + (which == "q")
        copied, rotated, split = ((self.k_copied, self.k_rotated, self.k_lo) if which == "k" else
                                  (self.q_copied, self.q_rotated, self.q_lo))
        full = [P, self.H, self.HD]
        cos = self.tables_now[:, 0:1, :].to_broadcast(full)
        sin = self.tables_now[:, 1:2, :].rearrange("p a (f e) -> p a f e", e=2).to_broadcast([P, self.H, self.HD // 2, 2])
        rows = self.rows[which][:, :].rearrange("p (h e) -> p h e", h=self.H)
        swapped = self.rows[which][:, :].rearrange("p (h f e) -> p h f e", h=self.H, e=2)[:, :, :, ::-1]
        pool.wait_ge(copied, done(m))
        pool.wait_ge(self.tables_copied, done(m))
        pool.tensor_tensor(self.by_cos[:, :].rearrange("p (h e) -> p h e", h=self.H), rows, cos, ALU.mult)
        pool.tensor_tensor(self.by_sin[:, :].rearrange("p (h f e) -> p h f e", h=self.H, e=2), swapped, sin, ALU.mult)\
            .then_inc(self.rope_parts, 1)
        pool.wait_ge(self.rope_parts, done(n))
        pool.wait_ge(split, done(m - 1))
        pool.tensor_tensor(self.rotated[which][:, :], self.by_cos[:, :], self.by_sin[:, :], ALU.add).then_inc(rotated, 1)
        pool.wait_ge(rotated, done(m))

    def add_bias(self, pool, m):
        at = slice(m, m + 1) if isinstance(m, int) else bass.ds(m, 1)
        row = self.x[:, at, :].rearrange("p b d -> p (b d)")
        pool.wait_ge(self.normed_done, done(m))
        pool.wait_ge(self.bias_in, 16)
        pool.tensor_tensor(row, row, self.bias[:, :], ALU.add).then_inc(self.biased, 1)

    def pool_step(self, pool, m):
        self.rotate(pool, "k", m)
        self.add_bias(pool, m)
        self.rotate(pool, "q", m)

    def run(self, block):
        NB, H, HD = self.NB, self.H, self.HD
        TWO_PI = 2 * math.pi

        @block.sync
        def _(sp):
            for raw, w, got in zip(self.raw, (self.Wq, self.Wkv, self.Wout), self.w_in):
                sp.dma_start(raw, w.rearrange("(k p) n -> p k n", p=P)).then_inc(got, 16)
            sp.dma_start(self.pos[:, :, :], self.pos_dram.rearrange("b t a -> t b a")).then_inc(self.pos_in, 16)
            sp.dma_start(self.bias[:, :], self.bout.rearrange("(a d) -> a d", a=1).to_broadcast([P, self.D]))\
                .then_inc(self.bias_in, 16)
            for p in range(2):
                sp.dma_start(self.ctx_rows[p][:, :], self.ctx_dram[p]).then_inc(self.ctx_in[p], 16)
            with sp.Fori(1, NB // 2) as i:
                for p in range(2):
                    m = i * 2 + p
                    sp.wait_ge(self.ctx_turned, done(m - 2))
                    sp.dma_start(self.ctx_rows[p][:, :], self.ctx_dram[bass.ds(m, 1)].rearrange("b t d -> (b t) d"))\
                        .then_inc(self.ctx_in[p], 16)

        @block.gpsimd
        def _(pool):
            start(pool, self.rope_parts, self.k_rotated, self.q_rotated, self.biased)
            for which in "qk":
                pool.memset(self.slots[which][:, :, 3 * HD:self.SLOT].bitcast(F32), 0.0).then_inc(self.const_set, 1)
            pool.memset(self.max_rows[:, :], 0.0).then_inc(self.const_set, 1)
            for i in range(2):
                pool.memset(self.values[i][:, :, HD:HD + 1], 1.0).then_inc(self.const_set, 1)
                pool.memset(self.values[i][:, :, HD + 1:32], 0.0).then_inc(self.const_set, 1)
                pool.memset(self.k_cols[i][0:self.SLOT, :, 1, :].bitcast(F32), 0.0).then_inc(self.const_set, 1)
            pool.memset(self.half_pi[:, :], math.pi / 2).then_inc(self.const_set, 1)
            pool.wait_ge(self.const_set, self.CONSTS - 2)
            for i in range(2):
                pool.memset(self.k_cols[i][self.SLOT:P, :, 0, :].bitcast(F32), 0.0).then_inc(self.const_set, 1)
            pool.wait_ge(self.const_set, self.CONSTS)
            pool.wait_ge(self.var_done, 1)
            pool.tensor_tensor(self.rstd[:, :], self.var_eps[:, :], self.minus_half[:, :].to_broadcast([P, NB]),
                               ALU.pow).then_inc(self.rstd_done, 1)
            pool.wait_ge(self.rstd_done, 1)
            self.pool_step(pool, 0)
            self.pool_step(pool, 1)
            with pool.Fori(1, NB // 2) as i:
                for p in range(2):
                    self.pool_step(pool, i * 2 + p)

        @block.scalar
        def _(act):
            start(act, self.ctx_hi, self.x_hi, self.k_copied, self.v_copied, self.q_copied, self.q_cols_done,
                  self.max_copied, self.exp_done, self.o_copied, self.attn_hi)
            for n, (raw, w) in enumerate(zip(self.raw, (self.wq, self.wkv, self.wo))):
                act.wait_ge(self.w_in[n], 16)
                act.activation(w[0][:, :, :], raw, ACT.Copy).then_inc(self.w_hi, 1)
            act.wait_ge(self.const_set, self.CONSTS)
            act.wait_ge(self.angle_step, 10)
            act.activation(self.sin[:, :, :, :, 1], self.angle[:, :, :, :], ACT.Sin)
            act.activation(self.turns[:, :, :, :], self.angle[:, :, :, :], ACT.Abs).then_inc(self.trig, 1)
            act.wait_ge(self.trig, 1)
            for e in range(2):
                ins = act.activation(self.cos[:, :, :, :, e], self.turns[:, :, :, :], ACT.Sin, bias=self.half_pi[:, :],
                                     scale=-1.0)
            ins.then_inc(self.trig, 1)
            self.scalar_prepare_first(act)
            self.scalar_step(act, 0, 0, True, False)
            with act.Fori(0, (NB - 2) // 2) as i:
                for q in range(2):
                    self.scalar_step(act, i * 2 + 1 + q, (1 + q) % 2, True, True)
            self.scalar_step(act, NB - 1, 1, False, True)
            self.attn_high(act, NB - 1)

        @block.vector
        def _(dve):
            start(dve, self.normed_done, self.tables_copied, self.ctx_lo, self.x_lo, self.k_hi, self.k_lo, self.q_hi, self.q_lo,
                  self.k_cols_done, self.maxed, self.max_hi, self.max_lo, self.inverted, self.scaled, self.attn_lo,
                  self.added)
            for b in range(NB):
                dve.bn_stats(self.stats[:, b, :], self.x[:, b, :]).then_inc(self.stats_done, 1)
            dve.wait_ge(self.stats_done, NB)
            for b in range(NB):
                dve.bn_aggr(self.mean_var[:, b, :], self.stats[:, b, :]).then_inc(self.mean_done, 1)
            dve.wait_ge(self.mean_done, NB)
            dve.tensor_scalar(self.var_eps[:, :], self.mean_var[:, :, 1], EPS_LN, None, ALU.add).then_inc(self.var_done, 1)
            dve.wait_ge(self.pos_in, 16)
            steps = [0]

            def stepped(ins):
                ins.then_inc(self.angle_step, 1)
                steps[0] += 1
                dve.wait_ge(self.angle_step, steps[0])

            for f in range(4):
                stepped(dve.tensor_scalar(self.angle[:, :, :, f], self.pos[:, :, :], 10000.0 ** (-f / 4), None, ALU.mult))
            ROUND = 1.5 * 2.0 ** 23
            stepped(dve.tensor_scalar(self.turns[:, :, :, :], self.angle[:, :, :, :], 1 / TWO_PI, ROUND, ALU.mult, ALU.add))
            stepped(dve.tensor_scalar(self.turns[:, :, :, :], self.turns[:, :, :, :], ROUND, None, ALU.subtract))
            high = 6.28125
            middle = math.floor((TWO_PI - high) * 2 ** 21) / 2 ** 21
            for part in (high, middle, TWO_PI - high - middle):
                stepped(dve.scalar_tensor_tensor(self.angle[:, :, :, :].rearrange("p b a f -> p (b a f)"),
                                                 self.turns[:, :, :, :].rearrange("p b a f -> p (b a f)"), -part,
                                                 self.angle[:, :, :, :].rearrange("p b a f -> p (b a f)"), ALU.mult, ALU.add))
            stepped(dve.tensor_scalar(self.angle[:, :, :, :], self.angle[:, :, :, :], 3.1415925, -3.1415925, ALU.min, ALU.max))
            for n, (raw, w) in enumerate(zip(self.raw, (self.wq, self.wkv, self.wo))):
                dve.wait_ge(self.w_hi, n + 1)
                dve.tensor_tensor(w[1][:, :, :], raw, w[0][:, :, :].bitcast(F32), ALU.subtract).then_inc(self.w_lo, 1)
            dve.tensor_copy(self.ident16[:, :], self.ident[:, :]).then_inc(self.ident_made, 1)
            dve.tensor_copy(self.ident_r[:, :], self.ident[:, :]).then_inc(self.ident_made, 1)
            dve.tensor_reduce(self.minus[:, :], self.ident[:, 0:16].rearrange("p (a h) -> p h a", a=2), AX_X, ALU.add,
                              negate=True).then_inc(self.minus_made, 1)
            dve.wait_ge(self.minus_made, 1)
            dve.tensor_copy(self.minus_head[:, :, :], self.minus[:, :].unsqueeze(2).to_broadcast([P, 8, P]))\
                .then_inc(self.minus_made, 1)
            dve.wait_ge(self.trig, 2)
            dve.tensor_scalar(self.sin[:, :, :, :, 0], self.sin[:, :, :, :, 1], -1.0, None, ALU.mult).then_inc(self.trig_signed, 1)
            dve.wait_ge(self.trig_signed, 1)
            dve.wait_ge(self.rstd_done, 1)
            dve.wait_ge(self.const_set, self.CONSTS)
            self.vector_prepare_first(dve)
            self.vector_step(dve, 0, 0, True, False)
            with dve.Fori(0, (NB - 2) // 2) as i:
                for q in range(2):
                    self.vector_step(dve, i * 2 + 1 + q, (1 + q) % 2, True, True)
            self.vector_step(dve, NB - 1, 1, False, True)
            self.scale_heads(dve, NB - 1)
            self.attn_low(dve, NB - 1)
            self.add_output(dve, NB - 1)
            dve.wait_ge(self.added, done(NB - 1))

        @block.tensor
        def _(pe):
            start(pe, self.ctx_turned, self.x_turned, self.k_done, self.v_done, self.q_done, self.k_turned,
                  self.q_turned, self.logits_done, self.max_turned, self.logits_t_done, self.values_done,
                  self.attn_turned, self.out_done, self.o_turned)
            pe.wait_ge(self.w_lo, 3)
            pe.wait_ge(self.minus_made, 2)
            pe.wait_ge(self.ident_made, 2)
            self.tensor_prepare_first(pe)
            pe.wait_ge(self.const_set, self.CONSTS)
            self.tensor_step(pe, 0, 0, True, False)
            with pe.Fori(0, (NB - 2) // 2) as i:
                for q in range(2):
                    self.tensor_step(pe, i * 2 + 1 + q, (1 + q) % 2, True, True)
            self.tensor_step(pe, NB - 1, 1, False, True)
            self.turn_out(pe, NB - 1)
            self.turn_attn(pe, NB - 1)
            self.project_out(pe, NB - 1)


class FeedForward:

    def __init__(self, nc, ctx, x, ident, ones, minus_half, gu_packed, gu_scales, down_packed, down_scales, out):
        sb = lambda n, s, d: ctx.enter_context(nc.sbuf_tensor("c_" + n, s, d))
        ps = lambda n, s, d: ctx.enter_context(nc.psum_tensor("c_" + n, s, d))
        sem = lambda n: ctx.enter_context(nc.semaphore("c_" + n))
        self.nc, self.x, self.ident, self.out = nc, x, ident, out
        self.gu_packed, self.gu_scales, self.down_packed, self.down_scales = gu_packed, gu_scales, down_packed, down_scales
        NB = self.NB = x.shape[1]
        D = self.D = x.shape[2]
        KT = self.KT = D // P
        C = self.C = gu_packed.shape[0] // 2 // P
        self.BLK = 4
        self.TILES_AT = ((), (), (0, 1), (2,))
        self.WG, self.WD = D // 8, P // 8
        self.WORDS = 2 * self.WG + KT * self.WD

        self.x_cols = [sb(f"x_cols{s}", [P, KT, NB * P], F32R) for s in "hl"]
        self.y = sb("y", [P, NB, D], F32)
        self.gu_s16 = sb("gu_s16", [KT, 2 * C * P], F16)
        self.gu_s = sb("gu_s", [P, 2, C, KT], F32)
        self.down_s16 = sb("down_s16", [C, D], F16)
        self.down_s = sb("down_s", [P, KT, C], F32)
        self.ident16 = sb("ident16", [P, P], F16)
        self.packed = [sb(f"packed{i}", [P, self.WORDS], I32) for i in range(2)]
        self.magnitude = sb("magnitude", [P, 4, self.WORDS], U32)
        self.sign = sb("sign", [P, 4, self.WORDS], U32)
        self.code = sb("code", [P, 4, self.WORDS], U32)
        self.scaled = sb("scaled", [P, 12, P], F32)
        self.w = [[[sb(f"w{i}{n}{s}", [P, KT, P], F32R) for s in "hl"] for n in range(3)] for i in range(2)]
        self.silu = [sb(f"silu{i}", [P, 512], F32) for i in range(2)]
        self.h = [sb(f"h{i}", [P, 512], F32) for i in range(2)]
        self.h_cols = [sb(f"h_cols{s}", [P, NB * P], F32R) for s in "hl"]
        self.squares = sb("squares", [P, D], F32)
        self.sum_sq = sb("sum_sq", [P, NB], F32)
        self.mean_sq = sb("mean_sq", [P, NB], F32)
        self.inv_rms = sb("inv_rms", [P, NB], F32)
        self.minus_half = minus_half

        self.ps_g = ps("ps_g", [P, 2, 512], F32)
        self.ps_u = ps("ps_u", [P, 2, 512], F32)
        self.ps_y = ps("ps_y", [P, 2, 512], F32)
        self.ps_w = ps("ps_w", [P, 2, KT, P], F32)
        self.ln = LayerNorm(nc, sb, sem, "ln_", x, self.x_cols, self.ps_g[:, :, :].rearrange("p h (k t) -> p h k t", k=KT),
                            ident, minus_half, NB, KT)
        self.scales_in, self.stored = sem("scales_in"), sem("stored")
        self.packed_in = [sem(f"packed_in{i}") for i in range(2)]
        self.ident16_made = sem("ident16_made")
        self.scales_turned = sem("scales_turned")
        self.scales_copied = sem("scales_copied")
        self.bits_cut = sem("bits_cut")
        self.coded = sem("coded")
        self.weights_scaled = sem("weights_scaled")
        self.w_turned = sem("w_turned")
        self.w_hi = sem("w_hi")
        self.w_lo = sem("w_lo")
        self.gu_done = sem("gu_done")
        self.silu_done = sem("silu_done")
        self.h_made = sem("h_made")
        self.h_hi = sem("h_hi")
        self.h_lo = sem("h_lo")
        self.y_done = sem("y_done")
        self.y_added = sem("y_added")
        self.y_cleared = sem("y_cleared")
        self.squared = sem("squared")
        self.mean_done = sem("mean_done")
        self.rms_done = sem("rms_done")
        self.out_made = sem("out_made")

    def load_packed(self, sp, c, p):
        at = slice(c, c + 1) if isinstance(c, int) else bass.ds(c, 1)
        sp.wait_ge(self.coded, done(c - 2))
        for a in range(2):
            src = self.gu_packed.rearrange("(a c p) w -> a c p w", a=2, p=P)[a, at]
            sp.dma_start(self.packed[p][:, a * self.WG:(a + 1) * self.WG], src.rearrange("c p w -> (c p) w"))\
                .then_inc(self.packed_in[p], 16)
        src = self.down_packed.rearrange("(t p) (c w) -> c p t w", p=P, w=self.WD)[at]
        sp.dma_start(self.packed[p][:, 2 * self.WG:].rearrange("p (t w) -> p t w", w=self.WD),
                     src.rearrange("c p t w -> (c p) t w")).then_inc(self.packed_in[p], 16)

    def decode(self, dve, c, p):
        dve.wait_ge(self.packed_in[p], 48 * (c // 2 + 1) if isinstance(c, int) else (c + 2 - p) * 24)
        packed = self.packed[p][:, :].bitcast(U32)
        for j in range(4):
            for into, left, mask in ((self.magnitude, 9 - 4 * j, 0x0E000E00), (self.sign, 12 - 4 * j, 0x80008000)):
                op = ALU.logical_shift_left if left >= 0 else ALU.logical_shift_right
                ins = dve.tensor_scalar(into[:, j, :], packed, abs(left), mask, op, ALU.bitwise_and)
        ins.then_inc(self.bits_cut, 1)
        dve.wait_ge(self.bits_cut, done(c))
        dve.wait_ge(self.weights_scaled, done(12 * c - 1))
        dve.tensor_tensor(self.code[:, :, :], self.magnitude[:, :, :], self.sign[:, :, :], ALU.bitwise_or)\
            .then_inc(self.coded, 1)

    def scale_weights(self, act, c, n):
        at = slice(c, c + 1) if isinstance(c, int) else bass.ds(c, 1)
        a, g = n // 4, n % 4
        words = self.code[:, :, n * self.WD:(n + 1) * self.WD].bitcast(F16).rearrange("p j (w h) -> p w h j", h=2)
        scale = self.gu_s[:, a, at, g] if a < 2 else self.down_s[:, g, at]
        act.wait_ge(self.coded, done(c))
        act.wait_ge(self.w_turned, done(3 * c - 3 + a))
        act.activation(self.scaled[:, n, :].rearrange("p (w h j) -> p w h j", h=2, j=4), words, ACT.Copy,
                       scale=scale).then_inc(self.weights_scaled, 1)

    def turn_weights(self, pe, c, p, a):
        bank = (p + a) % 2
        pe.wait_ge(self.weights_scaled, done(12 * c + 4 * a + 3))
        pe.wait_ge(self.w_lo, done(3 * c + a - 2))
        for t in range(4):
            mm = pe.transpose(self.ps_w[:, bank, t, :], self.scaled[:, 4 * a + t, :], self.ident[:, :])
        mm.then_inc(self.w_turned, 1)

    def split_high(self, act, c, p, a):
        act.wait_ge(self.w_turned, done(3 * c + a))
        act.wait_ge(self.y_done, done(16 * (c - 2) + 15))
        act.activation(self.w[p][a][0][:, :, :], self.ps_w[:, (p + a) % 2, :, :], ACT.Copy).then_inc(self.w_hi, 1)

    def split_low(self, dve, c, p, a):
        dve.wait_ge(self.w_hi, done(3 * c + a))
        dve.tensor_tensor(self.w[p][a][1][:, :, :], self.ps_w[:, (p + a) % 2, :, :],
                          self.w[p][a][0][:, :, :].bitcast(F32), ALU.subtract).then_inc(self.w_lo, 1)

    def gate_up(self, pe, c, p, tb):
        n, tok = 4 * c + tb, slice(tb * 512, (tb + 1) * 512)
        pe.wait_ge(self.w_lo, done(3 * c + 1))
        pe.wait_ge(self.h_made, done(n - 2))
        for a, bank in ((0, self.ps_g), (1, self.ps_u)):
            for k in range(self.KT):
                mm = matmul_split(pe, bank[:, tb % 2, :], [w[:, k, :] for w in self.w[p][a]],
                                  [x[:, k, tok] for x in self.x_cols], k == 0, k == self.KT - 1)
        mm.then_inc(self.gu_done, 1)

    def down(self, pe, c, p, tb):
        pe.wait_ge(self.h_lo, done(4 * c + tb))
        pe.wait_ge(self.w_lo, done(3 * c + 2))
        w = [v[:, :, :].rearrange("p t h -> p (t h)") for v in self.w[p][2]]
        for i in range(self.BLK):
            t = tb * self.BLK + i
            pe.wait_ge(self.y_added, done(16 * c + t - 2))
            matmul_split(pe, self.ps_y[:, t % 2, :], [h[:, t * P:(t + 1) * P] for h in self.h_cols], w, True, True)\
                .then_inc(self.y_done, 1)

    def tensor_chunk(self, pe, c, p, first, last):
        for tb in range(4):
            self.gate_up(pe, c, p, tb)
            if not last:
                for a in self.TILES_AT[tb]:
                    self.turn_weights(pe, c + 1, 1 - p, a)
            if tb > 0:
                self.down(pe, c, p, tb - 1)
            elif not first:
                self.down(pe, c - 1, 1 - p, 3)

    def gate_high(self, act, c, tb):
        n = 4 * c + tb
        act.wait_ge(self.gu_done, done(n))
        act.wait_ge(self.h_made, done(n - 2))
        act.activation(self.silu[tb % 2][:, :], self.ps_g[:, tb % 2, :], ACT.Silu).then_inc(self.silu_done, 1)
        act.wait_ge(self.h_made, done(n))
        act.wait_ge(self.y_done, done(16 * (c - 1) + 4 * tb + 3))
        act.activation(self.h_cols[0][:, tb * 512:(tb + 1) * 512], self.h[tb % 2][:, :], ACT.Copy).then_inc(self.h_hi, 1)

    def scalar_chunk(self, act, c, p, last):
        for tb in range(4):
            self.gate_high(act, c, tb)
            if not last and tb == 1:
                for n in range(12):
                    self.scale_weights(act, c + 1, n)
            if not last:
                for a in self.TILES_AT[tb]:
                    self.split_high(act, c + 1, 1 - p, a)

    def pool_chunk(self, pool, c):
        for tb in range(4):
            pool.wait_ge(self.h_hi, done(4 * c + tb))
            pool.tensor_tensor(self.h_cols[1][:, tb * 512:(tb + 1) * 512], self.h[tb % 2][:, :],
                               self.h_cols[0][:, tb * 512:(tb + 1) * 512].bitcast(F32), ALU.subtract).then_inc(self.h_lo, 1)

    def multiply(self, dve, c, tb):
        n = 4 * c + tb
        dve.wait_ge(self.silu_done, done(n))
        dve.wait_ge(self.h_lo, done(n - 2))
        dve.tensor_tensor(self.h[tb % 2][:, :], self.silu[tb % 2][:, :], self.ps_u[:, tb % 2, :], ALU.mult)\
            .then_inc(self.h_made, 1)

    def add_down(self, dve, c, tb, tiles):
        for i in tiles:
            t = tb * self.BLK + i
            dve.wait_ge(self.y_done, done(16 * c + t))
            dve.tensor_tensor(self.y[:, t, :], self.y[:, t, :], self.ps_y[:, t % 2, :], ALU.add).then_inc(self.y_added, 1)

    def vector_chunk(self, dve, c, p, first, last):
        for tb in range(4):
            before = (c, tb - 1) if tb > 0 else (c - 1, 3)
            if tb > 0 or not first:
                self.add_down(dve, *before, range(2))
            self.multiply(dve, c, tb)
            if tb > 0 or not first:
                self.add_down(dve, *before, range(2, 4))
            if not last:
                for a in self.TILES_AT[tb]:
                    self.split_low(dve, c + 1, 1 - p, a)
                if tb == 0:
                    self.decode(dve, c + 1, 1 - p)

    def run(self, block):
        NB, C, KT, D = self.NB, self.C, self.KT, self.D
        PAIRS = (C - 3) // 2
        rest = range(1 + 2 * PAIRS, C)

        @block.sync
        def _(sp):
            sp.dma_start(self.gu_s16[:, :], self.gu_scales).then_inc(self.scales_in, 16)
            sp.dma_start(self.down_s16[:, :], self.down_scales).then_inc(self.scales_in, 16)
            self.load_packed(sp, 0, 0)
            with sp.Fori(0, (C - 1) // 2) as i:
                for q in range(2):
                    self.load_packed(sp, i * 2 + 1 + q, (1 + q) % 2)
            for b in range(0, NB, 4):
                sp.wait_ge(self.out_made, b + 4)
                sp.dma_start(self.out[b:b + 4].rearrange("b t d -> t b d"), self.x[:, b:b + 4, :]).then_inc(self.stored, 16)
            sp.wait_ge(self.stored, 16 * (NB // 4))

        @block.gpsimd
        def _(pool):
            start(pool, self.h_lo)
            pool.memset(self.ident16[:, :], 0.0).then_inc(self.ident16_made, 1)
            pool.wait_ge(self.ident16_made, 1)
            pool.affine_select(out=self.ident16[:, :], in_=self.ident16[:, :], compare_op=ALU.not_equal, fill=1.0, base=0,
                               pattern=[[-1, P]], channel_multiplier=1).then_inc(self.ident16_made, 1)
            pool.memset(self.y[:, :, :], 0.0).then_inc(self.y_cleared, 1)
            pool.wait_ge(self.ident16_made, 2)
            for b in range(0, NB, 2):
                self.ln.pool(pool, b)
            self.pool_chunk(pool, 0)
            with pool.Fori(0, PAIRS) as i:
                for q in range(2):
                    self.pool_chunk(pool, i * 2 + 1 + q)
            for c in rest:
                self.pool_chunk(pool, c)
            for b in range(0, NB, 4):
                pool.wait_ge(self.mean_done, b // 4 + 1)
                pool.tensor_tensor(self.inv_rms[:, b:b + 4], self.mean_sq[:, b:b + 4],
                                   self.minus_half[:, :].to_broadcast([P, 4]), ALU.pow).then_inc(self.rms_done, 1)

        @block.scalar
        def _(act):
            start(act, self.weights_scaled, self.w_hi, self.silu_done, self.h_hi)
            act.wait_ge(self.scales_turned, 1)
            gu_turned = self.ps_u[:, 0, :].bitcast(F16)
            act.activation(self.gu_s[:, :, :, :].rearrange("p a c g -> p (a c g)"), gu_turned[:, 0:2 * C * KT], ACT.Copy,
                           scale=2.0 ** 14).then_inc(self.scales_copied, 1)
            down_turned = self.ps_u[:, 1, :].bitcast(F16)
            act.activation(self.down_s[:, :, :], down_turned[:, 0:KT * 16].rearrange("p (t c) -> p t c", c=16)[:, :, 0:C],
                           ACT.Copy, scale=2.0 ** 14).then_inc(self.scales_copied, 1)
            act.wait_ge(self.scales_copied, 2)
            for n in range(12):
                self.scale_weights(act, 0, n)
            for a in range(3):
                self.split_high(act, 0, 0, a)
            for b in range(0, NB, 2):
                self.ln.scalar(act, b)
            self.scalar_chunk(act, 0, 0, False)
            with act.Fori(0, PAIRS) as i:
                for q in range(2):
                    self.scalar_chunk(act, i * 2 + 1 + q, (1 + q) % 2, False)
            for c in rest:
                self.scalar_chunk(act, c, c % 2, c == C - 1)
            for b in range(NB):
                act.wait_ge(self.y_added, done(16 * (C - 1) + b))
                if b > 0:
                    act.wait_ge(self.squared, b)
                act.activation(self.squares[:, :], self.y[:, b, :], ACT.Square, accum_out=self.sum_sq[:, b:b + 1])\
                    .then_inc(self.squared, 1)

        @block.tensor
        def _(pe):
            start(pe, self.w_turned, self.gu_done, self.y_done)
            pe.wait_ge(self.scales_in, 32)
            pe.wait_ge(self.ident16_made, 2)
            for t in range(2 * C):
                pe.transpose(self.ps_u[:, 0, :].bitcast(F16)[:, t * KT:(t + 1) * KT], self.gu_s16[:, t * P:(t + 1) * P],
                             self.ident16[0:KT, 0:KT])
            for t in range(KT):
                mm = pe.transpose(self.ps_u[:, 1, :].bitcast(F16)[:, t * 16:t * 16 + C], self.down_s16[:, t * P:(t + 1) * P],
                                  self.ident16[0:C, 0:C])
            mm.then_inc(self.scales_turned, 1)
            for a in range(3):
                self.turn_weights(pe, 0, 0, a)
            for b in range(0, NB, 2):
                self.ln.tensor(pe, b)
            pe.wait_ge(self.ln.lo_done, NB)
            pe.wait_ge(self.scales_copied, 2)
            self.tensor_chunk(pe, 0, 0, True, False)
            with pe.Fori(0, PAIRS) as i:
                for q in range(2):
                    self.tensor_chunk(pe, i * 2 + 1 + q, (1 + q) % 2, False, False)
            for c in rest:
                self.tensor_chunk(pe, c, c % 2, False, c == C - 1)
            self.down(pe, C - 1, (C - 1) % 2, 3)

        @block.vector
        def _(dve):
            start(dve, self.bits_cut, self.coded, self.w_lo, self.h_made, self.y_added)
            self.decode(dve, 0, 0)
            for a in range(3):
                self.split_low(dve, 0, 0, a)
            for b in range(0, NB, 2):
                self.ln.vector(dve, b)
            dve.wait_ge(self.y_cleared, 1)
            self.vector_chunk(dve, 0, 0, True, False)
            with dve.Fori(0, PAIRS) as i:
                for q in range(2):
                    self.vector_chunk(dve, i * 2 + 1 + q, (1 + q) % 2, False, False)
            for c in rest:
                self.vector_chunk(dve, c, c % 2, False, c == C - 1)
            self.add_down(dve, C - 1, 3, range(4))
            for b in range(0, NB, 4):
                dve.wait_ge(self.squared, b + 4)
                dve.tensor_scalar(self.mean_sq[:, b:b + 4], self.sum_sq[:, b:b + 4], 1.0 / D, EPS_RMS, ALU.mult, ALU.add)\
                    .then_inc(self.mean_done, 1)
                dve.wait_ge(self.rms_done, b // 4 + 1)
                for t in range(b, b + 4):
                    dve.scalar_tensor_tensor(self.x[:, t, :], self.y[:, t, :], self.inv_rms[:, t:t + 1], self.x[:, t, :],
                                             ALU.mult, ALU.add).then_inc(self.out_made, 1)


def decoder_layer(nc, x_in, ctx_in, pos_in, Wq, Wk, Wv, Wo, bo, xWq, xWkv, xWout, xbout,
                  gu_packed, gu_scales, down_packed, down_scales, out):
    NB, T, D = x_in.shape
    with ExitStack() as ctx:
        sb = lambda n, s, d: ctx.enter_context(nc.sbuf_tensor(n, s, d))
        x = sb("x", [P, NB, D], F32)
        ident = sb("ident", [P, P], F32)
        minus_half = sb("minus_half", [P, 1], F32)
        ones = sb("ones", [P, 1], F32)
        const_set = ctx.enter_context(nc.semaphore("const_set"))
        with nc.Block() as block:
            @block.gpsimd
            def _(pool):
                pool.memset(minus_half[:, :], -0.5).then_inc(const_set, 1)
                pool.memset(ident[:, :], 0.0).then_inc(const_set, 1)
                pool.memset(ones[:, :], 1.0).then_inc(const_set, 1)
                pool.wait_ge(const_set, 3)
                pool.affine_select(out=ident[:, :], in_=ident[:, :], compare_op=ALU.not_equal, fill=1.0,
                                   base=0, pattern=[[-1, P]], channel_multiplier=1).then_inc(const_set, 1)
                pool.wait_ge(const_set, 4)
        linear_attention(nc, x, ident, ones, minus_half, x_in, Wq, Wk, Wv, Wo, bo)
        with ExitStack() as scope:
            attention = CrossAttention(nc, scope, x, ident, ones, minus_half, ctx_in, pos_in, xWq, xWkv, xWout, xbout)
            with nc.Block() as block:
                attention.run(block)
        with ExitStack() as scope:
            feed_forward = FeedForward(nc, scope, x, ident, ones, minus_half, gu_packed, gu_scales, down_packed,
                                       down_scales, out)
            with nc.Block() as block:
                feed_forward.run(block)


_INS = ['x', 'ctx_1024', 'fside_BxSx2_0', 'L0_attn_Wq', 'L0_attn_Wk', 'L0_attn_Wv', 'L0_attn_Wo', 'L0_attn_bo',
        'L0_xattn_Wq', 'L0_xattn_Wkv', 'L0_xattn_Wout', 'L0_xattn_bout', 'L0_ffn_gate_up_packed',
        'L0_ffn_gate_up_scales', 'L0_ffn_down_packed', 'L0_ffn_down_scales']


def kernel(**inputs):
    import numpy as _np
    import concourse.bacc as _bacc
    from concourse import mybir as _mybir
    from concourse.bass_utils import run_bass_kernel_spmd as _run

    nc = _bacc.Bacc("TRN2", target_bir_lowering=False, num_devices=1)
    arrays, args = {}, []
    for name in _INS:
        a = _np.ascontiguousarray(inputs[name])
        arrays[f"in_{name}"] = a
        args.append(nc.dram_tensor(f"in_{name}", a.shape, _mybir.dt.from_np(a.dtype), kind="ExternalInput").ap())
    args.append(nc.dram_tensor("out_x", (16, 128, 512), _mybir.dt.float32, kind="ExternalOutput").ap())
    decoder_layer(nc, *args)
    r = _run(nc, [arrays], core_ids=[0])
    return r.results[0]["out_x"]
```

```python
import math
from contextlib import ExitStack

import concourse.bass as bass
from concourse import mybir

F32 = mybir.dt.float32
F32R = mybir.dt.float32r
F16 = mybir.dt.float16
I32 = mybir.dt.int32
U32 = mybir.dt.uint32
BF16 = mybir.dt.bfloat16
ALU = mybir.AluOpType
ACT = mybir.ActivationFunctionType
AX_X = mybir.AxisListType.X

P = 128
EPS_LN = 1e-5
EPS_RMS = 1e-6
START = 32


def done(n):
    return START + 1 + n


def start(engine, *semaphores):
    for s in semaphores:
        engine.sem_inc(s, START)


def matmul_split(pe, out, stationary, moving, first, last):
    pe.matmul(out, stationary[0], moving[0], start=first, stop=False)
    pe.matmul(out, stationary[0], moving[1], start=False, stop=False)
    return pe.matmul(out, stationary[1], moving[0], start=False, stop=last)


class LayerNorm:

    def __init__(self, nc, sb, sem, tag, x, cols, psum, ident, minus_half, batches, k_tiles):
        self.x, self.cols, self.psum, self.ident, self.minus_half = x, cols, psum, ident, minus_half
        self.nc, self.nb, self.kt = nc, batches, k_tiles
        self.stats = sb(tag + "stats", [P, 2, 6], F32)
        self.mean_var = sb(tag + "mean_var", [P, 2, 2], F32)
        self.var_eps = sb(tag + "var_eps", [P, 2, 1], F32)
        self.rstd = sb(tag + "rstd", [P, 2, 1], F32)
        self.normed = sb(tag + "normed", [P, 2, k_tiles * P], F32)
        self.stats_done = sem(tag + "stats_done")
        self.mean_done = sem(tag + "mean_done")
        self.var_done = sem(tag + "var_done")
        self.rstd_done = sem(tag + "rstd_done")
        self.norm_done = sem(tag + "norm_done")
        self.turned = sem(tag + "turned")
        self.hi_done = sem(tag + "hi_done")
        self.lo_done = sem(tag + "lo_done")

    def vector(self, dve, b):
        for h in range(2):
            dve.bn_stats(self.stats[:, h, :], self.x[:, b + h, :]).then_inc(self.stats_done, 1)
        for h in range(2):
            dve.wait_ge(self.stats_done, b + h + 1)
            dve.bn_aggr(self.mean_var[:, h, :], self.stats[:, h, :]).then_inc(self.mean_done, 1)
        for h in range(2):
            dve.wait_ge(self.mean_done, b + h + 1)
            dve.tensor_scalar(self.var_eps[:, h, :], self.mean_var[:, h, 1:2], EPS_LN, None,
                              ALU.add).then_inc(self.var_done, 1)
        for h in range(2):
            dve.wait_ge(self.rstd_done, b + h + 1)
            dve.wait_ge(self.turned, b)
            dve.tensor_scalar(self.normed[:, h, :], self.x[:, b + h, :], self.mean_var[:, h, 0:1],
                              self.rstd[:, h, :], ALU.subtract, ALU.mult).then_inc(self.norm_done, 1)
        for h in range(2):
            dve.wait_ge(self.hi_done, b + h + 1)
            at = slice(None), slice(None), slice((b + h) * P, (b + h + 1) * P)
            dve.tensor_tensor(self.cols[1][at], self.psum[:, h, :, :],
                              self.cols[0].bitcast(F32)[at], ALU.subtract).then_inc(self.lo_done, 1)

    def pool(self, pool, b):
        for h in range(2):
            pool.wait_ge(self.var_done, b + h + 1)
            pool.tensor_tensor(self.rstd[:, h, :], self.var_eps[:, h, :], self.minus_half[:, :],
                               ALU.pow).then_inc(self.rstd_done, 1)

    def tensor(self, pe, b):
        for h in range(2):
            pe.wait_ge(self.norm_done, b + h + 1)
            pe.wait_ge(self.lo_done, b)
            for k in range(self.kt):
                mm = pe.transpose(self.psum[:, h, k, :], self.normed[:, h, k * P:(k + 1) * P],
                                  self.ident[:, :])
            mm.then_inc(self.turned, 1)

    def scalar(self, act, b):
        for h in range(2):
            act.wait_ge(self.turned, b + h + 1)
            act.activation(self.cols[0][:, :, (b + h) * P:(b + h + 1) * P], self.psum[:, h, :, :],
                           ACT.Copy).then_inc(self.hi_done, 1)


def linear_attention(nc, x, ident, ones, minus_half, x_dram, Wq, Wk, Wv, Wo, bo):
    D, INNER = Wq.shape
    KT = D // P
    NB = x.shape[1]
    HD = 64
    GW = 256
    GROUPS = INNER // GW
    HG, PAIRS = GW // HD, GW // P
    AUG = HD + 1
    with ExitStack() as ctx:
        sb = lambda n, s, d: ctx.enter_context(nc.sbuf_tensor("a_" + n, s, d))
        ps = lambda n, s, d: ctx.enter_context(nc.psum_tensor("a_" + n, s, d))
        sem = lambda n: ctx.enter_context(nc.semaphore("a_" + n))

        h_cols = [sb(f"h_cols{s}", [P, KT, NB * P], F32R) for s in "hl"]
        wq_raw = sb("wq_raw", [P, KT, GW], F32)
        wkv_raw = sb("wkv_raw", [P, KT, 2, GW], F32)
        wo_raw = sb("wo_raw", [P, PAIRS, D], F32)
        wq = [[sb(f"wq{g}{s}", [P, KT, GW], F32R) for s in "hl"] for g in range(2)]
        wkv = [[sb(f"wkv{g}{s}", [P, KT, 2 * GW], F32R) for s in "hl"] for g in range(2)]
        wo = [[sb(f"wo{g}{s}", [P, PAIRS, D], F32R) for s in "hl"] for g in range(2)]
        q_cols = [sb(f"q_cols{i}", [P, PAIRS, 4 * P], F32) for i in range(2)]
        k_rows = [sb(f"k_rows{i}", [P, GW], F32) for i in range(2)]
        v_rows = [sb(f"v_rows{i}", [P, HG, AUG], F32) for i in range(2)]
        kv_diag = [sb(f"kv_diag{i}", [P, PAIRS, 2 * AUG], F32) for i in range(2)]
        pair_mask = sb("pair_mask", [P, PAIRS, 2, AUG], F32)
        denom = [sb(f"denom{i}", [P, HG, 1], F32) for i in range(2)]
        inv = [sb(f"inv{i}", [P, HG, 1], F32) for i in range(2)]
        o_rows = [sb(f"o_rows{i}", [P, HG, HD], F32) for i in range(2)]
        o_cols = [[sb(f"o_cols{i}{s}", [P, PAIRS, P], F32R) for s in "hl"] for i in range(2)]
        bias = sb("bias", [P, D], F32)

        q_ps = ps("q_ps", [P, 2, 512], F32)
        kv_ps = ps("kv_ps", [P, 2, 512], F32)
        kvm_ps = ps("kvm_ps", [P, 512], F32)
        num_ps = ps("num_ps", [P, 512], F32)
        turn_ps = ps("turn_ps", [P, 512], F32)
        y_ps = ps("y_ps", [P, 512], F32)
        ln_ps = q_ps[:, :, :].rearrange("p h (k t) -> p h k t", k=KT)
        num_heads = num_ps[:, 0:HG * AUG].rearrange("p (h e) -> p h e", h=HG)

        ln = LayerNorm(nc, sb, sem, "ln_", x, h_cols, ln_ps, ident, minus_half, NB, KT)

        x_in = [sem(f"x_in{q}") for q in range(4)]
        bias_in, raw_in = sem("bias_in"), sem("raw_in")
        ones_set, mask_set, mask_cut = sem("ones_set"), sem("mask_set"), sem("mask_cut")
        hi_split, weights_ready = sem("hi_split"), sem("weights_ready")
        bias_added = sem("bias_added")
        q_done, q_copied = sem("q_done"), sem("q_copied")
        kv_done, kv_copied = sem("kv_done"), sem("kv_copied")
        kvm_done, kvm_masked = sem("kvm_done"), sem("kvm_masked")
        num_done = sem("num_done")
        den_clipped, den_inverted, o_scaled = sem("den_clipped"), sem("den_inverted"), sem("o_scaled")
        o_turned, o_hi, o_lo = sem("o_turned"), sem("o_hi"), sem("o_lo")
        y_done, y_added = sem("y_done"), sem("y_added")

        STEPS = 2 * NB
        block = ctx.enter_context(nc.Block())

        @block.sync
        def _(sp):
            for q in range(4):
                sp.dma_start(x[:, 4 * q:4 * q + 4, :],
                             x_dram[4 * q:4 * q + 4].rearrange("b t d -> t b d")).then_inc(x_in[q], 16)
            sp.dma_start(bias[:, :], bo.rearrange("(a d) -> a d", a=1).to_broadcast([P, D])).then_inc(bias_in, 16)
            with sp.Fori(0, GROUPS) as g:
                sp.wait_ge(weights_ready, done(g * 3 - 1))
                for raw, W in ((wq_raw[:, :, :], Wq), (wkv_raw[:, :, 0, :], Wk), (wkv_raw[:, :, 1, :], Wv)):
                    sp.dma_start(raw, W.rearrange("(k p) n -> p k n", p=P)[:, :, bass.ds(g * GW, GW)])\
                        .then_inc(raw_in, 16)
                sp.dma_start(wo_raw[:, :, :], Wo.rearrange("(g j p) n -> g p j n", j=PAIRS, p=P)
                             [bass.ds(g, 1)].rearrange("g p j n -> (g p) j n")).then_inc(raw_in, 16)

        @block.gpsimd
        def _(pool):
            start(pool, hi_split, weights_ready)
            for i in range(2):
                pool.memset(v_rows[i][:, :, HD:AUG], 1.0).then_inc(ones_set, 1)
            pool.memset(pair_mask[:, :, :, :], 0.0).then_inc(mask_set, 1)
            pool.wait_ge(mask_set, 1)
            for e in range(2):
                pool.memset(pair_mask[HD * e:HD * (e + 1), :, e, :], 1.0).then_inc(mask_cut, 1)
            pool.wait_ge(mask_cut, 2)
            for b in range(0, NB, 2):
                ln.pool(pool, b)
            with pool.Fori(0, GROUPS // 2) as it:
                for gg in range(2):
                    g = it * 2 + gg
                    pool.wait_ge(raw_in, (g + 1) * 64)
                    pool.wait_ge(y_done, done((g - 2) * NB + NB - 1))
                    parts = ((wq_raw[:, :, :], wq[gg]),
                             (wkv_raw[:, :, :, :].rearrange("p k a n -> p k (a n)"), wkv[gg]),
                             (wo_raw[:, :, :], wo[gg]))
                    for raw, w in parts:
                        pool.tensor_tensor(w[0][:, :, :], raw, ones[:, :].unsqueeze(2).to_broadcast(list(raw.shape)), ALU.mult)\
                            .then_inc(hi_split, 1)
                    for n, (raw, w) in enumerate(parts):
                        pool.wait_ge(hi_split, done(g * 3 + n))
                        pool.tensor_tensor(w[1][:, :, :], raw, w[0][:, :, :].bitcast(F32), ALU.subtract)\
                            .then_inc(weights_ready, 1)

        @block.scalar
        def _(act):
            start(act, q_copied, kv_copied, o_hi)
            for b in range(0, NB, 2):
                ln.scalar(act, b)
            act.wait_ge(ones_set, 2)
            with act.Fori(0, GROUPS // 2) as it:
                n0 = it * STEPS
                for s in range(STEPS + 3):
                    if s % 4 == 0 and s < STEPS:
                        blk = it * (STEPS // 4) + s // 4
                        act.wait_ge(num_done, done(blk * 4 - 5))
                        for f in range(PAIRS):
                            act.wait_ge(q_done, done(blk * 2 + f))
                            act.activation(q_cols[s // 4 % 2][:, f, :], q_ps[:, f, :], ACT.Relu)\
                                .then_inc(q_copied, 1)
                    if s < STEPS:
                        p = s % 2
                        act.wait_ge(kv_done, done(n0 + s))
                        act.wait_ge(kvm_done, done(n0 + s - 2))
                        act.activation(k_rows[p][:, :], kv_ps[:, p, 0:GW], ACT.Relu)
                        act.activation(v_rows[p][:, :, 0:HD],
                                       kv_ps[:, p, GW:2 * GW].rearrange("p (h e) -> p h e", h=HG),
                                       ACT.Copy).then_inc(kv_copied, 1)
                    if s >= 3:
                        p = (s - 3) % 2
                        act.wait_ge(o_turned, done(n0 + s - 3))
                        act.wait_ge(y_done, done(n0 + s - 5))
                        act.activation(o_cols[p][0][:, :, :],
                                       turn_ps[:, 0:GW].rearrange("p (j t) -> p j t", j=PAIRS),
                                       ACT.Copy).then_inc(o_hi, 1)

        @block.tensor
        def _(pe):
            start(pe, q_done, kv_done, kvm_done, num_done, o_turned, y_done)
            for b in range(0, NB, 2):
                ln.tensor(pe, b)
            pe.wait_ge(ln.lo_done, NB)
            with pe.Fori(0, GROUPS // 2) as it:
                n0 = it * STEPS
                for s in range(STEPS + 4):
                    if s % NB == 0 and s < STEPS:
                        pe.wait_ge(weights_ready, done((it * 2 + s // NB) * 3 + 2))
                    if s % 4 == 0 and s < STEPS:
                        w, blk, tok = wq[s // NB], it * (STEPS // 4) + s // 4, s % NB * P
                        pe.wait_ge(q_copied, done(blk * 2 - 1))
                        for f in range(PAIRS):
                            for k in range(KT):
                                mm = matmul_split(pe, q_ps[:, f, :], [w[i][:, k, f * P:(f + 1) * P] for i in range(2)],
                                                  [h_cols[i][:, k, tok:tok + 4 * P] for i in range(2)], k == 0, k == KT - 1)
                            mm.then_inc(q_done, 1)
                    if s < STEPS:
                        w, tok = wkv[s // NB], s % NB * P
                        pe.wait_ge(kv_copied, done(n0 + s - 2))
                        for k in range(KT):
                            mm = matmul_split(pe, kv_ps[:, s % 2, :], [h_cols[i][:, k, tok:tok + P] for i in range(2)],
                                              [w[i][:, k, :] for i in range(2)], k == 0, k == KT - 1)
                        mm.then_inc(kv_done, 1)
                    if 1 <= s < STEPS + 1:
                        n, p = n0 + s - 1, (s - 1) % 2
                        pe.wait_ge(kv_copied, done(n))
                        pe.wait_ge(kvm_masked, done(n - 1))
                        for j in range(PAIRS):
                            mm = pe.matmul(kvm_ps[:, j * 2 * AUG:(j + 1) * 2 * AUG], k_rows[p][:, j * P:(j + 1) * P],
                                           v_rows[p][:, 2 * j:2 * j + 2, :].rearrange("p h e -> p (h e)"),
                                           start=True, stop=True)
                        mm.then_inc(kvm_done, 1)
                    if 2 <= s < STEPS + 2:
                        n, p, sl = n0 + s - 2, (s - 2) % 2, s - 2
                        pe.wait_ge(kvm_masked, done(n))
                        pe.wait_ge(q_copied, done((it * (STEPS // 4) + sl // 4) * 2 + 1))
                        pe.wait_ge(o_scaled, done(n - 1))
                        for j in range(PAIRS):
                            mm = pe.matmul(num_ps[:, j * 2 * AUG:(j + 1) * 2 * AUG],
                                           q_cols[sl // 4 % 2][:, j, sl % 4 * P:(sl % 4 + 1) * P],
                                           kv_diag[p][:, j, :], start=True, stop=True)
                        mm.then_inc(num_done, 1)
                    if 3 <= s < STEPS + 3:
                        n, p = n0 + s - 3, (s - 3) % 2
                        pe.wait_ge(o_scaled, done(n))
                        pe.wait_ge(o_lo, done(n - 1))
                        for j in range(PAIRS):
                            mm = pe.transpose(turn_ps[:, j * P:(j + 1) * P],
                                              o_rows[p][:, 2 * j:2 * j + 2, :].rearrange("p h e -> p (h e)"), ident[:, :])
                        mm.then_inc(o_turned, 1)
                    if s >= 4:
                        n, p, w = n0 + s - 4, (s - 4) % 2, wo[(s - 4) // NB]
                        pe.wait_ge(o_lo, done(n))
                        pe.wait_ge(y_added, done(n - 1))
                        for j in range(PAIRS):
                            mm = matmul_split(pe, y_ps[:, :], [o_cols[p][i][:, j, :] for i in range(2)],
                                              [w[i][:, j, :] for i in range(2)], j == 0, j == PAIRS - 1)
                        mm.then_inc(y_done, 1)

        @block.vector
        def _(dve):
            start(dve, kvm_masked, den_clipped, den_inverted, o_scaled, o_lo, y_added)
            for b in range(0, NB, 2):
                if b % 4 == 0:
                    dve.wait_ge(x_in[b // 4], 16)
                ln.vector(dve, b)
            dve.wait_ge(bias_in, 16)
            dve.wait_ge(mask_cut, 2)
            with dve.Fori(0, NB) as b:
                dve.tensor_tensor(x[:, b, :], x[:, b, :], bias[:, :], ALU.add).then_inc(bias_added, 1)
            dve.wait_ge(bias_added, NB)
            with dve.Fori(0, GROUPS // 2) as it:
                n0 = it * STEPS
                for s in range(1, STEPS + 5):
                    if s < STEPS + 1:
                        n, p = n0 + s - 1, (s - 1) % 2
                        dve.wait_ge(kvm_done, done(n))
                        dve.wait_ge(num_done, done(n - 2))
                        dve.tensor_tensor(kv_diag[p][:, :, :], kvm_ps[:, 0:PAIRS * 2 * AUG].rearrange("p (j e) -> p j e", j=PAIRS),
                                          pair_mask[:, :, :, :].rearrange("p j h e -> p j (h e)"), ALU.mult)\
                            .then_inc(kvm_masked, 1)
                    if 2 <= s < STEPS + 2:
                        n, p = n0 + s - 2, (s - 2) % 2
                        dve.wait_ge(num_done, done(n))
                        dve.tensor_scalar(denom[p][:, :, :], num_heads[:, :, HD:AUG], 1e-6, None,
                                          ALU.max).then_inc(den_clipped, 1)
                        dve.wait_ge(den_clipped, done(n))
                        dve.reciprocal(inv[p][:, :, :], denom[p][:, :, :]).then_inc(den_inverted, 1)
                        dve.wait_ge(den_inverted, done(n))
                        dve.wait_ge(o_turned, done(n - 2))
                        dve.tensor_tensor(o_rows[p][:, :, :], num_heads[:, :, 0:HD],
                                          inv[p][:, :, :].to_broadcast([P, HG, HD]), ALU.mult).then_inc(o_scaled, 1)
                    if 3 <= s < STEPS + 3:
                        n, p = n0 + s - 3, (s - 3) % 2
                        dve.wait_ge(o_hi, done(n))
                        dve.tensor_tensor(o_cols[p][1][:, :, :], turn_ps[:, 0:GW].rearrange("p (j t) -> p j t", j=PAIRS),
                                          o_cols[p][0][:, :, :].bitcast(F32), ALU.subtract).then_inc(o_lo, 1)
                    if s >= 4 and s - 4 < STEPS:
                        n, b = n0 + s - 4, (s - 4) % NB
                        dve.wait_ge(y_done, done(n))
                        dve.tensor_tensor(x[:, b, :], x[:, b, :], y_ps[:, :], ALU.add).then_inc(y_added, 1)
            dve.wait_ge(y_added, done(NB * GROUPS - 1))


PROJECT, TURN, ATTEND, FINISH, NEXT = range(5)


class CrossAttention:

    def __init__(self, nc, ctx, x, ident, ones, minus_half, ctx_dram, pos, Wq, Wkv, Wout, bout):
        sb = lambda n, s, d: ctx.enter_context(nc.sbuf_tensor("b_" + n, s, d))
        ps = lambda n, s, d: ctx.enter_context(nc.psum_tensor("b_" + n, s, d))
        sem = lambda n: ctx.enter_context(nc.semaphore("b_" + n))
        self.nc, self.x, self.ident, self.ones, self.minus_half = nc, x, ident, ones, minus_half
        self.ctx_dram, self.pos_dram, self.Wq, self.Wkv, self.Wout, self.bout = ctx_dram, pos, Wq, Wkv, Wout, bout
        D = self.D = Wq.shape[0]
        self.KT, self.CT = D // P, Wkv.shape[0] // P
        self.NB = x.shape[1]
        self.H, self.HD = 32, 16
        self.CONSTS = 12
        self.SLOT = 64
        KT, CT, NB, H, HD, SLOT = self.KT, self.CT, self.NB, self.H, self.HD, self.SLOT

        self.wq = [sb(f"wq{s}", [P, KT, D], F32R) for s in "hl"]
        self.wkv = [sb(f"wkv{s}", [P, CT, 2 * D], F32R) for s in "hl"]
        self.wo = [sb(f"wo{s}", [P, KT, D], F32R) for s in "hl"]
        self.bias = sb("bias", [P, D], F32)
        self.pos = sb("pos", [P, NB, 2], F32)
        self.half_pi = sb("half_pi", [P, 1], F32)
        self.angle = sb("angle", [P, NB, 2, 4], F32)
        self.turns = sb("turns", [P, NB, 2, 4], F32)
        self.tables = sb("tables", [P, NB, 2, 2, 4, 2], F32)
        self.cos, self.sin = self.tables[:, :, 0, :, :, :], self.tables[:, :, 1, :, :, :]
        self.tables_now = sb("tables_now", [P, 2, HD], F32)
        self.stats = sb("stats", [P, NB, 6], F32)
        self.mean_var = sb("mean_var", [P, NB, 2], F32)
        self.var_eps = sb("var_eps", [P, NB], F32)
        self.rstd = sb("rstd", [P, NB], F32)
        self.normed = sb("normed", [P, D], F32)
        self.x_cols = [sb(f"x_cols{s}", [P, KT, P], F32R) for s in "hl"]
        self.ctx_rows = [sb(f"ctx_rows{i}", [P, CT * P], F32) for i in range(2)]
        self.ctx_cols = [sb(f"ctx_cols{s}", [P, CT, P], F32R) for s in "hl"]
        work = sb("work", [P, 12, D], F32)
        self.raw = [work[:, 0:4, :], work[:, 4:8, :].rearrange("p (k a) n -> p k (a n)", k=CT), work[:, 8:12, :]]
        self.rows = {"q": work[:, 0, :], "k": work[:, 1, :]}
        self.by_cos, self.by_sin = work[:, 2, :], work[:, 3, :]
        self.rotated = {"q": work[:, 4, :], "k": work[:, 5, :]}
        self.probs = [work[:, 6 + 2 * i:8 + 2 * i, :].rearrange("p a (h t) -> p (a h) t", t=P) for i in range(2)]
        self.o_cols = work[:, 10:12, :].rearrange("p a (g t) -> p (a g) t", t=P)
        self.slots = {w: sb(f"{w}_slots", [P, H, SLOT], F32R) for w in "qk"}
        self.q_cols = [sb(f"q_cols{i}", [P, H // 2, P], F32R) for i in range(2)]
        self.k_cols = [sb(f"k_cols{i}", [P, H // 2, 2, P], F32R) for i in range(2)]
        self.values = [sb(f"values{i}", [P, H, 32], F32) for i in range(2)]
        self.row_max = sb("row_max", [P, 8], F32)
        self.max_rows = sb("max_rows", [P, P], BF16)
        self.max_cols = sb("max_cols", [P, P], BF16)
        self.minus = sb("minus", [P, 8], F32)
        self.minus_head = sb("minus_head", [P, 8, P], BF16)
        self.ident16 = sb("ident16", [P, P], BF16)
        self.ident_r = sb("ident_r", [P, P], F32R)
        self.inv_sum = sb("inv_sum", [P, H, 1], F32)
        self.attn = sb("attn", [P, H, HD], F32)
        self.attn_cols = [sb(f"attn_cols{s}", [P, KT, P], F32R) for s in "hl"]

        self.ps_x = ps("ps_x", [P, 512], F32)
        self.ps_c = ps("ps_c", [P, 512], F32)
        self.ps_l = ps("ps_l", [P, 8, P], F32)
        self.ps_t = ps("ps_t", [P, 8, P], F32)
        self.ps_o = ps("ps_o", [P, H // 4, P], F32)
        self.out_heads = self.ps_o[:, :, :].rearrange("p g (h e) -> p (g h) e", e=32)

        self.w_in = [sem(f"w_in{i}") for i in range(3)]
        self.pos_in, self.bias_in = sem("pos_in"), sem("bias_in")
        self.ctx_in = [sem(f"ctx_in{i}") for i in range(2)]
        self.const_set = sem("const_set")
        self.minus_made = sem("minus_made")
        self.w_hi = sem("w_hi")
        self.w_lo = sem("w_lo")
        self.angle_step = sem("angle_step")
        self.trig = sem("trig")
        self.trig_signed = sem("trig_signed")
        self.stats_done = sem("stats_done")
        self.mean_done = sem("mean_done")
        self.var_done = sem("var_done")
        self.rstd_done = sem("rstd_done")
        self.normed_done = sem("normed_done")
        self.tables_copied = sem("tables_copied")
        self.ctx_turned = sem("ctx_turned")
        self.ctx_hi = sem("ctx_hi")
        self.ctx_lo = sem("ctx_lo")
        self.x_turned = sem("x_turned")
        self.x_hi = sem("x_hi")
        self.x_lo = sem("x_lo")
        self.k_done = sem("k_done")
        self.k_copied = sem("k_copied")
        self.v_done = sem("v_done")
        self.v_copied = sem("v_copied")
        self.q_done = sem("q_done")
        self.q_copied = sem("q_copied")
        self.rope_parts = sem("rope_parts")
        self.k_rotated = sem("k_rotated")
        self.q_rotated = sem("q_rotated")
        self.k_hi = sem("k_hi")
        self.k_lo = sem("k_lo")
        self.q_hi = sem("q_hi")
        self.q_lo = sem("q_lo")
        self.k_turned = sem("k_turned")
        self.even_copied = sem("even_copied")
        self.odd_copied = sem("odd_copied")
        self.q_turned = sem("q_turned")
        self.q_cols_done = sem("q_cols_done")
        self.biased = sem("biased")
        self.logits_done = sem("logits_done")
        self.maxed = sem("maxed")
        self.o_copied = sem("o_copied")
        self.o_turned = sem("o_turned")
        self.ident_made = sem("ident_made")
        self.max_hi = sem("max_hi")
        self.max_lo = sem("max_lo")
        self.max_turned = sem("max_turned")
        self.max_copied = sem("max_copied")
        self.logits_t_done = sem("logits_t_done")
        self.exp_done = sem("exp_done")
        self.values_done = sem("values_done")
        self.inverted = sem("inverted")
        self.scaled = sem("scaled")
        self.attn_turned = sem("attn_turned")
        self.attn_hi = sem("attn_hi")
        self.attn_lo = sem("attn_lo")
        self.out_done = sem("out_done")
        self.added = sem("added")

    def turn_ctx(self, pe, m, p):
        pe.wait_ge(self.ctx_in[p], (m // 2 + 1) * 16 if isinstance(m, int) else (m + 2 - p) * 8)
        pe.wait_ge(self.v_copied, done(m - 1))
        for k in range(self.CT):
            mm = pe.transpose(self.ps_c[:, k * P:(k + 1) * P], self.ctx_rows[p][:, k * P:(k + 1) * P], self.ident[:, :])
        mm.then_inc(self.ctx_turned, 1)

    def project_k(self, pe, m):
        pe.wait_ge(self.ctx_lo, done(m))
        for k in range(self.CT):
            mm = matmul_split(pe, self.ps_c[:, :], [c[:, k, :] for c in self.ctx_cols],
                              [w[:, k, 0:self.D] for w in self.wkv], k == 0, k == self.CT - 1)
        mm.then_inc(self.k_done, 1)

    def project_v(self, pe, m):
        pe.wait_ge(self.k_copied, done(m))
        pe.wait_ge(self.even_copied, done(4 * m - 1))
        pe.wait_ge(self.odd_copied, done(4 * m - 1))
        for k in range(self.CT):
            mm = matmul_split(pe, self.ps_c[:, :], [c[:, k, :] for c in self.ctx_cols],
                              [w[:, k, self.D:2 * self.D] for w in self.wkv], k == 0, k == self.CT - 1)
        mm.then_inc(self.v_done, 1)

    def turn_x(self, pe, m):
        pe.wait_ge(self.normed_done, done(m))
        pe.wait_ge(self.added, done(m - 4))
        pe.wait_ge(self.q_cols_done, done(4 * m - 5))
        pe.wait_ge(self.q_copied, done(m - 1))
        for k in range(self.KT):
            mm = pe.transpose(self.ps_x[:, k * P:(k + 1) * P], self.normed[:, k * P:(k + 1) * P], self.ident[:, :])
        mm.then_inc(self.x_turned, 1)

    def project_q(self, pe, m):
        pe.wait_ge(self.x_lo, done(m))
        for k in range(self.KT):
            mm = matmul_split(pe, self.ps_x[:, :], [c[:, k, :] for c in self.x_cols],
                              [w[:, k, :] for w in self.wq], k == 0, k == self.KT - 1)
        mm.then_inc(self.q_done, 1)

    def turn_k(self, pe, m, j, projected):
        pe.wait_ge(self.k_lo, done(m))
        if j > 0:
            pe.wait_ge(self.even_copied, done(4 * m + j - 1))
            pe.wait_ge(self.odd_copied, done(4 * m + j - 1))
        elif projected:
            pe.wait_ge(self.k_copied, done(m + 1))
        else:
            pe.wait_ge(self.v_copied, done(m))
        self.turn_slots(pe, "k", self.ps_c, j).then_inc(self.k_turned, 1)

    def turn_q(self, pe, m, j, projected, finished):
        pe.wait_ge(self.q_lo, done(m))
        if j > 0:
            pe.wait_ge(self.q_cols_done, done(4 * m + j - 1))
        elif finished:
            pe.wait_ge(self.attn_lo, done(m - 2))
        elif projected:
            pe.wait_ge(self.q_copied, done(m + 1))
        self.turn_slots(pe, "q", self.ps_x, j).then_inc(self.q_turned, 1)

    def turn_slots(self, pe, which, into, j):
        for i in range(4):
            t = 4 * j + i
            mm = pe.transpose(into[:, i * P:(i + 1) * P].bitcast(F32R),
                              self.slots[which][:, 2 * t:2 * t + 2, :].rearrange("p h s -> p (h s)"), self.ident_r[:, :])
        return mm

    def logits(self, pe, b, p, c):
        n = 4 * b + c
        pe.wait_ge(self.q_cols_done, done(n))
        pe.wait_ge(self.even_copied, done(n))
        pe.wait_ge(self.odd_copied, done(n))
        pe.wait_ge(self.maxed, done(n - 1))
        for i in range(4):
            t = 4 * c + i
            mm = pe.matmul(self.ps_l[:, 2 * i:2 * i + 2, :].rearrange("p r k -> p (r k)"), self.q_cols[p][:, t, :],
                           self.k_cols[p][:, t, :, :].rearrange("p r k -> p (r k)"), start=True, stop=True)
        mm.then_inc(self.logits_done, 1)

    def turn_max(self, pe, b, c):
        pe.wait_ge(self.max_lo, done(4 * b + c))
        pe.wait_ge(self.exp_done, done(4 * b + c - 1))
        pe.transpose(self.ps_t[:, 0, 0:P // 2].bitcast(BF16), self.max_rows[:, :], self.ident16[:, :])\
            .then_inc(self.max_turned, 1)

    def logits_t(self, pe, b, p, c):
        n = 4 * b + c
        pe.wait_ge(self.max_copied, done(n))
        for h in range(8):
            t = 4 * c + h // 2
            pe.matmul(self.ps_t[:, h, :], self.k_cols[p][:, t, h % 2, :], self.q_cols[p][:, t, :], start=True, stop=False)
            mm = pe.matmul(self.ps_t[:, h, :], self.minus_head[:, h, :], self.max_cols[:, :], start=False, stop=True)
        mm.then_inc(self.logits_t_done, 1)

    def weigh_values(self, pe, b, p, c):
        n = 4 * b + c
        pe.wait_ge(self.exp_done, done(n))
        pe.wait_ge(self.v_copied, done(b))
        pe.wait_ge(self.scaled, done(b - 1))
        for h in range(8):
            j = h % 4
            mm = pe.matmul(self.ps_o[32 * j:32 * j + 32, 2 * c + h // 4, :], self.values[p][:, 8 * c + h, :],
                           self.probs[c % 2][:, h, :], start=True, stop=True)
        mm.then_inc(self.values_done, 1)

    def turn_out(self, pe, n):
        pe.wait_ge(self.o_copied, done(n))
        for g in range(self.H // 4):
            mm = pe.transpose(self.ps_o[:, g, :], self.o_cols[:, g, :], self.ident[:, :])
        mm.then_inc(self.o_turned, 1)

    def turn_attn(self, pe, n, projected):
        pe.wait_ge(self.scaled, done(n))
        if projected:
            pe.wait_ge(self.q_copied, done(n + 3))
        else:
            pe.wait_ge(self.added, done(n - 1))
        rows = self.attn[:, :, :].rearrange("p h e -> p (h e)")
        for k in range(self.KT):
            mm = pe.transpose(self.ps_x[:, k * P:(k + 1) * P], rows[:, k * P:(k + 1) * P], self.ident[:, :])
        mm.then_inc(self.attn_turned, 1)

    def project_out(self, pe, n, turned):
        pe.wait_ge(self.attn_lo, done(n))
        if turned:
            pe.wait_ge(self.q_cols_done, done(4 * n + 11))
        for k in range(self.KT):
            mm = matmul_split(pe, self.ps_x[:, :], [c[:, k, :] for c in self.attn_cols],
                              [w[:, k, :] for w in self.wo], k == 0, k == self.KT - 1)
        mm.then_inc(self.out_done, 1)

    def tensor_step(self, pe, b, p, stages):
        project, turn, attend, finish = [s in stages for s in (PROJECT, TURN, ATTEND, FINISH)]
        l, m, n = b + 2, b + 1, b - 1
        if attend:
            self.logits(pe, b, p, 0)
        if turn:
            self.project_v(pe, m)
        if project:
            self.turn_x(pe, l)
            self.turn_ctx(pe, l, p)
        if finish:
            self.turn_out(pe, n)
        if attend:
            self.logits(pe, b, p, 1)
            self.turn_max(pe, b, 0)
            self.logits_t(pe, b, p, 0)
        if project:
            self.project_q(pe, l)
        if attend:
            self.weigh_values(pe, b, p, 0)
            self.logits(pe, b, p, 2)
            self.turn_max(pe, b, 1)
            self.logits_t(pe, b, p, 1)
        if finish:
            self.turn_attn(pe, n, project)
        if project:
            self.project_k(pe, l)
        if attend:
            self.weigh_values(pe, b, p, 1)
        if turn:
            self.turn_q(pe, m, 0, project, finish)
            self.turn_k(pe, m, 0, project)
        if attend:
            self.logits(pe, b, p, 3)
            self.turn_max(pe, b, 2)
            self.logits_t(pe, b, p, 2)
        if turn:
            self.turn_q(pe, m, 1, project, finish)
            self.turn_k(pe, m, 1, project)
        if attend:
            self.weigh_values(pe, b, p, 2)
        if turn:
            self.turn_q(pe, m, 2, project, finish)
            self.turn_k(pe, m, 2, project)
        if attend:
            self.turn_max(pe, b, 3)
            self.logits_t(pe, b, p, 3)
        if turn:
            self.turn_q(pe, m, 3, project, finish)
            self.turn_k(pe, m, 3, project)
        if attend:
            self.weigh_values(pe, b, p, 3)
        if finish:
            self.project_out(pe, n, turn)

    def ctx_high(self, act, m):
        act.wait_ge(self.ctx_turned, done(m))
        act.wait_ge(self.v_done, done(m - 1))
        act.activation(self.ctx_cols[0][:, :, :], self.ps_c[:, 0:self.CT * P].rearrange("p (k t) -> p k t", k=self.CT),
                       ACT.Copy).then_inc(self.ctx_hi, 1)

    def x_high(self, act, m):
        act.wait_ge(self.x_turned, done(m))
        act.wait_ge(self.q_done, done(m - 1))
        act.activation(self.x_cols[0][:, :, :], self.ps_x[:, :].rearrange("p (k t) -> p k t", k=self.KT),
                       ACT.Copy).then_inc(self.x_hi, 1)

    def copy_k(self, act, m):
        act.wait_ge(self.k_done, done(m))
        act.wait_ge(self.k_rotated, done(m - 1))
        act.activation(self.rows["k"][:, :], self.ps_c[:, :], ACT.Copy).then_inc(self.k_copied, 1)

    def copy_v(self, act, m, p):
        act.wait_ge(self.v_done, done(m))
        act.wait_ge(self.values_done, done(4 * m - 5))
        act.activation(self.values[p][:, :, 0:self.HD], self.ps_c[:, :].rearrange("p (h e) -> p h e", h=self.H),
                       ACT.Copy).then_inc(self.v_copied, 1)

    def copy_q(self, act, m):
        act.wait_ge(self.q_done, done(m))
        act.wait_ge(self.q_rotated, done(m - 1))
        act.activation(self.rows["q"][:, :], self.ps_x[:, :], ACT.Copy).then_inc(self.q_copied, 1)

    def copy_q_cols(self, act, m, p, j):
        act.wait_ge(self.q_turned, done(4 * m + j))
        act.wait_ge(self.logits_t_done, done(4 * m - 5))
        act.activation(self.q_cols[p][:, 4 * j:4 * j + 4, :], self.ps_x[:, :].rearrange("p (i t) -> p i t", i=4),
                       ACT.Copy).then_inc(self.q_cols_done, 1)

    def copy_odd(self, act, m, p, j):
        act.wait_ge(self.k_turned, done(4 * m + j))
        act.wait_ge(self.logits_t_done, done(4 * m - 5))
        self.copy_block(act.activation, p, j, 1, ACT.Copy).then_inc(self.odd_copied, 1)

    def copy_block(self, copy, p, j, r, *how):
        at = slice(self.SLOT * r, self.SLOT * (r + 1))
        return copy(self.k_cols[p][at, 4 * j:4 * j + 4, r, :], self.ps_c[at, :].rearrange("p (i t) -> p i t", i=4), *how)

    def copy_max(self, act, b, c):
        act.wait_ge(self.max_turned, done(4 * b + c))
        act.wait_ge(self.logits_t_done, done(4 * b + c - 1))
        act.activation(self.max_cols[:, :], self.ps_t[:, 0, 0:P // 2].bitcast(BF16), ACT.Copy).then_inc(self.max_copied, 1)

    def exponential(self, act, b, c):
        n = 4 * b + c
        act.wait_ge(self.logits_t_done, done(n))
        act.wait_ge(self.values_done, done(n - 2))
        act.activation(self.probs[c % 2][:, :, :], self.ps_t[:, :, :], ACT.Exp, scale=1.0 / math.sqrt(self.HD))\
            .then_inc(self.exp_done, 1)

    def copy_out(self, act, b):
        act.wait_ge(self.values_done, done(4 * b + 3))
        act.wait_ge(self.o_turned, done(b - 1))
        act.activation(self.o_cols[:, :, :], self.ps_o[:, :, :], ACT.Copy).then_inc(self.o_copied, 1)

    def attn_high(self, act, n):
        act.wait_ge(self.attn_turned, done(n))
        act.wait_ge(self.out_done, done(n - 1))
        act.activation(self.attn_cols[0][:, :, :], self.ps_x[:, :].rearrange("p (k t) -> p k t", k=self.KT),
                       ACT.Copy).then_inc(self.attn_hi, 1)

    def scalar_step(self, act, b, p, stages):
        project, turn, attend, finish = [s in stages for s in (PROJECT, TURN, ATTEND, FINISH)]
        l, m, n = b + 2, b + 1, b - 1
        if finish:
            self.copy_out(act, n)
        if turn:
            self.copy_v(act, m, 1 - p)
        if project:
            self.x_high(act, l)
            self.ctx_high(act, l)
        if attend:
            self.copy_max(act, b, 0)
            self.exponential(act, b, 0)
        if project:
            self.copy_q(act, l)
        if attend:
            self.copy_max(act, b, 1)
            self.exponential(act, b, 1)
        if finish:
            self.attn_high(act, n)
        if project:
            self.copy_k(act, l)
        if turn:
            self.copy_q_cols(act, m, 1 - p, 0)
            self.copy_odd(act, m, 1 - p, 0)
        if attend:
            self.copy_max(act, b, 2)
            self.exponential(act, b, 2)
        if turn:
            for j in (1, 2):
                self.copy_q_cols(act, m, 1 - p, j)
                self.copy_odd(act, m, 1 - p, j)
        if attend:
            self.copy_max(act, b, 3)
            self.exponential(act, b, 3)
        if turn:
            self.copy_q_cols(act, m, 1 - p, 3)
            self.copy_odd(act, m, 1 - p, 3)

    def normalise(self, dve, m):
        at = slice(m, m + 1) if isinstance(m, int) else bass.ds(m, 1)
        row = self.x[:, at, :].rearrange("p b d -> p (b d)")
        dve.wait_ge(self.x_turned, done(m - 1))
        dve.tensor_scalar(self.normed[:, :], row, self.mean_var[:, at, 0:1].rearrange("p b e -> p (b e)"),
                          self.rstd[:, at], ALU.subtract, ALU.mult).then_inc(self.normed_done, 1)

    def copy_tables(self, dve, m):
        at = slice(m, m + 1) if isinstance(m, int) else bass.ds(m, 1)
        dve.wait_ge(self.k_rotated, done(m - 1))
        dve.tensor_copy(self.tables_now[:, :, :], self.tables[:, at, :, :, :, :].rearrange("p b t a f e -> p (b t) (a f e)"))\
            .then_inc(self.tables_copied, 1)

    def ctx_low(self, dve, m):
        dve.wait_ge(self.ctx_hi, done(m))
        dve.tensor_tensor(self.ctx_cols[1][:, :, :], self.ps_c[:, 0:self.CT * P].rearrange("p (k t) -> p k t", k=self.CT),
                          self.ctx_cols[0][:, :, :].bitcast(F32), ALU.subtract).then_inc(self.ctx_lo, 1)

    def x_low(self, dve, m):
        dve.wait_ge(self.x_hi, done(m))
        dve.tensor_tensor(self.x_cols[1][:, :, :], self.ps_x[:, :].rearrange("p (k t) -> p k t", k=self.KT),
                          self.x_cols[0][:, :, :].bitcast(F32), ALU.subtract).then_inc(self.x_lo, 1)

    def fill_slots(self, dve, which, m):
        rot = self.rotated[which][:, :].rearrange("p (h e) -> p h e", h=self.H)
        slots, HD = self.slots[which], self.HD
        rotated, turned, hi_done, lo_done = ((self.k_rotated, self.k_turned, self.k_hi, self.k_lo) if which == "k" else
                                             (self.q_rotated, self.q_turned, self.q_hi, self.q_lo))
        dve.wait_ge(rotated, done(m))
        dve.wait_ge(turned, done(4 * m - 1))
        lo_at = 2 if which == "k" else 1
        hi_at = slots[:, :, 0:3 * HD].rearrange("p h (s e) -> p h s e", s=3)[:, :, 0:4 - lo_at:3 - lo_at, :]
        dve.tensor_copy(hi_at, rot.unsqueeze(2).to_broadcast([P, self.H, 2, HD])).then_inc(hi_done, 1)
        dve.wait_ge(hi_done, done(m))
        dve.tensor_tensor(slots[:, :, lo_at * HD:(lo_at + 1) * HD], rot, slots[:, :, 0:HD].bitcast(F32),
                          ALU.subtract).then_inc(lo_done, 1)

    def copy_even(self, dve, m, p, j):
        dve.wait_ge(self.k_turned, done(4 * m + j))
        dve.wait_ge(self.logits_t_done, done(4 * m - 5))
        self.copy_block(dve.tensor_copy, p, j, 0).then_inc(self.even_copied, 1)

    def maxima(self, dve, b, c):
        n = 4 * b + c
        dve.wait_ge(self.max_lo, done(n - 1))
        dve.wait_ge(self.logits_done, done(n))
        dve.tensor_reduce(self.row_max[:, :], self.ps_l[:, :, :], AX_X, ALU.max).then_inc(self.maxed, 1)
        dve.wait_ge(self.maxed, done(n))
        dve.wait_ge(self.max_turned, done(n - 1))
        dve.tensor_copy(self.max_rows[:, 0:8], self.row_max[:, :]).then_inc(self.max_hi, 1)
        dve.wait_ge(self.max_hi, done(n))
        dve.tensor_tensor(self.max_rows[:, 8:16], self.row_max[:, :], self.max_rows[:, 0:8], ALU.subtract)\
            .then_inc(self.max_lo, 1)

    def scale_heads(self, dve, b):
        dve.wait_ge(self.o_turned, done(b))
        dve.reciprocal(self.inv_sum[:, :, :], self.out_heads[:, :, self.HD:self.HD + 1]).then_inc(self.inverted, 1)
        dve.wait_ge(self.inverted, done(b))
        dve.wait_ge(self.attn_turned, done(b - 1))
        dve.tensor_tensor(self.attn[:, :, :], self.out_heads[:, :, 0:self.HD],
                          self.inv_sum[:, :, :].to_broadcast([P, self.H, self.HD]), ALU.mult).then_inc(self.scaled, 1)

    def attn_low(self, dve, n):
        dve.wait_ge(self.attn_hi, done(n))
        dve.tensor_tensor(self.attn_cols[1][:, :, :], self.ps_x[:, :].rearrange("p (k t) -> p k t", k=self.KT),
                          self.attn_cols[0][:, :, :].bitcast(F32), ALU.subtract).then_inc(self.attn_lo, 1)

    def add_output(self, dve, n):
        at = slice(n, n + 1) if isinstance(n, int) else bass.ds(n, 1)
        row = self.x[:, at, :].rearrange("p b d -> p (b d)")
        dve.wait_ge(self.out_done, done(n))
        dve.wait_ge(self.biased, done(n))
        dve.tensor_tensor(row, row, self.ps_x[:, :], ALU.add).then_inc(self.added, 1)

    def vector_step(self, dve, b, p, stages):
        project, turn, attend, finish = [s in stages for s in (PROJECT, TURN, ATTEND, FINISH)]
        l, m, n = b + 2, b + 1, b - 1
        if attend:
            self.maxima(dve, b, 0)
        if project:
            self.copy_tables(dve, l)
            self.x_low(dve, l)
            self.ctx_low(dve, l)
        if finish:
            self.scale_heads(dve, n)
        if attend:
            self.maxima(dve, b, 1)
        if turn:
            self.fill_slots(dve, "q", m)
            self.fill_slots(dve, "k", m)
        if attend:
            self.maxima(dve, b, 2)
        if finish:
            self.attn_low(dve, n)
        if turn:
            self.copy_even(dve, m, 1 - p, 0)
        if attend:
            self.maxima(dve, b, 3)
        if turn:
            for j in (1, 2, 3):
                self.copy_even(dve, m, 1 - p, j)
        if NEXT in stages:
            self.normalise(dve, l + 1)
        if finish:
            self.add_output(dve, n)

    def rotate(self, pool, which, m):
        n = 2 * m + (which == "k")
        copied, rotated, split = ((self.k_copied, self.k_rotated, self.k_lo) if which == "k" else
                                  (self.q_copied, self.q_rotated, self.q_lo))
        full = [P, self.H, self.HD]
        cos = self.tables_now[:, 0:1, :].to_broadcast(full)
        sin = self.tables_now[:, 1:2, :].rearrange("p a (f e) -> p a f e", e=2).to_broadcast([P, self.H, self.HD // 2, 2])
        rows = self.rows[which][:, :].rearrange("p (h e) -> p h e", h=self.H)
        swapped = self.rows[which][:, :].rearrange("p (h f e) -> p h f e", h=self.H, e=2)[:, :, :, ::-1]
        pool.wait_ge(copied, done(m))
        pool.wait_ge(self.tables_copied, done(m))
        pool.tensor_tensor(self.by_cos[:, :].rearrange("p (h e) -> p h e", h=self.H), rows, cos, ALU.mult)
        pool.tensor_tensor(self.by_sin[:, :].rearrange("p (h f e) -> p h f e", h=self.H, e=2), swapped, sin, ALU.mult)\
            .then_inc(self.rope_parts, 1)
        pool.wait_ge(self.rope_parts, done(n))
        pool.wait_ge(split, done(m - 1))
        pool.tensor_tensor(self.rotated[which][:, :], self.by_cos[:, :], self.by_sin[:, :], ALU.add).then_inc(rotated, 1)
        pool.wait_ge(rotated, done(m))

    def add_bias(self, pool, m):
        at = slice(m, m + 1) if isinstance(m, int) else bass.ds(m, 1)
        row = self.x[:, at, :].rearrange("p b d -> p (b d)")
        pool.wait_ge(self.normed_done, done(m))
        pool.wait_ge(self.bias_in, 16)
        pool.tensor_tensor(row, row, self.bias[:, :], ALU.add).then_inc(self.biased, 1)

    def pool_step(self, pool, l):
        self.rotate(pool, "q", l)
        self.add_bias(pool, l)
        self.rotate(pool, "k", l)

    def run(self, block):
        NB, H, HD = self.NB, self.H, self.HD
        ALL = {PROJECT, TURN, ATTEND, FINISH, NEXT}
        first = ((-2, {PROJECT, NEXT}), (-1, {PROJECT, TURN, NEXT}), (0, {PROJECT, TURN, ATTEND, NEXT}))
        LOOPS = (NB - 4) // 2
        last = ((NB - 3, {PROJECT, TURN, ATTEND, FINISH}), (NB - 2, {TURN, ATTEND, FINISH}), (NB - 1, {ATTEND, FINISH}),
                (NB, {FINISH}))
        TWO_PI = 2 * math.pi

        @block.sync
        def _(sp):
            for raw, w, got in zip(self.raw, (self.Wq, self.Wkv, self.Wout), self.w_in):
                sp.dma_start(raw, w.rearrange("(k p) n -> p k n", p=P)).then_inc(got, 16)
            sp.dma_start(self.pos[:, :, :], self.pos_dram.rearrange("b t a -> t b a")).then_inc(self.pos_in, 16)
            sp.dma_start(self.bias[:, :], self.bout.rearrange("(a d) -> a d", a=1).to_broadcast([P, self.D]))\
                .then_inc(self.bias_in, 16)
            for p in range(2):
                sp.dma_start(self.ctx_rows[p][:, :], self.ctx_dram[p]).then_inc(self.ctx_in[p], 16)
            with sp.Fori(1, NB // 2) as i:
                for p in range(2):
                    m = i * 2 + p
                    sp.wait_ge(self.ctx_turned, done(m - 2))
                    sp.dma_start(self.ctx_rows[p][:, :], self.ctx_dram[bass.ds(m, 1)].rearrange("b t d -> (b t) d"))\
                        .then_inc(self.ctx_in[p], 16)

        @block.gpsimd
        def _(pool):
            start(pool, self.rope_parts, self.k_rotated, self.q_rotated, self.biased)
            for which in "qk":
                pool.memset(self.slots[which][:, :, 3 * HD:self.SLOT].bitcast(F32), 0.0).then_inc(self.const_set, 1)
            pool.memset(self.max_rows[:, :], 0.0).then_inc(self.const_set, 1)
            for i in range(2):
                pool.memset(self.values[i][:, :, HD:HD + 1], 1.0).then_inc(self.const_set, 1)
                pool.memset(self.values[i][:, :, HD + 1:32], 0.0).then_inc(self.const_set, 1)
                pool.memset(self.k_cols[i][0:self.SLOT, :, 1, :].bitcast(F32), 0.0).then_inc(self.const_set, 1)
            pool.memset(self.half_pi[:, :], math.pi / 2).then_inc(self.const_set, 1)
            pool.wait_ge(self.const_set, self.CONSTS - 2)
            for i in range(2):
                pool.memset(self.k_cols[i][self.SLOT:P, :, 0, :].bitcast(F32), 0.0).then_inc(self.const_set, 1)
            pool.wait_ge(self.const_set, self.CONSTS)
            pool.wait_ge(self.var_done, 1)
            pool.tensor_tensor(self.rstd[:, :], self.var_eps[:, :], self.minus_half[:, :].to_broadcast([P, NB]),
                               ALU.pow).then_inc(self.rstd_done, 1)
            pool.wait_ge(self.rstd_done, 1)
            self.pool_step(pool, 0)
            self.pool_step(pool, 1)
            with pool.Fori(1, NB // 2) as i:
                for p in range(2):
                    self.pool_step(pool, i * 2 + p)

        @block.scalar
        def _(act):
            start(act, self.ctx_hi, self.x_hi, self.k_copied, self.v_copied, self.q_copied, self.q_cols_done,
                  self.max_copied, self.exp_done, self.o_copied, self.attn_hi, self.odd_copied)
            for n, (raw, w) in enumerate(zip(self.raw, (self.wq, self.wkv, self.wo))):
                act.wait_ge(self.w_in[n], 16)
                act.activation(w[0][:, :, :], raw, ACT.Copy).then_inc(self.w_hi, 1)
            act.wait_ge(self.const_set, self.CONSTS)
            act.wait_ge(self.angle_step, 10)
            act.activation(self.sin[:, :, :, :, 1], self.angle[:, :, :, :], ACT.Sin)
            act.activation(self.turns[:, :, :, :], self.angle[:, :, :, :], ACT.Abs).then_inc(self.trig, 1)
            act.wait_ge(self.trig, 1)
            for e in range(2):
                ins = act.activation(self.cos[:, :, :, :, e], self.turns[:, :, :, :], ACT.Sin, bias=self.half_pi[:, :],
                                     scale=-1.0)
            ins.then_inc(self.trig, 1)
            for b, stages in first:
                self.scalar_step(act, b, b % 2, stages)
            with act.Fori(0, LOOPS) as i:
                for q in range(2):
                    self.scalar_step(act, i * 2 + 1 + q, (1 + q) % 2, ALL)
            for b, stages in last:
                self.scalar_step(act, b, b % 2, stages)

        @block.vector
        def _(dve):
            start(dve, self.normed_done, self.tables_copied, self.ctx_lo, self.x_lo, self.k_hi, self.k_lo, self.q_hi, self.q_lo,
                  self.even_copied, self.maxed, self.max_hi, self.max_lo, self.inverted, self.scaled, self.attn_lo,
                  self.added)
            for b in range(NB):
                dve.bn_stats(self.stats[:, b, :], self.x[:, b, :]).then_inc(self.stats_done, 1)
            dve.wait_ge(self.stats_done, NB)
            for b in range(NB):
                dve.bn_aggr(self.mean_var[:, b, :], self.stats[:, b, :]).then_inc(self.mean_done, 1)
            dve.wait_ge(self.mean_done, NB)
            dve.tensor_scalar(self.var_eps[:, :], self.mean_var[:, :, 1], EPS_LN, None, ALU.add).then_inc(self.var_done, 1)
            dve.wait_ge(self.pos_in, 16)
            steps = [0]

            def stepped(ins):
                ins.then_inc(self.angle_step, 1)
                steps[0] += 1
                dve.wait_ge(self.angle_step, steps[0])

            for f in range(4):
                stepped(dve.tensor_scalar(self.angle[:, :, :, f], self.pos[:, :, :], 10000.0 ** (-f / 4), None, ALU.mult))
            ROUND = 1.5 * 2.0 ** 23
            stepped(dve.tensor_scalar(self.turns[:, :, :, :], self.angle[:, :, :, :], 1 / TWO_PI, ROUND, ALU.mult, ALU.add))
            stepped(dve.tensor_scalar(self.turns[:, :, :, :], self.turns[:, :, :, :], ROUND, None, ALU.subtract))
            high = 6.28125
            middle = math.floor((TWO_PI - high) * 2 ** 21) / 2 ** 21
            for part in (high, middle, TWO_PI - high - middle):
                stepped(dve.scalar_tensor_tensor(self.angle[:, :, :, :].rearrange("p b a f -> p (b a f)"),
                                                 self.turns[:, :, :, :].rearrange("p b a f -> p (b a f)"), -part,
                                                 self.angle[:, :, :, :].rearrange("p b a f -> p (b a f)"), ALU.mult, ALU.add))
            stepped(dve.tensor_scalar(self.angle[:, :, :, :], self.angle[:, :, :, :], 3.1415925, -3.1415925, ALU.min, ALU.max))
            for n, (raw, w) in enumerate(zip(self.raw, (self.wq, self.wkv, self.wo))):
                dve.wait_ge(self.w_hi, n + 1)
                dve.tensor_tensor(w[1][:, :, :], raw, w[0][:, :, :].bitcast(F32), ALU.subtract).then_inc(self.w_lo, 1)
            dve.tensor_copy(self.ident16[:, :], self.ident[:, :]).then_inc(self.ident_made, 1)
            dve.tensor_copy(self.ident_r[:, :], self.ident[:, :]).then_inc(self.ident_made, 1)
            dve.tensor_reduce(self.minus[:, :], self.ident[:, 0:16].rearrange("p (a h) -> p h a", a=2), AX_X, ALU.add,
                              negate=True).then_inc(self.minus_made, 1)
            dve.wait_ge(self.minus_made, 1)
            dve.tensor_copy(self.minus_head[:, :, :], self.minus[:, :].unsqueeze(2).to_broadcast([P, 8, P]))\
                .then_inc(self.minus_made, 1)
            dve.wait_ge(self.trig, 2)
            dve.tensor_scalar(self.sin[:, :, :, :, 0], self.sin[:, :, :, :, 1], -1.0, None, ALU.mult).then_inc(self.trig_signed, 1)
            dve.wait_ge(self.trig_signed, 1)
            dve.wait_ge(self.rstd_done, 1)
            dve.wait_ge(self.const_set, self.CONSTS)
            self.normalise(dve, 0)
            for b, stages in first:
                self.vector_step(dve, b, b % 2, stages)
            with dve.Fori(0, LOOPS) as i:
                for q in range(2):
                    self.vector_step(dve, i * 2 + 1 + q, (1 + q) % 2, ALL)
            for b, stages in last:
                self.vector_step(dve, b, b % 2, stages)
            dve.wait_ge(self.added, done(NB - 1))

        @block.tensor
        def _(pe):
            start(pe, self.ctx_turned, self.x_turned, self.k_done, self.v_done, self.q_done, self.k_turned,
                  self.q_turned, self.logits_done, self.max_turned, self.logits_t_done, self.values_done,
                  self.attn_turned, self.out_done, self.o_turned)
            pe.wait_ge(self.w_lo, 3)
            pe.wait_ge(self.minus_made, 2)
            pe.wait_ge(self.ident_made, 2)
            pe.wait_ge(self.const_set, self.CONSTS)
            for b, stages in first:
                self.tensor_step(pe, b, b % 2, stages)
            with pe.Fori(0, LOOPS) as i:
                for q in range(2):
                    self.tensor_step(pe, i * 2 + 1 + q, (1 + q) % 2, ALL)
            for b, stages in last:
                self.tensor_step(pe, b, b % 2, stages)


class FeedForward:

    def __init__(self, nc, ctx, x, ident, ones, minus_half, gu_packed, gu_scales, down_packed, down_scales, out):
        sb = lambda n, s, d: ctx.enter_context(nc.sbuf_tensor("c_" + n, s, d))
        ps = lambda n, s, d: ctx.enter_context(nc.psum_tensor("c_" + n, s, d))
        sem = lambda n: ctx.enter_context(nc.semaphore("c_" + n))
        self.nc, self.x, self.ident, self.out = nc, x, ident, out
        self.gu_packed, self.gu_scales, self.down_packed, self.down_scales = gu_packed, gu_scales, down_packed, down_scales
        NB = self.NB = x.shape[1]
        D = self.D = x.shape[2]
        KT = self.KT = D // P
        C = self.C = gu_packed.shape[0] // 2 // P
        self.BLK = 4
        self.TILES_AT = ((), (), (0, 1), (2,))
        self.WG, self.WD = D // 8, P // 8
        self.WORDS = 2 * self.WG + KT * self.WD

        self.x_cols = [sb(f"x_cols{s}", [P, KT, NB * P], F32R) for s in "hl"]
        self.y = sb("y", [P, NB, D], F32)
        self.gu_s16 = sb("gu_s16", [KT, 2 * C * P], F16)
        self.gu_s = sb("gu_s", [P, 2, C, KT], F32)
        self.down_s16 = sb("down_s16", [C, D], F16)
        self.down_s = sb("down_s", [P, KT, C], F32)
        self.ident16 = sb("ident16", [P, P], F16)
        self.packed = [sb(f"packed{i}", [P, self.WORDS], I32) for i in range(2)]
        self.magnitude = sb("magnitude", [P, 4, self.WORDS], U32)
        self.sign = sb("sign", [P, 4, self.WORDS], U32)
        self.code = sb("code", [P, 4, self.WORDS], U32)
        self.scaled = sb("scaled", [P, 12, P], F32)
        self.w = [[[sb(f"w{i}{n}{s}", [P, KT, P], F32R) for s in "hl"] for n in range(3)] for i in range(2)]
        self.silu = [sb(f"silu{i}", [P, 512], F32) for i in range(2)]
        self.h = [sb(f"h{i}", [P, 512], F32) for i in range(2)]
        self.h_cols = [sb(f"h_cols{s}", [P, NB * P], F32R) for s in "hl"]
        self.squares = sb("squares", [P, D], F32)
        self.sum_sq = sb("sum_sq", [P, NB], F32)
        self.mean_sq = sb("mean_sq", [P, NB], F32)
        self.inv_rms = sb("inv_rms", [P, NB], F32)
        self.minus_half = minus_half

        self.ps_g = ps("ps_g", [P, 2, 512], F32)
        self.ps_u = ps("ps_u", [P, 2, 512], F32)
        self.ps_y = ps("ps_y", [P, 2, 512], F32)
        self.ps_w = ps("ps_w", [P, 2, KT, P], F32)
        self.ln = LayerNorm(nc, sb, sem, "ln_", x, self.x_cols, self.ps_g[:, :, :].rearrange("p h (k t) -> p h k t", k=KT),
                            ident, minus_half, NB, KT)
        self.scales_in, self.stored = sem("scales_in"), sem("stored")
        self.packed_in = [sem(f"packed_in{i}") for i in range(2)]
        self.ident16_made = sem("ident16_made")
        self.scales_turned = sem("scales_turned")
        self.scales_copied = sem("scales_copied")
        self.bits_cut = sem("bits_cut")
        self.coded = sem("coded")
        self.weights_scaled = sem("weights_scaled")
        self.w_turned = sem("w_turned")
        self.w_hi = sem("w_hi")
        self.w_lo = sem("w_lo")
        self.gu_done = sem("gu_done")
        self.silu_done = sem("silu_done")
        self.h_made = sem("h_made")
        self.h_hi = sem("h_hi")
        self.h_lo = sem("h_lo")
        self.y_done = sem("y_done")
        self.y_added = sem("y_added")
        self.y_cleared = sem("y_cleared")
        self.squared = sem("squared")
        self.mean_done = sem("mean_done")
        self.rms_done = sem("rms_done")
        self.out_made = sem("out_made")

    def load_packed(self, sp, c, p):
        at = slice(c, c + 1) if isinstance(c, int) else bass.ds(c, 1)
        sp.wait_ge(self.coded, done(c - 2))
        for a in range(2):
            src = self.gu_packed.rearrange("(a c p) w -> a c p w", a=2, p=P)[a, at]
            sp.dma_start(self.packed[p][:, a * self.WG:(a + 1) * self.WG], src.rearrange("c p w -> (c p) w"))\
                .then_inc(self.packed_in[p], 16)
        src = self.down_packed.rearrange("(t p) (c w) -> c p t w", p=P, w=self.WD)[at]
        sp.dma_start(self.packed[p][:, 2 * self.WG:].rearrange("p (t w) -> p t w", w=self.WD),
                     src.rearrange("c p t w -> (c p) t w")).then_inc(self.packed_in[p], 16)

    def decode(self, dve, c, p):
        dve.wait_ge(self.packed_in[p], 48 * (c // 2 + 1) if isinstance(c, int) else (c + 2 - p) * 24)
        packed = self.packed[p][:, :].bitcast(U32)
        for j in range(4):
            for into, left, mask in ((self.magnitude, 9 - 4 * j, 0x0E000E00), (self.sign, 12 - 4 * j, 0x80008000)):
                op = ALU.logical_shift_left if left >= 0 else ALU.logical_shift_right
                ins = dve.tensor_scalar(into[:, j, :], packed, abs(left), mask, op, ALU.bitwise_and)
        ins.then_inc(self.bits_cut, 1)
        dve.wait_ge(self.bits_cut, done(c))
        dve.wait_ge(self.weights_scaled, done(12 * c - 1))
        dve.tensor_tensor(self.code[:, :, :], self.magnitude[:, :, :], self.sign[:, :, :], ALU.bitwise_or)\
            .then_inc(self.coded, 1)

    def scale_weights(self, act, c, n):
        at = slice(c, c + 1) if isinstance(c, int) else bass.ds(c, 1)
        a, g = n // 4, n % 4
        words = self.code[:, :, n * self.WD:(n + 1) * self.WD].bitcast(F16).rearrange("p j (w h) -> p w h j", h=2)
        scale = self.gu_s[:, a, at, g] if a < 2 else self.down_s[:, g, at]
        act.wait_ge(self.coded, done(c))
        act.wait_ge(self.w_turned, done(3 * c - 3 + a))
        act.activation(self.scaled[:, n, :].rearrange("p (w h j) -> p w h j", h=2, j=4), words, ACT.Copy,
                       scale=scale).then_inc(self.weights_scaled, 1)

    def turn_weights(self, pe, c, p, a):
        bank = (p + a) % 2
        pe.wait_ge(self.weights_scaled, done(12 * c + 4 * a + 3))
        pe.wait_ge(self.w_lo, done(3 * c + a - 2))
        for t in range(4):
            mm = pe.transpose(self.ps_w[:, bank, t, :], self.scaled[:, 4 * a + t, :], self.ident[:, :])
        mm.then_inc(self.w_turned, 1)

    def split_high(self, act, c, p, a):
        act.wait_ge(self.w_turned, done(3 * c + a))
        act.wait_ge(self.y_done, done(16 * (c - 2) + 15))
        act.activation(self.w[p][a][0][:, :, :], self.ps_w[:, (p + a) % 2, :, :], ACT.Copy).then_inc(self.w_hi, 1)

    def split_low(self, dve, c, p, a):
        dve.wait_ge(self.w_hi, done(3 * c + a))
        dve.tensor_tensor(self.w[p][a][1][:, :, :], self.ps_w[:, (p + a) % 2, :, :],
                          self.w[p][a][0][:, :, :].bitcast(F32), ALU.subtract).then_inc(self.w_lo, 1)

    def gate_up(self, pe, c, p, tb):
        n, tok = 4 * c + tb, slice(tb * 512, (tb + 1) * 512)
        pe.wait_ge(self.w_lo, done(3 * c + 1))
        pe.wait_ge(self.h_made, done(n - 2))
        for a, bank in ((0, self.ps_g), (1, self.ps_u)):
            for k in range(self.KT):
                mm = matmul_split(pe, bank[:, tb % 2, :], [w[:, k, :] for w in self.w[p][a]],
                                  [x[:, k, tok] for x in self.x_cols], k == 0, k == self.KT - 1)
        mm.then_inc(self.gu_done, 1)

    def down(self, pe, c, p, tb):
        pe.wait_ge(self.h_lo, done(4 * c + tb))
        pe.wait_ge(self.w_lo, done(3 * c + 2))
        w = [v[:, :, :].rearrange("p t h -> p (t h)") for v in self.w[p][2]]
        for i in range(self.BLK):
            t = tb * self.BLK + i
            pe.wait_ge(self.y_added, done(16 * c + t - 2))
            matmul_split(pe, self.ps_y[:, t % 2, :], [h[:, t * P:(t + 1) * P] for h in self.h_cols], w, True, True)\
                .then_inc(self.y_done, 1)

    def tensor_chunk(self, pe, c, p, first, last):
        for tb in range(4):
            self.gate_up(pe, c, p, tb)
            if not last:
                for a in self.TILES_AT[tb]:
                    self.turn_weights(pe, c + 1, 1 - p, a)
            if tb > 0:
                self.down(pe, c, p, tb - 1)
            elif not first:
                self.down(pe, c - 1, 1 - p, 3)

    def gate_high(self, act, c, tb):
        n = 4 * c + tb
        act.wait_ge(self.gu_done, done(n))
        act.wait_ge(self.h_made, done(n - 2))
        act.activation(self.silu[tb % 2][:, :], self.ps_g[:, tb % 2, :], ACT.Silu).then_inc(self.silu_done, 1)
        act.wait_ge(self.h_made, done(n))
        act.wait_ge(self.y_done, done(16 * (c - 1) + 4 * tb + 3))
        act.activation(self.h_cols[0][:, tb * 512:(tb + 1) * 512], self.h[tb % 2][:, :], ACT.Copy).then_inc(self.h_hi, 1)

    def scalar_chunk(self, act, c, p, last):
        for tb in range(4):
            self.gate_high(act, c, tb)
            if not last and tb == 1:
                for n in range(12):
                    self.scale_weights(act, c + 1, n)
            if not last:
                for a in self.TILES_AT[tb]:
                    self.split_high(act, c + 1, 1 - p, a)

    def pool_chunk(self, pool, c):
        for tb in range(4):
            pool.wait_ge(self.h_hi, done(4 * c + tb))
            pool.tensor_tensor(self.h_cols[1][:, tb * 512:(tb + 1) * 512], self.h[tb % 2][:, :],
                               self.h_cols[0][:, tb * 512:(tb + 1) * 512].bitcast(F32), ALU.subtract).then_inc(self.h_lo, 1)

    def multiply(self, dve, c, tb):
        n = 4 * c + tb
        dve.wait_ge(self.silu_done, done(n))
        dve.wait_ge(self.h_lo, done(n - 2))
        dve.tensor_tensor(self.h[tb % 2][:, :], self.silu[tb % 2][:, :], self.ps_u[:, tb % 2, :], ALU.mult)\
            .then_inc(self.h_made, 1)

    def add_down(self, dve, c, tb, tiles):
        for i in tiles:
            t = tb * self.BLK + i
            dve.wait_ge(self.y_done, done(16 * c + t))
            dve.tensor_tensor(self.y[:, t, :], self.y[:, t, :], self.ps_y[:, t % 2, :], ALU.add).then_inc(self.y_added, 1)

    def vector_chunk(self, dve, c, p, first, last):
        for tb in range(4):
            before = (c, tb - 1) if tb > 0 else (c - 1, 3)
            if tb > 0 or not first:
                self.add_down(dve, *before, range(2))
            self.multiply(dve, c, tb)
            if tb > 0 or not first:
                self.add_down(dve, *before, range(2, 4))
            if not last:
                for a in self.TILES_AT[tb]:
                    self.split_low(dve, c + 1, 1 - p, a)
                if tb == 0:
                    self.decode(dve, c + 1, 1 - p)

    def run(self, block):
        NB, C, KT, D = self.NB, self.C, self.KT, self.D
        PAIRS = (C - 3) // 2
        rest = range(1 + 2 * PAIRS, C)

        @block.sync
        def _(sp):
            sp.dma_start(self.gu_s16[:, :], self.gu_scales).then_inc(self.scales_in, 16)
            sp.dma_start(self.down_s16[:, :], self.down_scales).then_inc(self.scales_in, 16)
            self.load_packed(sp, 0, 0)
            with sp.Fori(0, (C - 1) // 2) as i:
                for q in range(2):
                    self.load_packed(sp, i * 2 + 1 + q, (1 + q) % 2)
            for b in range(0, NB, 4):
                sp.wait_ge(self.out_made, b + 4)
                sp.dma_start(self.out[b:b + 4].rearrange("b t d -> t b d"), self.x[:, b:b + 4, :]).then_inc(self.stored, 16)
            sp.wait_ge(self.stored, 16 * (NB // 4))

        @block.gpsimd
        def _(pool):
            start(pool, self.h_lo)
            pool.memset(self.ident16[:, :], 0.0).then_inc(self.ident16_made, 1)
            pool.wait_ge(self.ident16_made, 1)
            pool.affine_select(out=self.ident16[:, :], in_=self.ident16[:, :], compare_op=ALU.not_equal, fill=1.0, base=0,
                               pattern=[[-1, P]], channel_multiplier=1).then_inc(self.ident16_made, 1)
            pool.memset(self.y[:, :, :], 0.0).then_inc(self.y_cleared, 1)
            pool.wait_ge(self.ident16_made, 2)
            for b in range(0, NB, 2):
                self.ln.pool(pool, b)
            self.pool_chunk(pool, 0)
            with pool.Fori(0, PAIRS) as i:
                for q in range(2):
                    self.pool_chunk(pool, i * 2 + 1 + q)
            for c in rest:
                self.pool_chunk(pool, c)
            for b in range(0, NB, 4):
                pool.wait_ge(self.mean_done, b // 4 + 1)
                pool.tensor_tensor(self.inv_rms[:, b:b + 4], self.mean_sq[:, b:b + 4],
                                   self.minus_half[:, :].to_broadcast([P, 4]), ALU.pow).then_inc(self.rms_done, 1)

        @block.scalar
        def _(act):
            start(act, self.weights_scaled, self.w_hi, self.silu_done, self.h_hi)
            act.wait_ge(self.scales_turned, 1)
            gu_turned = self.ps_u[:, 0, :].bitcast(F16)
            act.activation(self.gu_s[:, :, :, :].rearrange("p a c g -> p (a c g)"), gu_turned[:, 0:2 * C * KT], ACT.Copy,
                           scale=2.0 ** 14).then_inc(self.scales_copied, 1)
            down_turned = self.ps_u[:, 1, :].bitcast(F16)
            act.activation(self.down_s[:, :, :], down_turned[:, 0:KT * 16].rearrange("p (t c) -> p t c", c=16)[:, :, 0:C],
                           ACT.Copy, scale=2.0 ** 14).then_inc(self.scales_copied, 1)
            act.wait_ge(self.scales_copied, 2)
            for n in range(12):
                self.scale_weights(act, 0, n)
            for a in range(3):
                self.split_high(act, 0, 0, a)
            for b in range(0, NB, 2):
                self.ln.scalar(act, b)
            self.scalar_chunk(act, 0, 0, False)
            with act.Fori(0, PAIRS) as i:
                for q in range(2):
                    self.scalar_chunk(act, i * 2 + 1 + q, (1 + q) % 2, False)
            for c in rest:
                self.scalar_chunk(act, c, c % 2, c == C - 1)
            for b in range(NB):
                act.wait_ge(self.y_added, done(16 * (C - 1) + b))
                if b > 0:
                    act.wait_ge(self.squared, b)
                act.activation(self.squares[:, :], self.y[:, b, :], ACT.Square, accum_out=self.sum_sq[:, b:b + 1])\
                    .then_inc(self.squared, 1)

        @block.tensor
        def _(pe):
            start(pe, self.w_turned, self.gu_done, self.y_done)
            pe.wait_ge(self.scales_in, 32)
            pe.wait_ge(self.ident16_made, 2)
            for t in range(2 * C):
                pe.transpose(self.ps_u[:, 0, :].bitcast(F16)[:, t * KT:(t + 1) * KT], self.gu_s16[:, t * P:(t + 1) * P],
                             self.ident16[0:KT, 0:KT])
            for t in range(KT):
                mm = pe.transpose(self.ps_u[:, 1, :].bitcast(F16)[:, t * 16:t * 16 + C], self.down_s16[:, t * P:(t + 1) * P],
                                  self.ident16[0:C, 0:C])
            mm.then_inc(self.scales_turned, 1)
            for a in range(3):
                self.turn_weights(pe, 0, 0, a)
            for b in range(0, NB, 2):
                self.ln.tensor(pe, b)
            pe.wait_ge(self.ln.lo_done, NB)
            pe.wait_ge(self.scales_copied, 2)
            self.tensor_chunk(pe, 0, 0, True, False)
            with pe.Fori(0, PAIRS) as i:
                for q in range(2):
                    self.tensor_chunk(pe, i * 2 + 1 + q, (1 + q) % 2, False, False)
            for c in rest:
                self.tensor_chunk(pe, c, c % 2, False, c == C - 1)
            self.down(pe, C - 1, (C - 1) % 2, 3)

        @block.vector
        def _(dve):
            start(dve, self.bits_cut, self.coded, self.w_lo, self.h_made, self.y_added)
            self.decode(dve, 0, 0)
            for a in range(3):
                self.split_low(dve, 0, 0, a)
            for b in range(0, NB, 2):
                self.ln.vector(dve, b)
            dve.wait_ge(self.y_cleared, 1)
            self.vector_chunk(dve, 0, 0, True, False)
            with dve.Fori(0, PAIRS) as i:
                for q in range(2):
                    self.vector_chunk(dve, i * 2 + 1 + q, (1 + q) % 2, False, False)
            for c in rest:
                self.vector_chunk(dve, c, c % 2, False, c == C - 1)
            self.add_down(dve, C - 1, 3, range(4))
            for b in range(0, NB, 4):
                dve.wait_ge(self.squared, b + 4)
                dve.tensor_scalar(self.mean_sq[:, b:b + 4], self.sum_sq[:, b:b + 4], 1.0 / D, EPS_RMS, ALU.mult, ALU.add)\
                    .then_inc(self.mean_done, 1)
                dve.wait_ge(self.rms_done, b // 4 + 1)
                for t in range(b, b + 4):
                    dve.scalar_tensor_tensor(self.x[:, t, :], self.y[:, t, :], self.inv_rms[:, t:t + 1], self.x[:, t, :],
                                             ALU.mult, ALU.add).then_inc(self.out_made, 1)


def decoder_layer(nc, x_in, ctx_in, pos_in, Wq, Wk, Wv, Wo, bo, xWq, xWkv, xWout, xbout,
                  gu_packed, gu_scales, down_packed, down_scales, out):
    NB, T, D = x_in.shape
    with ExitStack() as ctx:
        sb = lambda n, s, d: ctx.enter_context(nc.sbuf_tensor(n, s, d))
        x = sb("x", [P, NB, D], F32)
        ident = sb("ident", [P, P], F32)
        minus_half = sb("minus_half", [P, 1], F32)
        ones = sb("ones", [P, 1], F32)
        const_set = ctx.enter_context(nc.semaphore("const_set"))
        with nc.Block() as block:
            @block.gpsimd
            def _(pool):
                pool.memset(minus_half[:, :], -0.5).then_inc(const_set, 1)
                pool.memset(ident[:, :], 0.0).then_inc(const_set, 1)
                pool.memset(ones[:, :], 1.0).then_inc(const_set, 1)
                pool.wait_ge(const_set, 3)
                pool.affine_select(out=ident[:, :], in_=ident[:, :], compare_op=ALU.not_equal, fill=1.0,
                                   base=0, pattern=[[-1, P]], channel_multiplier=1).then_inc(const_set, 1)
                pool.wait_ge(const_set, 4)
        linear_attention(nc, x, ident, ones, minus_half, x_in, Wq, Wk, Wv, Wo, bo)
        with ExitStack() as scope:
            attention = CrossAttention(nc, scope, x, ident, ones, minus_half, ctx_in, pos_in, xWq, xWkv, xWout, xbout)
            with nc.Block() as block:
                attention.run(block)
        with ExitStack() as scope:
            feed_forward = FeedForward(nc, scope, x, ident, ones, minus_half, gu_packed, gu_scales, down_packed,
                                       down_scales, out)
            with nc.Block() as block:
                feed_forward.run(block)


_INS = ['x', 'ctx_1024', 'fside_BxSx2_0', 'L0_attn_Wq', 'L0_attn_Wk', 'L0_attn_Wv', 'L0_attn_Wo', 'L0_attn_bo',
        'L0_xattn_Wq', 'L0_xattn_Wkv', 'L0_xattn_Wout', 'L0_xattn_bout', 'L0_ffn_gate_up_packed',
        'L0_ffn_gate_up_scales', 'L0_ffn_down_packed', 'L0_ffn_down_scales']


def kernel(**inputs):
    import numpy as _np
    import concourse.bacc as _bacc
    from concourse import mybir as _mybir
    from concourse.bass_utils import run_bass_kernel_spmd as _run

    nc = _bacc.Bacc("TRN2", target_bir_lowering=False, num_devices=1)
    arrays, args = {}, []
    for name in _INS:
        a = _np.ascontiguousarray(inputs[name])
        arrays[f"in_{name}"] = a
        args.append(nc.dram_tensor(f"in_{name}", a.shape, _mybir.dt.from_np(a.dtype), kind="ExternalInput").ap())
    args.append(nc.dram_tensor("out_x", (16, 128, 512), _mybir.dt.float32, kind="ExternalOutput").ap())
    decoder_layer(nc, *args)
    r = _run(nc, [arrays], core_ids=[0])
    return r.results[0]["out_x"]
```

```python
import math
from contextlib import ExitStack

import concourse.bass as bass
from concourse import mybir

F32 = mybir.dt.float32
F32R = mybir.dt.float32r
F16 = mybir.dt.float16
I32 = mybir.dt.int32
U32 = mybir.dt.uint32
BF16 = mybir.dt.bfloat16
ALU = mybir.AluOpType
ACT = mybir.ActivationFunctionType
AX_X = mybir.AxisListType.X

P = 128
EPS_LN = 1e-5
EPS_RMS = 1e-6
START = 32


def done(n):
    return START + 1 + n


def start(engine, *semaphores):
    for s in semaphores:
        engine.sem_inc(s, START)


def matmul_split(pe, out, stationary, moving, first, last):
    pe.matmul(out, stationary[0], moving[0], start=first, stop=False)
    pe.matmul(out, stationary[0], moving[1], start=False, stop=False)
    return pe.matmul(out, stationary[1], moving[0], start=False, stop=last)


class LayerNorm:

    def __init__(self, sb, sem, tag, x, stats, cols, ident, minus_half):
        self.x, self.stats, self.cols, self.ident, self.minus_half = x, stats, cols, ident, minus_half
        batches, features = x.shape[1], x.shape[2]
        self.kt = features // P
        self.mean_var = sb(tag + "mean_var", [P, batches, 2], F32)
        self.var_eps = sb(tag + "var_eps", [P, batches], F32)
        self.rstd = sb(tag + "rstd", [P, batches], F32)
        self.shift = sb(tag + "shift", [P, batches], F32)
        self.normed = sb(tag + "normed", [P, 2, features], F32)
        self.stats_done = sem(tag + "stats_done")
        self.mean_done = sem(tag + "mean_done")
        self.var_done = sem(tag + "var_done")
        self.rstd_done = sem(tag + "rstd_done")
        self.shift_done = sem(tag + "shift_done")
        self.norm_done = sem(tag + "norm_done")
        self.turned = sem(tag + "turned")
        self.hi_done = sem(tag + "hi_done")
        self.lo_done = sem(tag + "lo_done")

    def statistics(self, dve, q):
        for b in range(4 * q, 4 * q + 4):
            dve.bn_stats(self.stats[:, b, :], self.x[:, b, :]).then_inc(self.stats_done, 1)

    def variances(self, dve, q):
        for b in range(4 * q, 4 * q + 4):
            dve.bn_aggr(self.mean_var[:, b, :], self.stats[:, b, :]).then_inc(self.mean_done, 1)
        dve.wait_ge(self.mean_done, 4 * q + 4)
        dve.tensor_scalar(self.var_eps[:, 4 * q:4 * q + 4], self.mean_var[:, 4 * q:4 * q + 4, 1], EPS_LN, None,
                          ALU.add).then_inc(self.var_done, 1)

    def pool(self, pool, q):
        pool.wait_ge(self.var_done, q + 1)
        pool.tensor_tensor(self.rstd[:, 4 * q:4 * q + 4], self.var_eps[:, 4 * q:4 * q + 4],
                           self.minus_half[:, :].to_broadcast([P, 4]), ALU.pow).then_inc(self.rstd_done, 1)

    def scalar(self, act, q, psum, normalise=False):
        for b in range(4 * q, 4 * q + 5):
            if normalise and b < 4 * q + 4:
                act.wait_ge(self.shift_done, q)
                act.wait_ge(self.turned, b if b % 4 == 0 else b - 1)
                act.activation(self.normed[:, b % 2, :], self.x[:, b, :], ACT.Identity, bias=self.shift[:, b:b + 1],
                               scale=self.rstd[:, b:b + 1]).then_inc(self.norm_done, 1)
            if b > 4 * q:
                act.wait_ge(self.turned, b)
                act.activation(self.cols[0][:, :, (b - 1) * P:b * P], psum[:, (b - 1) % 2, :, :],
                               ACT.Copy).then_inc(self.hi_done, 1)

    def tensor(self, pe, q, psum, batches=range(4)):
        for b in [4 * q + i for i in batches]:
            pe.wait_ge(self.norm_done, b + 1)
            if b >= 2:
                pe.wait_ge(self.lo_done, b - 1)
            for k in range(self.kt):
                mm = pe.transpose(psum[:, b % 2, k, :], self.normed[:, b % 2, k * P:(k + 1) * P], self.ident[:, :])
            mm.then_inc(self.turned, 1)

    def factors(self, dve, q):
        at = slice(4 * q, 4 * q + 4)
        dve.wait_ge(self.rstd_done, q + 1)
        dve.scalar_tensor_tensor(self.shift[:, at], self.mean_var[:, at, 0], -1.0, self.rstd[:, at], ALU.mult,
                                 ALU.mult).then_inc(self.shift_done, 1)

    def vector(self, dve, q, psum, normalise):
        for b in range(4 * q, 4 * q + 5):
            if normalise and b < 4 * q + 4:
                dve.wait_ge(self.rstd_done, q + 1)
                if b >= 2:
                    dve.wait_ge(self.turned, b - 1)
                dve.tensor_scalar(self.normed[:, b % 2, :], self.x[:, b, :], self.mean_var[:, b, 0:1],
                                  self.rstd[:, b:b + 1], ALU.subtract, ALU.mult).then_inc(self.norm_done, 1)
            if b > 4 * q:
                at = slice(None), slice(None), slice((b - 1) * P, b * P)
                dve.wait_ge(self.hi_done, b)
                dve.tensor_tensor(self.cols[1][at], psum[:, (b - 1) % 2, :, :], self.cols[0].bitcast(F32)[at],
                                  ALU.subtract).then_inc(self.lo_done, 1)


def linear_attention(nc, x, stats, ident, ones, minus_half, x_dram, Wq, Wk, Wv, Wo, bo):
    D, INNER = Wq.shape
    KT = D // P
    NB = x.shape[1]
    HD = 64
    GW = 256
    GROUPS = INNER // GW
    HG, PAIRS = GW // HD, GW // P
    AUG = HD + 1
    with ExitStack() as ctx:
        sb = lambda n, s, d: ctx.enter_context(nc.sbuf_tensor("a_" + n, s, d))
        ps = lambda n, s, d: ctx.enter_context(nc.psum_tensor("a_" + n, s, d))
        sem = lambda n: ctx.enter_context(nc.semaphore("a_" + n))

        h_cols = [sb(f"h_cols{s}", [P, KT, NB * P], F32R) for s in "hl"]
        wq_raw = sb("wq_raw", [P, KT, GW], F32)
        wkv_raw = sb("wkv_raw", [P, KT, 2, GW], F32)
        wo_raw = sb("wo_raw", [P, PAIRS, D], F32)
        wq = [[sb(f"wq{g}{s}", [P, KT, GW], F32R) for s in "hl"] for g in range(2)]
        wkv = [[sb(f"wkv{g}{s}", [P, KT, 2 * GW], F32R) for s in "hl"] for g in range(2)]
        wo = [[sb(f"wo{g}{s}", [P, PAIRS, D], F32R) for s in "hl"] for g in range(2)]
        q_cols = [sb(f"q_cols{i}", [P, PAIRS, 4 * P], F32) for i in range(2)]
        k_rows = [sb(f"k_rows{i}", [P, GW], F32) for i in range(2)]
        v_rows = [sb(f"v_rows{i}", [P, HG, AUG], F32) for i in range(2)]
        kv_diag = [sb(f"kv_diag{i}", [P, PAIRS, 2 * AUG], F32) for i in range(2)]
        denom = [sb(f"denom{i}", [P, HG, 1], F32) for i in range(2)]
        inv = [sb(f"inv{i}", [P, HG, 1], F32) for i in range(2)]
        o_rows = [sb(f"o_rows{i}", [P, HG, HD], F32) for i in range(2)]
        o_cols = [[sb(f"o_cols{i}{s}", [P, PAIRS, P], F32R) for s in "hl"] for i in range(2)]
        bias = sb("bias", [P, D], F32)

        q_ps = ps("q_ps", [P, 2, 512], F32)
        kv_ps = ps("kv_ps", [P, 2, 512], F32)
        kvm_ps = ps("kvm_ps", [P, 512], F32)
        num_ps = ps("num_ps", [P, 512], F32)
        last_ps = ps("last_ps", [P, 2, 512], F32)
        turn_ps, y_ps = last_ps[:, 0, :], last_ps[:, 1, :]
        ln_ps = [t[:, :, :].rearrange("p h (k t) -> p h k t", k=KT) for t in (q_ps, last_ps, last_ps, last_ps)]
        num_heads = num_ps[:, 0:HG * AUG].rearrange("p (h e) -> p h e", h=HG)

        ln = LayerNorm(sb, sem, "ln_", x, stats, h_cols, ident, minus_half)

        x_in = [sem(f"x_in{q}") for q in range(4)]
        bias_in, raw_in = sem("bias_in"), sem("raw_in")
        first_q_in, first_kv_in, first_o_in = sem("first_q_in"), sem("first_kv_in"), sem("first_o_in")
        first_hi = sem("first_hi")
        ones_set, zeros_set = sem("ones_set"), sem("zeros_set")
        hi_split, weights_ready = sem("hi_split"), sem("weights_ready")
        bias_added = sem("bias_added")
        q_done, q_copied = sem("q_done"), sem("q_copied")
        kv_done, kv_copied = sem("kv_done"), sem("kv_copied")
        kvm_done, kvm_placed = sem("kvm_done"), sem("kvm_placed")
        num_done = sem("num_done")
        den_clipped, den_inverted, o_scaled = sem("den_clipped"), sem("den_inverted"), sem("o_scaled")
        o_turned, o_hi, o_lo = sem("o_turned"), sem("o_hi"), sem("o_lo")
        y_done, y_added = sem("y_done"), sem("y_added")

        STEPS = 2 * NB
        split_parts = [((wq_raw[:, :, :], wq[i]), (wkv_raw[:, :, :, :].rearrange("p k a n -> p k (a n)"), wkv[i]),
                        (wo_raw[:, :, :], wo[i])) for i in range(2)]
        block = ctx.enter_context(nc.Block())

        @block.sync
        def _(sp):
            def load_x(q):
                sp.dma_start(x[:, 4 * q:4 * q + 4, :],
                             x_dram[4 * q:4 * q + 4].rearrange("b t d -> t b d")).then_inc(x_in[q], 16)

            def load_qkv(g, q_arrived, kv_arrived):
                for raw, W, arrived in ((wq_raw[:, :, :], Wq, q_arrived), (wkv_raw[:, :, 0, :], Wk, kv_arrived),
                                        (wkv_raw[:, :, 1, :], Wv, kv_arrived)):
                    sp.dma_start(raw, W.rearrange("(k p) n -> p k n", p=P)[:, :, bass.ds(g * GW, GW)])\
                        .then_inc(arrived, 16)

            def load_o(g, arrived):
                sp.dma_start(wo_raw[:, :, :], Wo.rearrange("(g j p) n -> g p j n", j=PAIRS, p=P)
                             [bass.ds(g, 1)].rearrange("g p j n -> (g p) j n")).then_inc(arrived, 16)

            load_x(0)
            load_qkv(0, first_q_in, first_kv_in)
            load_x(1)
            load_x(2)
            load_x(3)
            load_o(0, first_o_in)
            sp.dma_start(bias[:, :], bo.rearrange("(a d) -> a d", a=1).to_broadcast([P, D])).then_inc(bias_in, 16)
            with sp.Fori(1, GROUPS) as g:
                sp.wait_ge(weights_ready, done(g * 3 - 1))
                load_qkv(g, raw_in, raw_in)
                load_o(g, raw_in)

        @block.gpsimd
        def _(pool):
            start(pool, hi_split)
            for i in range(2):
                pool.memset(v_rows[i][:, :, HD:AUG], 1.0).then_inc(ones_set, 1)
            for i in range(2):
                pool.memset(kv_diag[i][:, :, :], 0.0).then_inc(zeros_set, 1)
            for q in range(4):
                ln.pool(pool, q)
            pool.wait_ge(bias_in, 16)
            for b in range(NB):
                pool.wait_ge(ln.norm_done, b + 1)
                pool.tensor_tensor(x[:, b, :], x[:, b, :], bias[:, :], ALU.add).then_inc(bias_added, 1)

            def split_group(g, gg):
                pool.wait_ge(raw_in, g * 64)
                pool.wait_ge(y_done, done((g - 2) * NB + NB - 1))
                for n, (raw, w) in enumerate(split_parts[gg]):
                    pool.tensor_tensor(w[0][:, :, :], raw, ones[:, :].unsqueeze(2).to_broadcast(list(raw.shape)), ALU.mult)\
                        .then_inc(hi_split, 1)
                for n, (raw, w) in enumerate(split_parts[gg]):
                    pool.wait_ge(hi_split, done((g - 1) * 3 + n))
                    pool.tensor_tensor(w[1][:, :, :], raw, w[0][:, :, :].bitcast(F32), ALU.subtract)\
                        .then_inc(weights_ready, 1)

            split_group(1, 1)
            with pool.Fori(1, GROUPS // 2) as it:
                for gg in range(2):
                    split_group(it * 2 + gg, gg)

        @block.scalar
        def _(act):
            start(act, q_copied, kv_copied, o_hi)

            def first_high(n):
                raw, w = split_parts[0][n]
                act.activation(w[0][:, :, :], raw, ACT.Copy).then_inc(first_hi, 1)

            act.wait_ge(first_q_in, 16)
            first_high(0)
            ln.scalar(act, 0, ln_ps[0])
            act.wait_ge(first_kv_in, 32)
            first_high(1)
            act.wait_ge(ones_set, 2)

            def steps(it, first):
                n0 = it * STEPS
                for s in range(STEPS + 3):
                    if s % 4 == 0 and s < STEPS:
                        blk = it * (STEPS // 4) + s // 4
                        act.wait_ge(num_done, done(blk * 4 - 5))
                        for f in range(PAIRS):
                            act.wait_ge(q_done, done(blk * 2 + f))
                            act.activation(q_cols[s // 4 % 2][:, f, :], q_ps[:, f, :], ACT.Relu)\
                                .then_inc(q_copied, 1)
                    if s < STEPS:
                        p = s % 2
                        act.wait_ge(kv_done, done(n0 + s))
                        act.wait_ge(kvm_done, done(n0 + s - 2))
                        act.activation(k_rows[p][:, :], kv_ps[:, p, 0:GW], ACT.Relu)
                        act.activation(v_rows[p][:, :, 0:HD],
                                       kv_ps[:, p, GW:2 * GW].rearrange("p (h e) -> p h e", h=HG),
                                       ACT.Copy).then_inc(kv_copied, 1)
                    if first and s < 3:
                        ln.scalar(act, s + 1, ln_ps[s + 1], normalise=True)
                    if first and s == 2:
                        act.wait_ge(first_o_in, 16)
                        first_high(2)
                    if s >= 3:
                        p = (s - 3) % 2
                        act.wait_ge(o_turned, done(n0 + s - 3))
                        act.wait_ge(y_done, done(n0 + s - 5))
                        act.activation(o_cols[p][0][:, :, :],
                                       turn_ps[:, 0:GW].rearrange("p (j t) -> p j t", j=PAIRS),
                                       ACT.Copy).then_inc(o_hi, 1)

            steps(0, True)
            with act.Fori(1, GROUPS // 2) as it:
                steps(it, False)

        @block.tensor
        def _(pe):
            start(pe, q_done, kv_done, kvm_done, num_done, o_turned, y_done)
            ln.tensor(pe, 0, ln_ps[0])
            pe.wait_ge(ln.lo_done, 4)

            def steps(it, first):
                n0 = it * STEPS
                for s in range(STEPS + 4):
                    if s % NB == 0 and s < STEPS:
                        pe.wait_ge(weights_ready, done((it * 2 + s // NB) * 3))
                    if first and s % 4 == 0 and s < NB:
                        pe.wait_ge(ln.lo_done, s + 4)
                    if s % 4 == 0 and s < STEPS:
                        w, blk, tok = wq[s // NB], it * (STEPS // 4) + s // 4, s % NB * P
                        pe.wait_ge(q_copied, done(blk * 2 - 1))
                        for f in range(PAIRS):
                            for k in range(KT):
                                mm = matmul_split(pe, q_ps[:, f, :], [w[i][:, k, f * P:(f + 1) * P] for i in range(2)],
                                                  [h_cols[i][:, k, tok:tok + 4 * P] for i in range(2)], k == 0, k == KT - 1)
                            mm.then_inc(q_done, 1)
                    if s < STEPS:
                        w, tok = wkv[s // NB], s % NB * P
                        if s % NB == 0:
                            pe.wait_ge(weights_ready, done((it * 2 + s // NB) * 3 + 1))
                        pe.wait_ge(kv_copied, done(n0 + s - 2))
                        for k in range(KT):
                            mm = matmul_split(pe, kv_ps[:, s % 2, :], [h_cols[i][:, k, tok:tok + P] for i in range(2)],
                                              [w[i][:, k, :] for i in range(2)], k == 0, k == KT - 1)
                        mm.then_inc(kv_done, 1)
                    if 1 <= s < STEPS + 1:
                        n, p = n0 + s - 1, (s - 1) % 2
                        pe.wait_ge(kv_copied, done(n))
                        pe.wait_ge(kvm_placed, done(n - 1))
                        for h in range(HG):
                            mm = pe.matmul(kvm_ps[HD * (h % 2):HD * (h % 2 + 1), h // 2 * AUG:(h // 2 + 1) * AUG],
                                           k_rows[p][:, h * HD:(h + 1) * HD], v_rows[p][:, h, :], start=True, stop=True)
                        mm.then_inc(kvm_done, 1)
                    if 2 <= s < STEPS + 2:
                        n, p, sl = n0 + s - 2, (s - 2) % 2, s - 2
                        pe.wait_ge(kvm_placed, done(n))
                        pe.wait_ge(q_copied, done((it * (STEPS // 4) + sl // 4) * 2 + 1))
                        pe.wait_ge(o_scaled, done(n - 1))
                        for j in range(PAIRS):
                            mm = pe.matmul(num_ps[:, j * 2 * AUG:(j + 1) * 2 * AUG],
                                           q_cols[sl // 4 % 2][:, j, sl % 4 * P:(sl % 4 + 1) * P],
                                           kv_diag[p][:, j, :], start=True, stop=True)
                        mm.then_inc(num_done, 1)
                    if first and s < 3:
                        ln.tensor(pe, s + 1, ln_ps[s + 1])
                    if first and s == 3:
                        pe.wait_ge(ln.lo_done, NB)
                    if 3 <= s < STEPS + 3:
                        n, p = n0 + s - 3, (s - 3) % 2
                        pe.wait_ge(o_scaled, done(n))
                        pe.wait_ge(o_lo, done(n - 1))
                        for j in range(PAIRS):
                            mm = pe.transpose(turn_ps[:, j * P:(j + 1) * P],
                                              o_rows[p][:, 2 * j:2 * j + 2, :].rearrange("p h e -> p (h e)"), ident[:, :])
                        mm.then_inc(o_turned, 1)
                    if s >= 4:
                        n, p, w = n0 + s - 4, (s - 4) % 2, wo[(s - 4) // NB]
                        if (s - 4) % NB == 0:
                            pe.wait_ge(weights_ready, done((it * 2 + (s - 4) // NB) * 3 + 2))
                        pe.wait_ge(o_lo, done(n))
                        pe.wait_ge(y_added, done(n - 1))
                        for j in range(PAIRS):
                            mm = matmul_split(pe, y_ps[:, :], [o_cols[p][i][:, j, :] for i in range(2)],
                                              [w[i][:, j, :] for i in range(2)], j == 0, j == PAIRS - 1)
                        mm.then_inc(y_done, 1)

            steps(0, True)
            with pe.Fori(1, GROUPS // 2) as it:
                steps(it, False)

        @block.vector
        def _(dve):
            start(dve, kvm_placed, den_clipped, den_inverted, o_scaled, o_lo, y_added, weights_ready)

            def measure(q):
                dve.wait_ge(x_in[q], 16)
                ln.statistics(dve, q)
                dve.wait_ge(ln.stats_done, 4 * q + 4)
                ln.variances(dve, q)

            def first_low(n):
                raw, w = split_parts[0][n]
                dve.wait_ge(first_hi, n + 1)
                dve.tensor_tensor(w[1][:, :, :], raw, w[0][:, :, :].bitcast(F32), ALU.subtract).then_inc(weights_ready, 1)

            measure(0)
            first_low(0)
            ln.vector(dve, 0, ln_ps[0], normalise=True)
            first_low(1)
            measure(1)
            dve.wait_ge(zeros_set, 2)
            ln.factors(dve, 1)

            def steps(it, first):
                n0 = it * STEPS
                for s in range(1, STEPS + 5):
                    if first and s < 4:
                        if s < 3:
                            measure(s + 1)
                        ln.vector(dve, s, ln_ps[s], normalise=False)
                        if s < 3:
                            ln.factors(dve, s + 1)
                        else:
                            first_low(2)
                    if s < STEPS + 1:
                        n, p = n0 + s - 1, (s - 1) % 2
                        dve.wait_ge(kvm_done, done(n))
                        dve.wait_ge(num_done, done(n - 2))
                        for e in range(2):
                            at = slice(HD * e, HD * (e + 1))
                            ins = dve.tensor_copy(kv_diag[p][at, :, AUG * e:AUG * (e + 1)],
                                                  kvm_ps[at, 0:PAIRS * AUG].rearrange("p (j e) -> p j e", j=PAIRS))
                        ins.then_inc(kvm_placed, 1)
                    if 2 <= s < STEPS + 2:
                        n, p = n0 + s - 2, (s - 2) % 2
                        dve.wait_ge(num_done, done(n))
                        dve.tensor_scalar(denom[p][:, :, :], num_heads[:, :, HD:AUG], 1e-6, None,
                                          ALU.max).then_inc(den_clipped, 1)
                        dve.wait_ge(den_clipped, done(n))
                        dve.reciprocal(inv[p][:, :, :], denom[p][:, :, :]).then_inc(den_inverted, 1)
                        dve.wait_ge(den_inverted, done(n))
                        dve.wait_ge(o_turned, done(n - 2))
                        dve.tensor_tensor(o_rows[p][:, :, :], num_heads[:, :, 0:HD],
                                          inv[p][:, :, :].to_broadcast([P, HG, HD]), ALU.mult).then_inc(o_scaled, 1)
                    if 3 <= s < STEPS + 3:
                        n, p = n0 + s - 3, (s - 3) % 2
                        dve.wait_ge(o_hi, done(n))
                        dve.tensor_tensor(o_cols[p][1][:, :, :], turn_ps[:, 0:GW].rearrange("p (j t) -> p j t", j=PAIRS),
                                          o_cols[p][0][:, :, :].bitcast(F32), ALU.subtract).then_inc(o_lo, 1)
                    if s >= 4 and s - 4 < STEPS:
                        n, b = n0 + s - 4, (s - 4) % NB
                        if first and s - 4 < NB:
                            dve.wait_ge(bias_added, b + 1)
                        dve.wait_ge(y_done, done(n))
                        dve.tensor_tensor(x[:, b, :], x[:, b, :], y_ps[:, :], ALU.add).then_inc(y_added, 1)

            steps(0, True)
            with dve.Fori(1, GROUPS // 2) as it:
                steps(it, False)
            dve.wait_ge(y_added, done(NB * GROUPS - 1))


PROJECT, TURN, ATTEND, FINISH, NEXT = range(5)


class CrossAttention:

    def __init__(self, nc, ctx, x, stats, ident, minus_half, ctx_dram, pos, Wq, Wkv, Wout, bout):
        sb = lambda n, s, d: ctx.enter_context(nc.sbuf_tensor("b_" + n, s, d))
        ps = lambda n, s, d: ctx.enter_context(nc.psum_tensor("b_" + n, s, d))
        sem = lambda n: ctx.enter_context(nc.semaphore("b_" + n))
        self.nc, self.x, self.stats, self.ident, self.minus_half = nc, x, stats, ident, minus_half
        self.ctx_dram, self.pos_dram, self.Wq, self.Wkv, self.Wout, self.bout = ctx_dram, pos, Wq, Wkv, Wout, bout
        D = self.D = Wq.shape[0]
        self.KT, self.CT = D // P, Wkv.shape[0] // P
        self.NB = x.shape[1]
        self.H, self.HD = 32, 16
        self.CONSTS = 12
        self.SLOT = 64
        KT, CT, NB, H, HD, SLOT = self.KT, self.CT, self.NB, self.H, self.HD, self.SLOT

        self.wq = [sb(f"wq{s}", [P, KT, D], F32R) for s in "hl"]
        self.wkv = [sb(f"wkv{s}", [P, CT, 2 * D], F32R) for s in "hl"]
        self.wo = [sb(f"wo{s}", [P, KT, D], F32R) for s in "hl"]
        self.bias = sb("bias", [P, D], F32)
        self.pos = sb("pos", [P, NB, 2], F32)
        self.half_pi = sb("half_pi", [P, 1], F32)
        self.angle = sb("angle", [P, NB, 2, 4], F32)
        self.turns = sb("turns", [P, NB, 2, 4], F32)
        self.tables = sb("tables", [P, NB, 2, 2, 4, 2], F32)
        self.cos, self.sin = self.tables[:, :, 0, :, :, :], self.tables[:, :, 1, :, :, :]
        self.tables_now = sb("tables_now", [P, 2, HD], F32)
        self.mean_var = sb("mean_var", [P, NB, 2], F32)
        self.var_eps = sb("var_eps", [P, NB], F32)
        self.rstd = sb("rstd", [P, NB], F32)
        self.normed = sb("normed", [P, D], F32)
        self.x_cols = [sb(f"x_cols{s}", [P, KT, P], F32R) for s in "hl"]
        self.ctx_rows = [sb(f"ctx_rows{i}", [P, CT * P], F32) for i in range(2)]
        self.ctx_cols = [sb(f"ctx_cols{s}", [P, CT, P], F32R) for s in "hl"]
        work = sb("work", [P, 12, D], F32)
        self.raw = [work[:, 0:4, :], work[:, 4:8, :].rearrange("p (k a) n -> p k (a n)", k=CT), work[:, 8:12, :]]
        self.rows = {"q": work[:, 0, :], "k": work[:, 1, :]}
        self.by_cos, self.by_sin = work[:, 2, :], work[:, 3, :]
        self.rotated = {"q": work[:, 4, :], "k": work[:, 5, :]}
        self.probs = [work[:, 6 + 2 * i:8 + 2 * i, :].rearrange("p a (h t) -> p (a h) t", t=P) for i in range(2)]
        self.o_cols = work[:, 10:12, :].rearrange("p a (g t) -> p (a g) t", t=P)
        self.slots = {w: sb(f"{w}_slots", [P, H, SLOT], F32R) for w in "qk"}
        self.q_cols = [sb(f"q_cols{i}", [P, H // 2, P], F32R) for i in range(2)]
        self.k_cols = [sb(f"k_cols{i}", [P, H // 2, 2, P], F32R) for i in range(2)]
        self.values = [sb(f"values{i}", [P, H, 32], F32) for i in range(2)]
        self.row_max = sb("row_max", [P, 8], F32)
        self.max_rows = sb("max_rows", [P, P], BF16)
        self.max_cols = sb("max_cols", [P, P], BF16)
        self.minus = sb("minus", [P, 8], F32)
        self.minus_head = sb("minus_head", [P, 8, P], BF16)
        self.ident16 = sb("ident16", [P, P], BF16)
        self.ident_r = sb("ident_r", [P, P], F32R)
        self.inv_sum = sb("inv_sum", [P, H, 1], F32)
        self.attn = sb("attn", [P, H, HD], F32)
        self.attn_cols = [sb(f"attn_cols{s}", [P, KT, P], F32R) for s in "hl"]

        self.ps_x = ps("ps_x", [P, 512], F32)
        self.ps_c = ps("ps_c", [P, 512], F32)
        self.ps_l = ps("ps_l", [P, 8, P], F32)
        self.ps_t = ps("ps_t", [P, 8, P], F32)
        self.ps_o = ps("ps_o", [P, H // 4, P], F32)
        self.out_heads = self.ps_o[:, :, :].rearrange("p g (h e) -> p (g h) e", e=32)

        self.w_in = [sem(f"w_in{i}") for i in range(3)]
        self.pos_in, self.bias_in = sem("pos_in"), sem("bias_in")
        self.ctx_in = [sem(f"ctx_in{i}") for i in range(2)]
        self.const_set = sem("const_set")
        self.minus_made = sem("minus_made")
        self.w_hi = sem("w_hi")
        self.w_lo = sem("w_lo")
        self.angle_step = sem("angle_step")
        self.trig = sem("trig")
        self.trig_signed = sem("trig_signed")
        self.stats_done = sem("stats_done")
        self.mean_done = sem("mean_done")
        self.var_done = sem("var_done")
        self.rstd_done = sem("rstd_done")
        self.normed_done = sem("normed_done")
        self.tables_copied = sem("tables_copied")
        self.ctx_turned = sem("ctx_turned")
        self.ctx_hi = sem("ctx_hi")
        self.ctx_lo = sem("ctx_lo")
        self.x_turned = sem("x_turned")
        self.x_hi = sem("x_hi")
        self.x_lo = sem("x_lo")
        self.k_done = sem("k_done")
        self.k_copied = sem("k_copied")
        self.v_done = sem("v_done")
        self.v_copied = sem("v_copied")
        self.q_done = sem("q_done")
        self.q_copied = sem("q_copied")
        self.rope_parts = sem("rope_parts")
        self.k_rotated = sem("k_rotated")
        self.q_rotated = sem("q_rotated")
        self.k_hi = sem("k_hi")
        self.k_lo = sem("k_lo")
        self.q_hi = sem("q_hi")
        self.q_lo = sem("q_lo")
        self.k_turned = sem("k_turned")
        self.even_copied = sem("even_copied")
        self.odd_copied = sem("odd_copied")
        self.q_turned = sem("q_turned")
        self.q_cols_done = sem("q_cols_done")
        self.biased = sem("biased")
        self.logits_done = sem("logits_done")
        self.maxed = sem("maxed")
        self.o_copied = sem("o_copied")
        self.o_turned = sem("o_turned")
        self.ident_made = sem("ident_made")
        self.max_hi = sem("max_hi")
        self.max_lo = sem("max_lo")
        self.max_turned = sem("max_turned")
        self.max_copied = sem("max_copied")
        self.logits_t_done = sem("logits_t_done")
        self.exp_done = sem("exp_done")
        self.values_done = sem("values_done")
        self.inverted = sem("inverted")
        self.scaled = sem("scaled")
        self.attn_turned = sem("attn_turned")
        self.attn_hi = sem("attn_hi")
        self.attn_lo = sem("attn_lo")
        self.out_done = sem("out_done")
        self.added = sem("added")
        self.measured = sem("measured")

    def turn_ctx(self, pe, m, p):
        pe.wait_ge(self.ctx_in[p], (m // 2 + 1) * 16 if isinstance(m, int) else (m + 2 - p) * 8)
        pe.wait_ge(self.v_copied, done(m - 1))
        for k in range(self.CT):
            mm = pe.transpose(self.ps_c[:, k * P:(k + 1) * P], self.ctx_rows[p][:, k * P:(k + 1) * P], self.ident[:, :])
        mm.then_inc(self.ctx_turned, 1)

    def project_k(self, pe, m):
        pe.wait_ge(self.ctx_lo, done(m))
        for k in range(self.CT):
            mm = matmul_split(pe, self.ps_c[:, :], [c[:, k, :] for c in self.ctx_cols],
                              [w[:, k, 0:self.D] for w in self.wkv], k == 0, k == self.CT - 1)
        mm.then_inc(self.k_done, 1)

    def project_v(self, pe, m):
        pe.wait_ge(self.k_copied, done(m))
        pe.wait_ge(self.even_copied, done(4 * m - 1))
        pe.wait_ge(self.odd_copied, done(4 * m - 1))
        for k in range(self.CT):
            mm = matmul_split(pe, self.ps_c[:, :], [c[:, k, :] for c in self.ctx_cols],
                              [w[:, k, self.D:2 * self.D] for w in self.wkv], k == 0, k == self.CT - 1)
        mm.then_inc(self.v_done, 1)

    def turn_x(self, pe, m):
        pe.wait_ge(self.normed_done, done(m))
        pe.wait_ge(self.added, done(m - 4))
        pe.wait_ge(self.q_cols_done, done(4 * m - 5))
        pe.wait_ge(self.q_copied, done(m - 1))
        for k in range(self.KT):
            mm = pe.transpose(self.ps_x[:, k * P:(k + 1) * P], self.normed[:, k * P:(k + 1) * P], self.ident[:, :])
        mm.then_inc(self.x_turned, 1)

    def project_q(self, pe, m):
        pe.wait_ge(self.x_lo, done(m))
        for k in range(self.KT):
            mm = matmul_split(pe, self.ps_x[:, :], [c[:, k, :] for c in self.x_cols],
                              [w[:, k, :] for w in self.wq], k == 0, k == self.KT - 1)
        mm.then_inc(self.q_done, 1)

    def turn_k(self, pe, m, j, projected):
        pe.wait_ge(self.k_lo, done(m))
        if j > 0:
            pe.wait_ge(self.even_copied, done(4 * m + j - 1))
            pe.wait_ge(self.odd_copied, done(4 * m + j - 1))
        elif projected:
            pe.wait_ge(self.k_copied, done(m + 1))
        else:
            pe.wait_ge(self.v_copied, done(m))
        self.turn_slots(pe, "k", self.ps_c, j).then_inc(self.k_turned, 1)

    def turn_q(self, pe, m, j, projected, finished):
        pe.wait_ge(self.q_lo, done(m))
        if j > 0:
            pe.wait_ge(self.q_cols_done, done(4 * m + j - 1))
        elif finished:
            pe.wait_ge(self.attn_lo, done(m - 2))
        elif projected:
            pe.wait_ge(self.q_copied, done(m + 1))
        self.turn_slots(pe, "q", self.ps_x, j).then_inc(self.q_turned, 1)

    def turn_slots(self, pe, which, into, j):
        for i in range(4):
            t = 4 * j + i
            mm = pe.transpose(into[:, i * P:(i + 1) * P].bitcast(F32R),
                              self.slots[which][:, 2 * t:2 * t + 2, :].rearrange("p h s -> p (h s)"), self.ident_r[:, :])
        return mm

    def logits(self, pe, b, p, c):
        n = 4 * b + c
        pe.wait_ge(self.q_cols_done, done(n))
        pe.wait_ge(self.even_copied, done(n))
        pe.wait_ge(self.odd_copied, done(n))
        pe.wait_ge(self.maxed, done(n - 1))
        for i in range(4):
            t = 4 * c + i
            mm = pe.matmul(self.ps_l[:, 2 * i:2 * i + 2, :].rearrange("p r k -> p (r k)"), self.q_cols[p][:, t, :],
                           self.k_cols[p][:, t, :, :].rearrange("p r k -> p (r k)"), start=True, stop=True)
        mm.then_inc(self.logits_done, 1)

    def turn_max(self, pe, b, c):
        pe.wait_ge(self.max_lo, done(4 * b + c))
        pe.wait_ge(self.exp_done, done(4 * b + c - 1))
        pe.transpose(self.ps_t[:, 0, 0:P // 2].bitcast(BF16), self.max_rows[:, :], self.ident16[:, :])\
            .then_inc(self.max_turned, 1)

    def logits_t(self, pe, b, p, c):
        n = 4 * b + c
        for h in (4, 5, 6, 7, 0, 1, 2, 3):
            if h == 0:
                pe.wait_ge(self.max_copied, done(n))
            pe.matmul(self.ps_t[:, h, :], self.k_cols[p][:, 4 * c + h // 2, h % 2, :],
                      self.q_cols[p][:, 4 * c + h // 2, :], start=h % 4 == 0, stop=False)
        for h in range(8):
            mm = pe.matmul(self.ps_t[:, h, :], self.minus_head[:, h, :], self.max_cols[:, :], start=False,
                           stop=h % 4 == 3)
        mm.then_inc(self.logits_t_done, 1)

    def weigh_values(self, pe, b, p, c):
        n = 4 * b + c
        pe.wait_ge(self.exp_done, done(n))
        pe.wait_ge(self.v_copied, done(b))
        pe.wait_ge(self.scaled, done(b - 1))
        for h in range(8):
            j = h % 4
            mm = pe.matmul(self.ps_o[32 * j:32 * j + 32, 2 * c + h // 4, :], self.values[p][:, 8 * c + h, :],
                           self.probs[c % 2][:, h, :], start=True, stop=True)
        mm.then_inc(self.values_done, 1)

    def turn_out(self, pe, n):
        pe.wait_ge(self.o_copied, done(n))
        for g in range(self.H // 4):
            mm = pe.transpose(self.ps_o[:, g, :], self.o_cols[:, g, :], self.ident[:, :])
        mm.then_inc(self.o_turned, 1)

    def turn_attn(self, pe, n, projected):
        pe.wait_ge(self.scaled, done(n))
        if projected:
            pe.wait_ge(self.q_copied, done(n + 3))
        else:
            pe.wait_ge(self.added, done(n - 1))
        rows = self.attn[:, :, :].rearrange("p h e -> p (h e)")
        for k in range(self.KT):
            mm = pe.transpose(self.ps_x[:, k * P:(k + 1) * P], rows[:, k * P:(k + 1) * P], self.ident[:, :])
        mm.then_inc(self.attn_turned, 1)

    def project_out(self, pe, n, turned, half):
        if half == 0:
            pe.wait_ge(self.attn_lo, done(n))
            if turned:
                pe.wait_ge(self.q_cols_done, done(4 * n + 11))
        tiles = self.KT // 2
        for k in range(tiles * half, tiles * (half + 1)):
            mm = matmul_split(pe, self.ps_x[:, :], [c[:, k, :] for c in self.attn_cols],
                              [w[:, k, :] for w in self.wo], k == 0, k == self.KT - 1)
        if half == 1:
            mm.then_inc(self.out_done, 1)

    def tensor_step(self, pe, b, p, stages):
        project, turn, attend, finish = [s in stages for s in (PROJECT, TURN, ATTEND, FINISH)]
        l, m, n = b + 2, b + 1, b - 1
        if attend:
            self.logits(pe, b, p, 1)
        if turn:
            self.project_v(pe, m)
        if project:
            self.turn_x(pe, l)
        if attend:
            self.turn_max(pe, b, 0)
        if finish:
            self.turn_out(pe, n)
        if attend:
            self.logits_t(pe, b, p, 0)
            self.logits(pe, b, p, 2)
        if project:
            self.turn_ctx(pe, l, p)
            if isinstance(b, int) and b == -2:
                pe.wait_ge(self.w_lo, 1)
            self.project_q(pe, l)
        if attend:
            self.turn_max(pe, b, 1)
            self.weigh_values(pe, b, p, 0)
        if finish:
            self.turn_attn(pe, n, project)
        if attend:
            self.logits_t(pe, b, p, 1)
            self.logits(pe, b, p, 3)
        if project:
            if isinstance(b, int) and b == -2:
                pe.wait_ge(self.w_lo, 2)
            self.project_k(pe, l)
        if attend:
            self.turn_max(pe, b, 2)
            self.weigh_values(pe, b, p, 1)
        if turn:
            self.turn_q(pe, m, 0, project, finish)
            self.turn_k(pe, m, 0, project)
        if attend:
            self.logits_t(pe, b, p, 2)
        if turn:
            self.turn_q(pe, m, 1, project, finish)
            self.turn_k(pe, m, 1, project)
            self.logits(pe, m, 1 - p, 0)
        if attend:
            self.turn_max(pe, b, 3)
            self.weigh_values(pe, b, p, 2)
        if turn:
            self.turn_q(pe, m, 2, project, finish)
        if attend:
            self.logits_t(pe, b, p, 3)
        if turn:
            self.turn_q(pe, m, 3, project, finish)
            self.turn_k(pe, m, 2, project)
        if finish:
            self.project_out(pe, n, turn, 0)
        if turn:
            self.turn_k(pe, m, 3, project)
        if attend:
            self.weigh_values(pe, b, p, 3)
        if finish:
            self.project_out(pe, n, turn, 1)

    def ctx_high(self, act, m):
        act.wait_ge(self.ctx_turned, done(m))
        act.wait_ge(self.v_done, done(m - 1))
        act.activation(self.ctx_cols[0][:, :, :], self.ps_c[:, 0:self.CT * P].rearrange("p (k t) -> p k t", k=self.CT),
                       ACT.Copy).then_inc(self.ctx_hi, 1)

    def x_high(self, act, m):
        act.wait_ge(self.x_turned, done(m))
        act.wait_ge(self.q_done, done(m - 1))
        act.activation(self.x_cols[0][:, :, :], self.ps_x[:, :].rearrange("p (k t) -> p k t", k=self.KT),
                       ACT.Copy).then_inc(self.x_hi, 1)

    def copy_k(self, act, m):
        act.wait_ge(self.k_done, done(m))
        act.wait_ge(self.k_rotated, done(m - 1))
        act.activation(self.rows["k"][:, :], self.ps_c[:, :], ACT.Copy).then_inc(self.k_copied, 1)

    def copy_v(self, act, m, p):
        act.wait_ge(self.v_done, done(m))
        act.wait_ge(self.values_done, done(4 * m - 5))
        act.activation(self.values[p][:, :, 0:self.HD], self.ps_c[:, :].rearrange("p (h e) -> p h e", h=self.H),
                       ACT.Copy).then_inc(self.v_copied, 1)

    def copy_q(self, act, m):
        act.wait_ge(self.q_done, done(m))
        act.wait_ge(self.q_rotated, done(m - 1))
        act.activation(self.rows["q"][:, :], self.ps_x[:, :], ACT.Copy).then_inc(self.q_copied, 1)

    def copy_q_cols(self, act, m, p, j):
        act.wait_ge(self.q_turned, done(4 * m + j))
        act.wait_ge(self.logits_t_done, done(4 * m - 5))
        act.activation(self.q_cols[p][:, 4 * j:4 * j + 4, :], self.ps_x[:, :].rearrange("p (i t) -> p i t", i=4),
                       ACT.Copy).then_inc(self.q_cols_done, 1)

    def copy_odd(self, act, m, p, j):
        act.wait_ge(self.k_turned, done(4 * m + j))
        act.wait_ge(self.logits_t_done, done(4 * m - 5))
        self.copy_block(act.activation, p, j, 1, ACT.Copy).then_inc(self.odd_copied, 1)

    def copy_block(self, copy, p, j, r, *how):
        at = slice(self.SLOT * r, self.SLOT * (r + 1))
        return copy(self.k_cols[p][at, 4 * j:4 * j + 4, r, :], self.ps_c[at, :].rearrange("p (i t) -> p i t", i=4), *how)

    def copy_max(self, act, b, c):
        act.wait_ge(self.max_turned, done(4 * b + c))
        act.wait_ge(self.logits_t_done, done(4 * b + c - 1))
        act.activation(self.max_cols[:, :], self.ps_t[:, 0, 0:P // 2].bitcast(BF16), ACT.Copy).then_inc(self.max_copied, 1)

    def exponential(self, act, b, c):
        n = 4 * b + c
        act.wait_ge(self.logits_t_done, done(n))
        act.wait_ge(self.values_done, done(n - 2))
        act.activation(self.probs[c % 2][:, :, :], self.ps_t[:, :, :], ACT.Exp, scale=1.0 / math.sqrt(self.HD))\
            .then_inc(self.exp_done, 1)

    def copy_out(self, act, b):
        act.wait_ge(self.values_done, done(4 * b + 3))
        act.wait_ge(self.o_turned, done(b - 1))
        act.activation(self.o_cols[:, :, :], self.ps_o[:, :, :], ACT.Copy).then_inc(self.o_copied, 1)

    def attn_high(self, act, n):
        act.wait_ge(self.attn_turned, done(n))
        act.wait_ge(self.out_done, done(n - 1))
        act.activation(self.attn_cols[0][:, :, :], self.ps_x[:, :].rearrange("p (k t) -> p k t", k=self.KT),
                       ACT.Copy).then_inc(self.attn_hi, 1)

    def weight_high(self, act, n):
        w = (self.wq, self.wkv, self.wo)[n]
        act.wait_ge(self.w_in[n], 16)
        act.activation(w[0][:, :, :], self.raw[n], ACT.Copy).then_inc(self.w_hi, 1)

    def trigonometry(self, act):
        act.wait_ge(self.const_set, self.CONSTS)
        act.wait_ge(self.angle_step, 10)
        act.activation(self.sin[:, :, :, :, 1], self.angle[:, :, :, :], ACT.Sin)
        act.activation(self.turns[:, :, :, :], self.angle[:, :, :, :], ACT.Abs).then_inc(self.trig, 1)
        act.wait_ge(self.trig, 1)
        for e in range(2):
            ins = act.activation(self.cos[:, :, :, :, e], self.turns[:, :, :, :], ACT.Sin, bias=self.half_pi[:, :],
                                 scale=-1.0)
        ins.then_inc(self.trig, 1)

    def scalar_step(self, act, b, p, stages):
        project, turn, attend, finish = [s in stages for s in (PROJECT, TURN, ATTEND, FINISH)]
        l, m, n = b + 2, b + 1, b - 1
        if finish:
            self.copy_out(act, n)
        if turn:
            self.copy_v(act, m, 1 - p)
        if project:
            self.x_high(act, l)
        if attend:
            self.copy_max(act, b, 0)
            self.exponential(act, b, 0)
        if project:
            self.ctx_high(act, l)
            if isinstance(b, int) and b == -2:
                self.weight_high(act, 1)
                self.trigonometry(act)
            self.copy_q(act, l)
        if attend:
            self.copy_max(act, b, 1)
        if finish:
            self.attn_high(act, n)
        if attend:
            self.exponential(act, b, 1)
        if project:
            self.copy_k(act, l)
        if attend:
            self.copy_max(act, b, 2)
        if turn:
            self.copy_q_cols(act, m, 1 - p, 0)
            self.copy_odd(act, m, 1 - p, 0)
        if attend:
            self.exponential(act, b, 2)
        if turn:
            self.copy_q_cols(act, m, 1 - p, 1)
            self.copy_odd(act, m, 1 - p, 1)
        if attend:
            self.copy_max(act, b, 3)
        if turn:
            self.copy_q_cols(act, m, 1 - p, 2)
            self.copy_q_cols(act, m, 1 - p, 3)
        if attend:
            self.exponential(act, b, 3)
        if turn:
            self.copy_odd(act, m, 1 - p, 2)
            self.copy_odd(act, m, 1 - p, 3)

    def normalise(self, dve, m):
        at = slice(m, m + 1) if isinstance(m, int) else bass.ds(m, 1)
        row = self.x[:, at, :].rearrange("p b d -> p (b d)")
        early = isinstance(m, int) and m < 4
        dve.wait_ge(self.rstd_done, 1 + m // 2 if early else 4)
        dve.wait_ge(self.x_turned, done(m - 1))
        dve.tensor_scalar(self.normed[:, :], row, self.mean_var[:, at, 0:1].rearrange("p b e -> p (b e)"),
                          self.rstd[:, at], ALU.subtract, ALU.mult).then_inc(self.normed_done, 1)

    def copy_tables(self, dve, m):
        at = slice(m, m + 1) if isinstance(m, int) else bass.ds(m, 1)
        dve.wait_ge(self.k_rotated, done(m - 1))
        dve.tensor_copy(self.tables_now[:, :, :], self.tables[:, at, :, :, :, :].rearrange("p b t a f e -> p (b t) (a f e)"))\
            .then_inc(self.tables_copied, 1)

    def ctx_low(self, dve, m):
        dve.wait_ge(self.ctx_hi, done(m))
        dve.tensor_tensor(self.ctx_cols[1][:, :, :], self.ps_c[:, 0:self.CT * P].rearrange("p (k t) -> p k t", k=self.CT),
                          self.ctx_cols[0][:, :, :].bitcast(F32), ALU.subtract).then_inc(self.ctx_lo, 1)

    def x_low(self, dve, m):
        dve.wait_ge(self.x_hi, done(m))
        dve.tensor_tensor(self.x_cols[1][:, :, :], self.ps_x[:, :].rearrange("p (k t) -> p k t", k=self.KT),
                          self.x_cols[0][:, :, :].bitcast(F32), ALU.subtract).then_inc(self.x_lo, 1)

    def fill_slots(self, dve, which, m):
        rot = self.rotated[which][:, :].rearrange("p (h e) -> p h e", h=self.H)
        slots, HD = self.slots[which], self.HD
        rotated, turned, hi_done, lo_done = ((self.k_rotated, self.k_turned, self.k_hi, self.k_lo) if which == "k" else
                                             (self.q_rotated, self.q_turned, self.q_hi, self.q_lo))
        dve.wait_ge(rotated, done(m))
        dve.wait_ge(turned, done(4 * m - 1))
        lo_at = 2 if which == "k" else 1
        hi_at = slots[:, :, 0:3 * HD].rearrange("p h (s e) -> p h s e", s=3)[:, :, 0:4 - lo_at:3 - lo_at, :]
        dve.tensor_copy(hi_at, rot.unsqueeze(2).to_broadcast([P, self.H, 2, HD])).then_inc(hi_done, 1)
        dve.wait_ge(hi_done, done(m))
        dve.tensor_tensor(slots[:, :, lo_at * HD:(lo_at + 1) * HD], rot, slots[:, :, 0:HD].bitcast(F32),
                          ALU.subtract).then_inc(lo_done, 1)

    def copy_even(self, dve, m, p, j):
        dve.wait_ge(self.k_turned, done(4 * m + j))
        dve.wait_ge(self.logits_t_done, done(4 * m - 5))
        self.copy_block(dve.tensor_copy, p, j, 0).then_inc(self.even_copied, 1)

    def maxima(self, dve, b, c):
        n = 4 * b + c
        dve.wait_ge(self.max_lo, done(n - 1))
        dve.wait_ge(self.logits_done, done(n))
        dve.tensor_reduce(self.row_max[:, :], self.ps_l[:, :, :], AX_X, ALU.max).then_inc(self.maxed, 1)
        dve.wait_ge(self.maxed, done(n))
        dve.wait_ge(self.max_turned, done(n - 1))
        dve.tensor_copy(self.max_rows[:, 0:8], self.row_max[:, :]).then_inc(self.max_hi, 1)
        dve.wait_ge(self.max_hi, done(n))
        dve.tensor_tensor(self.max_rows[:, 8:16], self.row_max[:, :], self.max_rows[:, 0:8], ALU.subtract)\
            .then_inc(self.max_lo, 1)

    def scale_heads(self, dve, b):
        dve.wait_ge(self.o_turned, done(b))
        dve.reciprocal(self.inv_sum[:, :, :], self.out_heads[:, :, self.HD:self.HD + 1]).then_inc(self.inverted, 1)
        dve.wait_ge(self.inverted, done(b))
        dve.wait_ge(self.attn_turned, done(b - 1))
        dve.tensor_tensor(self.attn[:, :, :], self.out_heads[:, :, 0:self.HD],
                          self.inv_sum[:, :, :].to_broadcast([P, self.H, self.HD]), ALU.mult).then_inc(self.scaled, 1)

    def attn_low(self, dve, n):
        dve.wait_ge(self.attn_hi, done(n))
        dve.tensor_tensor(self.attn_cols[1][:, :, :], self.ps_x[:, :].rearrange("p (k t) -> p k t", k=self.KT),
                          self.attn_cols[0][:, :, :].bitcast(F32), ALU.subtract).then_inc(self.attn_lo, 1)

    def add_output(self, dve, n):
        at = slice(n, n + 1) if isinstance(n, int) else bass.ds(n, 1)
        row = self.x[:, at, :].rearrange("p b d -> p (b d)")
        dve.wait_ge(self.out_done, done(n))
        dve.wait_ge(self.biased, done(n))
        dve.tensor_tensor(row, row, self.ps_x[:, :], ALU.add).then_inc(self.added, 1)
        dve.wait_ge(self.added, done(n))
        dve.bn_stats(self.stats[:, at, :].rearrange("p b s -> p (b s)"), row).then_inc(self.measured, 1)

    def weight_low(self, dve, n):
        w = (self.wq, self.wkv, self.wo)[n]
        dve.wait_ge(self.w_hi, n + 1)
        dve.tensor_tensor(w[1][:, :, :], self.raw[n], w[0][:, :, :].bitcast(F32), ALU.subtract).then_inc(self.w_lo, 1)

    def vector_step(self, dve, b, p, stages):
        project, turn, attend, finish = [s in stages for s in (PROJECT, TURN, ATTEND, FINISH)]
        l, m, n = b + 2, b + 1, b - 1
        if attend:
            self.maxima(dve, b, 1)
        if project:
            self.x_low(dve, l)
        if finish:
            self.scale_heads(dve, n)
        if attend:
            self.maxima(dve, b, 2)
        if project:
            self.ctx_low(dve, l)
            if isinstance(b, int) and b == -2:
                self.weight_low(dve, 1)
                dve.wait_ge(self.trig, 2)
                dve.tensor_scalar(self.sin[:, :, :, :, 0], self.sin[:, :, :, :, 1], -1.0, None, ALU.mult)\
                    .then_inc(self.trig_signed, 1)
                dve.wait_ge(self.trig_signed, 1)
            self.copy_tables(dve, l)
        if turn:
            self.fill_slots(dve, "q", m)
        if finish:
            self.attn_low(dve, n)
        if turn:
            self.fill_slots(dve, "k", m)
        if attend:
            self.maxima(dve, b, 3)
        if turn:
            self.copy_even(dve, m, 1 - p, 0)
            self.copy_even(dve, m, 1 - p, 1)
            self.maxima(dve, m, 0)
            self.copy_even(dve, m, 1 - p, 2)
        if NEXT in stages:
            self.normalise(dve, l + 1)
        if turn:
            self.copy_even(dve, m, 1 - p, 3)
        if finish:
            self.add_output(dve, n)

    def rotate(self, pool, which, m):
        n = 2 * m + (which == "k")
        copied, rotated, split = ((self.k_copied, self.k_rotated, self.k_lo) if which == "k" else
                                  (self.q_copied, self.q_rotated, self.q_lo))
        full = [P, self.H, self.HD]
        cos = self.tables_now[:, 0:1, :].to_broadcast(full)
        sin = self.tables_now[:, 1:2, :].rearrange("p a (f e) -> p a f e", e=2).to_broadcast([P, self.H, self.HD // 2, 2])
        rows = self.rows[which][:, :].rearrange("p (h e) -> p h e", h=self.H)
        swapped = self.rows[which][:, :].rearrange("p (h f e) -> p h f e", h=self.H, e=2)[:, :, :, ::-1]
        pool.wait_ge(copied, done(m))
        pool.wait_ge(self.tables_copied, done(m))
        pool.tensor_tensor(self.by_cos[:, :].rearrange("p (h e) -> p h e", h=self.H), rows, cos, ALU.mult)
        pool.tensor_tensor(self.by_sin[:, :].rearrange("p (h f e) -> p h f e", h=self.H, e=2), swapped, sin, ALU.mult)\
            .then_inc(self.rope_parts, 1)
        pool.wait_ge(self.rope_parts, done(n))
        pool.wait_ge(split, done(m - 1))
        pool.tensor_tensor(self.rotated[which][:, :], self.by_cos[:, :], self.by_sin[:, :], ALU.add).then_inc(rotated, 1)
        pool.wait_ge(rotated, done(m))

    def add_bias(self, pool, m):
        at = slice(m, m + 1) if isinstance(m, int) else bass.ds(m, 1)
        row = self.x[:, at, :].rearrange("p b d -> p (b d)")
        pool.wait_ge(self.normed_done, done(m))
        pool.wait_ge(self.bias_in, 16)
        pool.tensor_tensor(row, row, self.bias[:, :], ALU.add).then_inc(self.biased, 1)

    def pool_step(self, pool, l):
        self.rotate(pool, "q", l)
        self.rotate(pool, "k", l)
        self.add_bias(pool, l)

    def run(self, block):
        NB, H, HD = self.NB, self.H, self.HD
        ALL = {PROJECT, TURN, ATTEND, FINISH, NEXT}
        first = ((-2, {PROJECT, NEXT}), (-1, {PROJECT, TURN, NEXT}), (0, {PROJECT, TURN, ATTEND, NEXT}))
        LOOPS = (NB - 4) // 2
        last = ((NB - 3, {PROJECT, TURN, ATTEND, FINISH}), (NB - 2, {TURN, ATTEND, FINISH}), (NB - 1, {ATTEND, FINISH}),
                (NB, {FINISH}))
        BATCHES = (0, 2, 4, 10, NB)
        TWO_PI = 2 * math.pi

        @block.sync
        def _(sp):
            def load(n, w):
                sp.dma_start(self.raw[n], w.rearrange("(k p) n -> p k n", p=P)).then_inc(self.w_in[n], 16)

            sp.dma_start(self.pos[:, :, :], self.pos_dram.rearrange("b t a -> t b a")).then_inc(self.pos_in, 16)
            load(0, self.Wq)
            for p in range(2):
                sp.dma_start(self.ctx_rows[p][:, :], self.ctx_dram[p]).then_inc(self.ctx_in[p], 16)
            load(1, self.Wkv)
            load(2, self.Wout)
            sp.dma_start(self.bias[:, :], self.bout.rearrange("(a d) -> a d", a=1).to_broadcast([P, self.D]))\
                .then_inc(self.bias_in, 16)
            with sp.Fori(1, NB // 2) as i:
                for p in range(2):
                    m = i * 2 + p
                    sp.wait_ge(self.ctx_turned, done(m - 2))
                    sp.dma_start(self.ctx_rows[p][:, :], self.ctx_dram[bass.ds(m, 1)].rearrange("b t d -> (b t) d"))\
                        .then_inc(self.ctx_in[p], 16)

        @block.gpsimd
        def _(pool):
            start(pool, self.rope_parts, self.k_rotated, self.q_rotated, self.biased)

            def invert(n):
                at = slice(BATCHES[n], BATCHES[n + 1])
                pool.wait_ge(self.var_done, n + 1)
                pool.tensor_tensor(self.rstd[:, at], self.var_eps[:, at],
                                   self.minus_half[:, :].to_broadcast([P, BATCHES[n + 1] - BATCHES[n]]), ALU.pow)\
                    .then_inc(self.rstd_done, 1)

            invert(0)
            for which in "qk":
                pool.memset(self.slots[which][:, :, 3 * HD:self.SLOT].bitcast(F32), 0.0).then_inc(self.const_set, 1)
            pool.memset(self.max_rows[:, :], 0.0).then_inc(self.const_set, 1)
            for i in range(2):
                pool.memset(self.values[i][:, :, HD:HD + 1], 1.0).then_inc(self.const_set, 1)
                pool.memset(self.values[i][:, :, HD + 1:32], 0.0).then_inc(self.const_set, 1)
                pool.memset(self.k_cols[i][0:self.SLOT, :, 1, :].bitcast(F32), 0.0).then_inc(self.const_set, 1)
            pool.memset(self.half_pi[:, :], math.pi / 2).then_inc(self.const_set, 1)
            pool.wait_ge(self.const_set, self.CONSTS - 2)
            for i in range(2):
                pool.memset(self.k_cols[i][self.SLOT:P, :, 0, :].bitcast(F32), 0.0).then_inc(self.const_set, 1)
            pool.wait_ge(self.const_set, self.CONSTS)
            for l in range(4):
                self.pool_step(pool, l)
                if l < 3:
                    invert(l + 1)
            with pool.Fori(2, NB // 2) as i:
                for p in range(2):
                    self.pool_step(pool, i * 2 + p)

        @block.scalar
        def _(act):
            start(act, self.ctx_hi, self.x_hi, self.k_copied, self.v_copied, self.q_copied, self.q_cols_done,
                  self.max_copied, self.exp_done, self.o_copied, self.attn_hi, self.odd_copied)
            self.weight_high(act, 0)
            for b, stages in first:
                self.scalar_step(act, b, b % 2, stages)
                if b == -2:
                    self.weight_high(act, 2)
            with act.Fori(0, LOOPS) as i:
                for q in range(2):
                    self.scalar_step(act, i * 2 + 1 + q, (1 + q) % 2, ALL)
            for b, stages in last:
                self.scalar_step(act, b, b % 2, stages)

        @block.vector
        def _(dve):
            start(dve, self.normed_done, self.tables_copied, self.ctx_lo, self.x_lo, self.k_hi, self.k_lo, self.q_hi, self.q_lo,
                  self.even_copied, self.maxed, self.max_hi, self.max_lo, self.inverted, self.scaled, self.attn_lo,
                  self.added)
            def variances(first, last):
                for b in range(first, last):
                    dve.bn_stats(self.stats[:, b, :], self.x[:, b, :]).then_inc(self.stats_done, 1)
                dve.wait_ge(self.stats_done, last)
                for b in range(first, last):
                    dve.bn_aggr(self.mean_var[:, b, :], self.stats[:, b, :]).then_inc(self.mean_done, 1)
                dve.wait_ge(self.mean_done, last)
                dve.tensor_scalar(self.var_eps[:, first:last], self.mean_var[:, first:last, 1], EPS_LN, None, ALU.add)\
                    .then_inc(self.var_done, 1)

            variances(*BATCHES[0:2])
            dve.wait_ge(self.pos_in, 16)
            steps = [0]

            def stepped(ins):
                ins.then_inc(self.angle_step, 1)
                steps[0] += 1
                dve.wait_ge(self.angle_step, steps[0])

            for f in range(4):
                stepped(dve.tensor_scalar(self.angle[:, :, :, f], self.pos[:, :, :], 10000.0 ** (-f / 4), None, ALU.mult))
            ROUND = 1.5 * 2.0 ** 23
            stepped(dve.tensor_scalar(self.turns[:, :, :, :], self.angle[:, :, :, :], 1 / TWO_PI, ROUND, ALU.mult, ALU.add))
            stepped(dve.tensor_scalar(self.turns[:, :, :, :], self.turns[:, :, :, :], ROUND, None, ALU.subtract))
            high = 6.28125
            middle = math.floor((TWO_PI - high) * 2 ** 21) / 2 ** 21
            for part in (high, middle, TWO_PI - high - middle):
                stepped(dve.scalar_tensor_tensor(self.angle[:, :, :, :].rearrange("p b a f -> p (b a f)"),
                                                 self.turns[:, :, :, :].rearrange("p b a f -> p (b a f)"), -part,
                                                 self.angle[:, :, :, :].rearrange("p b a f -> p (b a f)"), ALU.mult, ALU.add))
            stepped(dve.tensor_scalar(self.angle[:, :, :, :], self.angle[:, :, :, :], 3.1415925, -3.1415925, ALU.min, ALU.max))
            self.normalise(dve, 0)
            self.weight_low(dve, 0)
            for b, stages in first:
                self.vector_step(dve, b, b % 2, stages)
                if b == -2:
                    dve.tensor_copy(self.ident16[:, :], self.ident[:, :]).then_inc(self.ident_made, 1)
                    dve.tensor_copy(self.ident_r[:, :], self.ident[:, :]).then_inc(self.ident_made, 1)
                    dve.tensor_reduce(self.minus[:, :], self.ident[:, 0:16].rearrange("p (a h) -> p h a", a=2), AX_X, ALU.add,
                                      negate=True).then_inc(self.minus_made, 1)
                    dve.wait_ge(self.minus_made, 1)
                    dve.tensor_copy(self.minus_head[:, :, :], self.minus[:, :].unsqueeze(2).to_broadcast([P, 8, P]))\
                        .then_inc(self.minus_made, 1)
                    self.weight_low(dve, 2)
                    dve.wait_ge(self.const_set, self.CONSTS)
                variances(BATCHES[b + 3], BATCHES[b + 4])
            with dve.Fori(0, LOOPS) as i:
                for q in range(2):
                    self.vector_step(dve, i * 2 + 1 + q, (1 + q) % 2, ALL)
            for b, stages in last:
                self.vector_step(dve, b, b % 2, stages)
            dve.wait_ge(self.measured, NB)

        @block.tensor
        def _(pe):
            start(pe, self.ctx_turned, self.x_turned, self.k_done, self.v_done, self.q_done, self.k_turned,
                  self.q_turned, self.logits_done, self.max_turned, self.logits_t_done, self.values_done,
                  self.attn_turned, self.out_done, self.o_turned)
            for b, stages in first:
                self.tensor_step(pe, b, b % 2, stages)
                if b == -2:
                    pe.wait_ge(self.const_set, self.CONSTS)
                    pe.wait_ge(self.w_lo, 3)
                    pe.wait_ge(self.minus_made, 2)
                    pe.wait_ge(self.ident_made, 2)
            with pe.Fori(0, LOOPS) as i:
                for q in range(2):
                    self.tensor_step(pe, i * 2 + 1 + q, (1 + q) % 2, ALL)
            for b, stages in last:
                self.tensor_step(pe, b, b % 2, stages)


class FeedForward:

    def __init__(self, nc, ctx, x, stats, ident, minus_half, gu_packed, gu_scales, down_packed, down_scales, out):
        sb = lambda n, s, d: ctx.enter_context(nc.sbuf_tensor("c_" + n, s, d))
        ps = lambda n, s, d: ctx.enter_context(nc.psum_tensor("c_" + n, s, d))
        sem = lambda n: ctx.enter_context(nc.semaphore("c_" + n))
        self.nc, self.x, self.ident, self.out = nc, x, ident, out
        self.gu_packed, self.gu_scales, self.down_packed, self.down_scales = gu_packed, gu_scales, down_packed, down_scales
        NB = self.NB = x.shape[1]
        D = self.D = x.shape[2]
        KT = self.KT = D // P
        C = self.C = gu_packed.shape[0] // 2 // P
        self.BLK = 4
        self.TILES_AT = ((), (), (0, 1), (2,))
        self.WG, self.WD = D // 8, P // 8
        self.WORDS = 2 * self.WG + KT * self.WD

        self.x_cols = [sb(f"x_cols{s}", [P, KT, NB * P], F32R) for s in "hl"]
        self.y = sb("y", [P, NB, D], F32)
        self.gu_s16 = sb("gu_s16", [KT, 2 * C * P], F16)
        self.gu_s = sb("gu_s", [P, 2, C, KT], F32)
        self.down_s16 = sb("down_s16", [C, D], F16)
        self.down_s = sb("down_s", [P, KT, C], F32)
        self.ident16 = sb("ident16", [P, P], F16)
        self.packed = [sb(f"packed{i}", [P, self.WORDS], I32) for i in range(2)]
        self.magnitude = sb("magnitude", [P, 4, self.WORDS], U32)
        self.sign = sb("sign", [P, 4, self.WORDS], U32)
        self.code = sb("code", [P, 4, self.WORDS], U32)
        self.scaled = sb("scaled", [P, 12, P], F32)
        self.w = [[[sb(f"w{i}{n}{s}", [P, KT, P], F32R) for s in "hl"] for n in range(3)] for i in range(2)]
        self.silu = [sb(f"silu{i}", [P, 512], F32) for i in range(2)]
        self.h = [sb(f"h{i}", [P, 512], F32) for i in range(2)]
        self.h_cols = [sb(f"h_cols{s}", [P, NB * P], F32R) for s in "hl"]
        self.squares = sb("squares", [P, D], F32)
        self.sum_sq = sb("sum_sq", [P, NB], F32)
        self.mean_sq = sb("mean_sq", [P, NB], F32)
        self.inv_rms = sb("inv_rms", [P, NB], F32)
        self.minus_half = minus_half

        self.ps_g = ps("ps_g", [P, 2, 512], F32)
        self.ps_u = ps("ps_u", [P, 2, 512], F32)
        self.ps_y = ps("ps_y", [P, 2, 512], F32)
        self.ps_w = ps("ps_w", [P, 2, KT, P], F32)
        self.ln = LayerNorm(sb, sem, "ln_", x, stats, self.x_cols, ident, minus_half)
        gate_banks, y_banks = [t[:, :, :].rearrange("p h (k t) -> p h k t", k=KT) for t in (self.ps_g, self.ps_y)]
        self.ln_psum = (gate_banks, y_banks, self.ps_w, self.ps_w)
        self.scales_in, self.stored = sem("scales_in"), sem("stored")
        self.packed_in = [sem(f"packed_in{i}") for i in range(2)]
        self.ident16_made = sem("ident16_made")
        self.scales_turned = sem("scales_turned")
        self.scales_copied = sem("scales_copied")
        self.bits_cut = sem("bits_cut")
        self.coded = sem("coded")
        self.weights_scaled = sem("weights_scaled")
        self.w_turned = sem("w_turned")
        self.w_hi = sem("w_hi")
        self.w_lo = sem("w_lo")
        self.gu_done = sem("gu_done")
        self.silu_done = sem("silu_done")
        self.h_made = sem("h_made")
        self.h_hi = sem("h_hi")
        self.h_lo = sem("h_lo")
        self.y_done = sem("y_done")
        self.y_added = sem("y_added")
        self.y_cleared = sem("y_cleared")
        self.squared = sem("squared")
        self.mean_done = sem("mean_done")
        self.rms_done = sem("rms_done")
        self.out_made = sem("out_made")

    def load_packed(self, sp, c, p):
        at = slice(c, c + 1) if isinstance(c, int) else bass.ds(c, 1)
        sp.wait_ge(self.coded, done(c - 2))
        for a in range(2):
            src = self.gu_packed.rearrange("(a c p) w -> a c p w", a=2, p=P)[a, at]
            sp.dma_start(self.packed[p][:, a * self.WG:(a + 1) * self.WG], src.rearrange("c p w -> (c p) w"))\
                .then_inc(self.packed_in[p], 16)
        src = self.down_packed.rearrange("(t p) (c w) -> c p t w", p=P, w=self.WD)[at]
        sp.dma_start(self.packed[p][:, 2 * self.WG:].rearrange("p (t w) -> p t w", w=self.WD),
                     src.rearrange("c p t w -> (c p) t w")).then_inc(self.packed_in[p], 16)

    def decode(self, dve, c, p):
        dve.wait_ge(self.packed_in[p], 48 * (c // 2 + 1) if isinstance(c, int) else (c + 2 - p) * 24)
        packed = self.packed[p][:, :].bitcast(U32)
        for j in range(4):
            for into, left, mask in ((self.magnitude, 9 - 4 * j, 0x0E000E00), (self.sign, 12 - 4 * j, 0x80008000)):
                op = ALU.logical_shift_left if left >= 0 else ALU.logical_shift_right
                ins = dve.tensor_scalar(into[:, j, :], packed, abs(left), mask, op, ALU.bitwise_and)
        ins.then_inc(self.bits_cut, 1)
        dve.wait_ge(self.bits_cut, done(c))
        dve.wait_ge(self.weights_scaled, done(12 * c - 1))
        dve.tensor_tensor(self.code[:, :, :], self.magnitude[:, :, :], self.sign[:, :, :], ALU.bitwise_or)\
            .then_inc(self.coded, 1)

    def scale_weights(self, act, c, n):
        at = slice(c, c + 1) if isinstance(c, int) else bass.ds(c, 1)
        a, g = n // 4, n % 4
        words = self.code[:, :, n * self.WD:(n + 1) * self.WD].bitcast(F16).rearrange("p j (w h) -> p w h j", h=2)
        scale = self.gu_s[:, a, at, g] if a < 2 else self.down_s[:, g, at]
        act.wait_ge(self.coded, done(c))
        act.wait_ge(self.w_turned, done(3 * c - 3 + a))
        act.activation(self.scaled[:, n, :].rearrange("p (w h j) -> p w h j", h=2, j=4), words, ACT.Copy,
                       scale=scale).then_inc(self.weights_scaled, 1)

    def turn_weights(self, pe, c, p, a):
        bank = (p + a) % 2
        pe.wait_ge(self.weights_scaled, done(12 * c + 4 * a + 3))
        pe.wait_ge(self.w_lo, done(3 * c + a - 2))
        for t in range(4):
            mm = pe.transpose(self.ps_w[:, bank, t, :], self.scaled[:, 4 * a + t, :], self.ident[:, :])
        mm.then_inc(self.w_turned, 1)

    def split_high(self, act, c, p, a):
        act.wait_ge(self.w_turned, done(3 * c + a))
        act.wait_ge(self.y_done, done(16 * (c - 2) + 15))
        act.activation(self.w[p][a][0][:, :, :], self.ps_w[:, (p + a) % 2, :, :], ACT.Copy).then_inc(self.w_hi, 1)

    def split_low(self, dve, c, p, a):
        dve.wait_ge(self.w_hi, done(3 * c + a))
        dve.tensor_tensor(self.w[p][a][1][:, :, :], self.ps_w[:, (p + a) % 2, :, :],
                          self.w[p][a][0][:, :, :].bitcast(F32), ALU.subtract).then_inc(self.w_lo, 1)

    def gate_up(self, pe, c, p, tb):
        n, tok = 4 * c + tb, slice(tb * 512, (tb + 1) * 512)
        if isinstance(c, int) and c == 0:
            pe.wait_ge(self.ln.lo_done, 4 * tb + 4)
        pe.wait_ge(self.w_lo, done(3 * c + 1))
        pe.wait_ge(self.h_made, done(n - 2))
        for a, bank in ((0, self.ps_g), (1, self.ps_u)):
            if isinstance(c, int) and c == 0 and tb == 0:
                self.turn_next(pe, tb, a)
            for k in range(self.KT):
                mm = matmul_split(pe, bank[:, tb % 2, :], [w[:, k, :] for w in self.w[p][a]],
                                  [x[:, k, tok] for x in self.x_cols], k == 0, k == self.KT - 1)
            if a == 1:
                mm.then_inc(self.gu_done, 1)
            if isinstance(c, int) and c == 0 and 0 < tb < 3:
                self.turn_next(pe, tb, a)

    def turn_next(self, pe, tb, a):
        if tb > 0:
            pe.wait_ge(self.w_lo, done(2))
        self.ln.tensor(pe, tb + 1, self.ln_psum[tb + 1], range(2 * a, 2 * a + 2))

    def down(self, pe, c, p, tb):
        pe.wait_ge(self.h_lo, done(4 * c + tb))
        pe.wait_ge(self.w_lo, done(3 * c + 2))
        w = [v[:, :, :].rearrange("p t h -> p (t h)") for v in self.w[p][2]]
        for i in range(self.BLK):
            t = tb * self.BLK + i
            pe.wait_ge(self.y_added, done(16 * c + t - 2))
            matmul_split(pe, self.ps_y[:, t % 2, :], [h[:, t * P:(t + 1) * P] for h in self.h_cols], w, True, True)\
                .then_inc(self.y_done, 1)

    def tensor_chunk(self, pe, c, p, first, last):
        for tb in range(4):
            self.gate_up(pe, c, p, tb)
            if first and tb == 2:
                pe.wait_ge(self.ln.lo_done, self.NB)
            if not last:
                for a in self.TILES_AT[tb]:
                    self.turn_weights(pe, c + 1, 1 - p, a)
            if tb > 0:
                self.down(pe, c, p, tb - 1)
            elif not first:
                self.down(pe, c - 1, 1 - p, 3)

    def gate_high(self, act, c, tb):
        n = 4 * c + tb
        act.wait_ge(self.gu_done, done(n))
        act.wait_ge(self.h_made, done(n - 2))
        act.activation(self.silu[tb % 2][:, :], self.ps_g[:, tb % 2, :], ACT.Silu).then_inc(self.silu_done, 1)
        act.wait_ge(self.h_made, done(n))
        act.wait_ge(self.y_done, done(16 * (c - 1) + 4 * tb + 3))
        act.activation(self.h_cols[0][:, tb * 512:(tb + 1) * 512], self.h[tb % 2][:, :], ACT.Copy).then_inc(self.h_hi, 1)

    def scalar_chunk(self, act, c, p, first, last):
        for tb in range(4):
            if first and tb < 3:
                self.ln.scalar(act, tb + 1, self.ln_psum[tb + 1], normalise=tb > 0)
            self.gate_high(act, c, tb)
            if last and tb >= 2:
                self.square(act, tb - 2)
            if not last and tb == 1:
                for n in range(12):
                    self.scale_weights(act, c + 1, n)
            if not last:
                for a in self.TILES_AT[tb]:
                    self.split_high(act, c + 1, 1 - p, a)

    def square(self, act, q):
        for b in range(4 * q, 4 * q + 4):
            act.wait_ge(self.y_added, done(16 * (self.C - 1) + b))
            if b > 0:
                act.wait_ge(self.squared, b)
            act.activation(self.squares[:, :], self.y[:, b, :], ACT.Square, accum_out=self.sum_sq[:, b:b + 1])\
                .then_inc(self.squared, 1)

    def invert_rms(self, pool, q):
        at = slice(4 * q, 4 * q + 4)
        pool.wait_ge(self.mean_done, q + 1)
        pool.tensor_tensor(self.inv_rms[:, at], self.mean_sq[:, at], self.minus_half[:, :].to_broadcast([P, 4]),
                           ALU.pow).then_inc(self.rms_done, 1)

    def mean_squares(self, dve, q):
        at = slice(4 * q, 4 * q + 4)
        dve.wait_ge(self.squared, 4 * q + 4)
        dve.tensor_scalar(self.mean_sq[:, at], self.sum_sq[:, at], 1.0 / self.D, EPS_RMS, ALU.mult, ALU.add)\
            .then_inc(self.mean_done, 1)

    def add_normed(self, dve, q):
        dve.wait_ge(self.rms_done, q + 1)
        for t in range(4 * q, 4 * q + 4):
            dve.scalar_tensor_tensor(self.x[:, t, :], self.y[:, t, :], self.inv_rms[:, t:t + 1], self.x[:, t, :],
                                     ALU.mult, ALU.add).then_inc(self.out_made, 1)

    def pool_chunk(self, pool, c, last=False):
        for tb in range(4):
            if last and tb == 3:
                self.invert_rms(pool, 0)
            pool.wait_ge(self.h_hi, done(4 * c + tb))
            pool.tensor_tensor(self.h_cols[1][:, tb * 512:(tb + 1) * 512], self.h[tb % 2][:, :],
                               self.h_cols[0][:, tb * 512:(tb + 1) * 512].bitcast(F32), ALU.subtract).then_inc(self.h_lo, 1)

    def multiply(self, dve, c, tb):
        n = 4 * c + tb
        dve.wait_ge(self.silu_done, done(n))
        dve.wait_ge(self.h_lo, done(n - 2))
        dve.tensor_tensor(self.h[tb % 2][:, :], self.silu[tb % 2][:, :], self.ps_u[:, tb % 2, :], ALU.mult)\
            .then_inc(self.h_made, 1)

    def add_down(self, dve, c, tb, tiles):
        for i in tiles:
            t = tb * self.BLK + i
            dve.wait_ge(self.y_done, done(16 * c + t))
            if isinstance(c, int) and c == 0:
                ins = dve.tensor_copy(self.y[:, t, :], self.ps_y[:, t % 2, :])
            else:
                ins = dve.tensor_tensor(self.y[:, t, :], self.y[:, t, :], self.ps_y[:, t % 2, :], ALU.add)
            ins.then_inc(self.y_added, 1)

    def vector_chunk(self, dve, c, p, first, last):
        for tb in range(4):
            before = (c, tb - 1) if tb > 0 else (c - 1, 3)
            if first and tb < 3:
                self.ln.vector(dve, tb + 1, self.ln_psum[tb + 1], normalise=tb == 0)
            if tb > 0 or not first:
                self.add_down(dve, *before, range(2))
            self.multiply(dve, c, tb)
            if tb > 0 or not first:
                self.add_down(dve, *before, range(2, 4))
            if not last:
                for a in self.TILES_AT[tb]:
                    self.split_low(dve, c + 1, 1 - p, a)
                if tb == 0:
                    self.decode(dve, c + 1, 1 - p)
            elif tb == 2:
                self.mean_squares(dve, 0)
            elif tb == 3:
                self.add_normed(dve, 0)
                self.mean_squares(dve, 1)

    def run(self, block):
        NB, C, KT, D = self.NB, self.C, self.KT, self.D
        PAIRS = (C - 3) // 2
        rest = range(1 + 2 * PAIRS, C)

        @block.sync
        def _(sp):
            sp.dma_start(self.gu_s16[:, :], self.gu_scales).then_inc(self.scales_in, 16)
            sp.dma_start(self.down_s16[:, :], self.down_scales).then_inc(self.scales_in, 16)
            self.load_packed(sp, 0, 0)
            with sp.Fori(0, (C - 1) // 2) as i:
                for q in range(2):
                    self.load_packed(sp, i * 2 + 1 + q, (1 + q) % 2)
            for b in range(0, NB, 4):
                sp.wait_ge(self.out_made, b + 4)
                sp.dma_start(self.out[b:b + 4].rearrange("b t d -> t b d"), self.x[:, b:b + 4, :]).then_inc(self.stored, 16)
            sp.wait_ge(self.stored, 16 * (NB // 4))

        @block.gpsimd
        def _(pool):
            start(pool, self.h_lo)
            pool.memset(self.ident16[:, :], 0.0).then_inc(self.ident16_made, 1)
            pool.wait_ge(self.ident16_made, 1)
            pool.affine_select(out=self.ident16[:, :], in_=self.ident16[:, :], compare_op=ALU.not_equal, fill=1.0, base=0,
                               pattern=[[-1, P]], channel_multiplier=1).then_inc(self.ident16_made, 1)
            pool.wait_ge(self.ident16_made, 2)
            for q in range(4):
                self.ln.pool(pool, q)
            pool.memset(self.y[:, NB - self.BLK:NB, :], 0.0).then_inc(self.y_cleared, 1)
            self.pool_chunk(pool, 0)
            with pool.Fori(0, PAIRS) as i:
                for q in range(2):
                    self.pool_chunk(pool, i * 2 + 1 + q)
            for c in rest:
                self.pool_chunk(pool, c, c == C - 1)
            for q in (1, 2, 3):
                self.invert_rms(pool, q)

        @block.scalar
        def _(act):
            start(act, self.weights_scaled, self.w_hi, self.silu_done, self.h_hi)
            act.wait_ge(self.scales_turned, 1)
            gu_turned = self.ps_u[:, 0, :].bitcast(F16)
            act.activation(self.gu_s[:, :, :, :].rearrange("p a c g -> p (a c g)"), gu_turned[:, 0:2 * C * KT], ACT.Copy,
                           scale=2.0 ** 14).then_inc(self.scales_copied, 1)
            down_turned = self.ps_u[:, 1, :].bitcast(F16)
            act.activation(self.down_s[:, :, :], down_turned[:, 0:KT * 16].rearrange("p (t c) -> p t c", c=16)[:, :, 0:C],
                           ACT.Copy, scale=2.0 ** 14).then_inc(self.scales_copied, 1)
            act.wait_ge(self.scales_copied, 2)
            for n in range(8):
                self.scale_weights(act, 0, n)
            self.ln.scalar(act, 0, self.ln_psum[0])
            for a in range(2):
                self.split_high(act, 0, 0, a)
            for n in range(8, 12):
                self.scale_weights(act, 0, n)
            self.split_high(act, 0, 0, 2)
            self.scalar_chunk(act, 0, 0, True, False)
            with act.Fori(0, PAIRS) as i:
                for q in range(2):
                    self.scalar_chunk(act, i * 2 + 1 + q, (1 + q) % 2, False, False)
            for c in rest:
                self.scalar_chunk(act, c, c % 2, False, c == C - 1)
            self.square(act, 2)
            self.square(act, 3)

        @block.tensor
        def _(pe):
            start(pe, self.w_turned, self.gu_done, self.y_done)
            pe.wait_ge(self.scales_in, 32)
            pe.wait_ge(self.ident16_made, 2)
            for t in range(2 * C):
                pe.transpose(self.ps_u[:, 0, :].bitcast(F16)[:, t * KT:(t + 1) * KT], self.gu_s16[:, t * P:(t + 1) * P],
                             self.ident16[0:KT, 0:KT])
            for t in range(KT):
                mm = pe.transpose(self.ps_u[:, 1, :].bitcast(F16)[:, t * 16:t * 16 + C], self.down_s16[:, t * P:(t + 1) * P],
                                  self.ident16[0:C, 0:C])
            mm.then_inc(self.scales_turned, 1)
            for a in range(2):
                self.turn_weights(pe, 0, 0, a)
            self.ln.tensor(pe, 0, self.ln_psum[0])
            self.turn_weights(pe, 0, 0, 2)
            pe.wait_ge(self.scales_copied, 2)
            self.tensor_chunk(pe, 0, 0, True, False)
            with pe.Fori(0, PAIRS) as i:
                for q in range(2):
                    self.tensor_chunk(pe, i * 2 + 1 + q, (1 + q) % 2, False, False)
            for c in rest:
                self.tensor_chunk(pe, c, c % 2, False, c == C - 1)
            self.down(pe, C - 1, (C - 1) % 2, 3)

        @block.vector
        def _(dve):
            start(dve, self.bits_cut, self.coded, self.w_lo, self.h_made, self.y_added)
            self.ln.variances(dve, 0)
            self.ln.variances(dve, 1)
            self.decode(dve, 0, 0)
            self.ln.vector(dve, 0, self.ln_psum[0], normalise=True)
            for a in range(2):
                self.split_low(dve, 0, 0, a)
            self.ln.variances(dve, 2)
            self.ln.variances(dve, 3)
            self.split_low(dve, 0, 0, 2)
            for q in (1, 2, 3):
                self.ln.factors(dve, q)
            self.vector_chunk(dve, 0, 0, True, False)
            dve.wait_ge(self.y_cleared, 1)
            with dve.Fori(0, PAIRS) as i:
                for q in range(2):
                    self.vector_chunk(dve, i * 2 + 1 + q, (1 + q) % 2, False, False)
            for c in rest:
                self.vector_chunk(dve, c, c % 2, False, c == C - 1)
            self.add_down(dve, C - 1, 3, range(4))
            self.mean_squares(dve, 2)
            self.add_normed(dve, 1)
            self.mean_squares(dve, 3)
            self.add_normed(dve, 2)
            self.add_normed(dve, 3)


def decoder_layer(nc, x_in, ctx_in, pos_in, Wq, Wk, Wv, Wo, bo, xWq, xWkv, xWout, xbout,
                  gu_packed, gu_scales, down_packed, down_scales, out):
    NB, T, D = x_in.shape
    with ExitStack() as ctx:
        sb = lambda n, s, d: ctx.enter_context(nc.sbuf_tensor(n, s, d))
        x = sb("x", [P, NB, D], F32)
        ident = sb("ident", [P, P], F32)
        minus_half = sb("minus_half", [P, 1], F32)
        ones = sb("ones", [P, 1], F32)
        stats = sb("stats", [P, NB, 6], F32)
        const_set = ctx.enter_context(nc.semaphore("const_set"))
        with nc.Block() as block:
            @block.gpsimd
            def _(pool):
                pool.memset(minus_half[:, :], -0.5).then_inc(const_set, 1)
                pool.memset(ident[:, :], 0.0).then_inc(const_set, 1)
                pool.memset(ones[:, :], 1.0).then_inc(const_set, 1)
                pool.wait_ge(const_set, 3)
                pool.affine_select(out=ident[:, :], in_=ident[:, :], compare_op=ALU.not_equal, fill=1.0,
                                   base=0, pattern=[[-1, P]], channel_multiplier=1).then_inc(const_set, 1)
                pool.wait_ge(const_set, 4)
        linear_attention(nc, x, stats, ident, ones, minus_half, x_in, Wq, Wk, Wv, Wo, bo)
        with ExitStack() as scope:
            attention = CrossAttention(nc, scope, x, stats, ident, minus_half, ctx_in, pos_in, xWq, xWkv, xWout, xbout)
            with nc.Block() as block:
                attention.run(block)
        with ExitStack() as scope:
            feed_forward = FeedForward(nc, scope, x, stats, ident, minus_half, gu_packed, gu_scales, down_packed,
                                       down_scales, out)
            with nc.Block() as block:
                feed_forward.run(block)


_INS = ['x', 'ctx_1024', 'fside_BxSx2_0', 'L0_attn_Wq', 'L0_attn_Wk', 'L0_attn_Wv', 'L0_attn_Wo', 'L0_attn_bo',
        'L0_xattn_Wq', 'L0_xattn_Wkv', 'L0_xattn_Wout', 'L0_xattn_bout', 'L0_ffn_gate_up_packed',
        'L0_ffn_gate_up_scales', 'L0_ffn_down_packed', 'L0_ffn_down_scales']


def kernel(**inputs):
    import numpy as _np
    import concourse.bacc as _bacc
    from concourse import mybir as _mybir
    from concourse.bass_utils import run_bass_kernel_spmd as _run

    nc = _bacc.Bacc("TRN2", target_bir_lowering=False, num_devices=1)
    arrays, args = {}, []
    for name in _INS:
        a = _np.ascontiguousarray(inputs[name])
        arrays[f"in_{name}"] = a
        args.append(nc.dram_tensor(f"in_{name}", a.shape, _mybir.dt.from_np(a.dtype), kind="ExternalInput").ap())
    args.append(nc.dram_tensor("out_x", (16, 128, 512), _mybir.dt.float32, kind="ExternalOutput").ap())
    decoder_layer(nc, *args)
    r = _run(nc, [arrays], core_ids=[0])
    return r.results[0]["out_x"]
```
